# Optimizing a Trainium2 kernel written in Bass

```python
import numpy as np
import jax
import jax.numpy as jnp

def _softmax(x, axis=-1):
    return jax.nn.softmax(x, axis=axis)

def _gelu(x):
    return jax.nn.gelu(x, approximate=True)

def _silu(x):
    return jax.nn.silu(x)

def _sigmoid(x):
    return jax.nn.sigmoid(x)

def _layernorm(x, axis=-1, eps=1e-05):
    m = jnp.mean(x, axis=axis, keepdims=True)
    v = jnp.var(x, axis=axis, keepdims=True)
    return (x - m) / jnp.sqrt(v + eps)

def _scatter_add(tgt, idx, src, axis=0):
    return tgt.at[idx].add(src)

def _segment_sum(src, seg, n):
    return jax.ops.segment_sum(src, seg, n)
kernel_name = 'mk_decoder_postln_d1_seqx_r4_99ec3c'

def setup_inputs(seed: int=0):
    np.random.seed(seed)
    _w = jnp.asarray

    def _rec_inputs():
        import jax
        import jax.numpy as jnp
        _rk = jax.random.key(seed)
        x = -0.0003929 + 0.9999 * jax.random.normal(jax.random.fold_in(_rk, 1), (4, 1024, 256), jnp.float32)
        _lenS = 1024 - jax.random.randint(jax.random.fold_in(_rk, 7), (4,), 0, max(1, 1024 // 4) + 1, jnp.int32)
        _lenS2 = 64 - jax.random.randint(jax.random.fold_in(_rk, 8), (4,), 0, max(1, 64 // 4) + 1, jnp.int32)
        _ctx_768P = jax.random.normal(jax.random.fold_in(_rk, 11), (4, 16, 192), jnp.float32)
        _ctx_768c = jax.random.dirichlet(jax.random.fold_in(_rk, 511), 0.3 * jnp.ones((16,), jnp.float32), (4, 64))
        _ctx_768t = jnp.einsum('bsk,bkd->bsd', _ctx_768c, _ctx_768P)
        _ctx_768t = _ctx_768t * jax.lax.rsqrt(jnp.mean(jnp.square(_ctx_768t)) + 1e-12) * 0.953939
        ctx_768 = 0.00095986 + 0.999812 * (_ctx_768t + 0.3 * jax.random.normal(jax.random.fold_in(_rk, 611), (4, 64, 192), jnp.float32))
        _validS = jnp.arange(1024)[None, :] < _lenS[:, None]
        _validS2 = jnp.arange(64)[None, :] < _lenS2[:, None]
        _causal = jnp.tril(jnp.ones((1024, 1024), dtype=bool))
        mask_BxS2_bf1 = jnp.ones((4, 64), dtype=bool)
        return (x, ctx_768, mask_BxS2_bf1)
    x, ctx_768, mask_BxS2_bf1 = _rec_inputs()

    def _L0_attn_setup():
        import jax, jax.numpy as jnp
        import numpy as np
        D_MODEL, D_INNER, D_CONV, D_STATE, DT_RANK = (256, 512, 4, 16, 64)
        ALPHA, CHUNK = (0.1, 64)

        def rmsnorm(x, w, eps=1e-05):
            return x * jax.lax.rsqrt(jnp.mean(x * x, axis=-1, keepdims=True) + eps) * w

        def mamba_block(x, in_w, in_b, conv_w, conv_b, xp_w, dt_w, dt_b, A_log, D_ssm, out_w, out_b):
            B, T, _ = x.shape
            xz = x @ in_w.T + in_b
            xm, res = jnp.split(xz, 2, axis=-1)
            xc = jax.lax.conv_general_dilated(xm.transpose(0, 2, 1), conv_w, (1,), [(D_CONV - 1, 0)], dimension_numbers=('NCH', 'OIH', 'NCH'), feature_group_count=D_INNER)
            xm = jax.nn.silu(xc.transpose(0, 2, 1) + conv_b)
            x_dbl = xm @ xp_w.T
            delta = jax.nn.softplus(x_dbl[..., :DT_RANK] @ dt_w.T + dt_b)
            Bm = x_dbl[..., DT_RANK:DT_RANK + D_STATE]
            Cm = x_dbl[..., DT_RANK + D_STATE:]
            A = -jnp.exp(A_log)

            def step(h, ins):
                d_t, B_t, C_t, u_t = ins
                dA = jnp.exp(d_t[:, :, None] * A)
                h = h * dA + (d_t * u_t)[:, :, None] * B_t[:, None, :]
                y = jnp.einsum('bds,bs->bd', h, C_t)
                return (h, y)
            h0 = jnp.zeros((B, D_INNER, D_STATE), x.dtype)
            _, ys = jax.lax.scan(step, h0, (delta.transpose(1, 0, 2), Bm.transpose(1, 0, 2), Cm.transpose(1, 0, 2), xm.transpose(1, 0, 2)))
            y = ys.transpose(1, 0, 2) + xm * D_ssm
            y = y * jax.nn.silu(res)
            return y @ out_w.T + out_b

        def memory_attend(out, w_write, w_read, decay):
            B, T, D = out.shape
            C = CHUNK
            gamma = jax.nn.sigmoid(decay)
            log_gamma = jnp.log(gamma)
            v = out @ w_write.T
            wk = jnp.pad(out[:, :-1], ((0, 0), (1, 0), (0, 0)))
            rk = out
            n = T // C
            p = jnp.arange(C)
            diffs = jnp.clip(p[:, None] - 1 - p[None, :], 0, None).astype(out.dtype)
            causal = (p[:, None] > p[None, :]).astype(out.dtype)
            M = jnp.exp(diffs * log_gamma) * causal
            g_in = gamma ** p
            g_w = gamma ** (C - 1 - p)
            chunked = lambda a: a.reshape(B, n, C, D).transpose(1, 0, 2, 3)

            def step(W, ins):
                rk_c, wk_c, v_c = ins
                inter = jnp.einsum('bde,bce->bcd', W, rk_c) * g_in[None, :, None]
                S = jnp.einsum('bcd,bkd->bck', rk_c, wk_c)
                intra = jnp.einsum('bck,bkd->bcd', S * M, v_c)
                W_new = gamma ** C * W + jnp.einsum('bcd,bce->bde', v_c * g_w[None, :, None], wk_c)
                return (W_new, inter + intra)
            W0 = jnp.zeros((B, D, D), out.dtype)
            _, reads = jax.lax.scan(step, W0, (chunked(rk), chunked(wk), chunked(v)))
            reads = reads.transpose(1, 0, 2, 3).reshape(B, T, D)
            return out + ALPHA * (reads @ w_read.T)
        key = jax.random.key(seed)
        ks = jax.random.split(key, 10)
        B, T = (2, 512)
        s = lambda k, shape, scale: jax.random.normal(k, shape, jnp.float32) * scale
        return {'x': s(ks[0], (B, T, D_MODEL), 1.0), 'norm1_w': jnp.ones((D_MODEL,), jnp.float32), 'norm2_w': jnp.ones((D_MODEL,), jnp.float32), 'in_proj_w': s(ks[1], (2 * D_INNER, D_MODEL), 0.02), 'in_proj_b': jnp.zeros((2 * D_INNER,), jnp.float32), 'conv_w': s(ks[2], (D_INNER, 1, D_CONV), 0.1), 'conv_b': jnp.zeros((D_INNER,), jnp.float32), 'x_proj_w': s(ks[3], (DT_RANK + 2 * D_STATE, D_INNER), 0.02), 'dt_proj_w': s(ks[4], (D_INNER, DT_RANK), 0.02), 'dt_proj_b': s(ks[5], (D_INNER,), 0.02), 'A_log': jnp.log(jnp.broadcast_to(jnp.arange(1, D_STATE + 1, dtype=jnp.float32), (D_INNER, D_STATE))) + 0.0, 'D_ssm': jnp.ones((D_INNER,), jnp.float32), 'out_proj_w': s(ks[6], (D_MODEL, D_INNER), 0.02), 'out_proj_b': jnp.zeros((D_MODEL,), jnp.float32), 'proj_write_w': s(ks[7], (D_MODEL, D_MODEL), 0.02), 'proj_read_w': s(ks[8], (D_MODEL, D_MODEL), 0.02), 'decay': jnp.float32(4.6)}
    _L0_attn_all = _L0_attn_setup()
    _L0_attn_in = {k: v for k, v in _L0_attn_all.items() if k in ('norm1_w', 'norm2_w', 'in_proj_w', 'in_proj_b', 'conv_w', 'conv_b', 'x_proj_w', 'dt_proj_w', 'dt_proj_b', 'A_log', 'D_ssm', 'out_proj_w', 'out_proj_b', 'proj_write_w', 'proj_read_w', 'decay')}
    del _L0_attn_all

    def _L0_xattn_setup():
        import jax, jax.numpy as jnp
        import numpy as np
        DIM = 256
        CTX_DIM = 192
        HEADS = 16
        key = jax.random.key(seed)
        ks = jax.random.split(key, 7)
        B, N, M = (4, 1024, 64)
        x = jax.random.normal(ks[0], (B, N, DIM), dtype=jnp.float32)
        context = jax.random.normal(ks[1], (B, M, CTX_DIM), dtype=jnp.float32)
        context_mask = jnp.ones((B, M), dtype=bool)
        s_d = 1.0 / np.sqrt(DIM)
        s_c = 1.0 / np.sqrt(CTX_DIM)
        Wq = jax.random.normal(ks[2], (DIM, DIM), dtype=jnp.float32) * s_d
        Wk = jax.random.normal(ks[3], (CTX_DIM, DIM), dtype=jnp.float32) * s_c
        Wv = jax.random.normal(ks[4], (CTX_DIM, DIM), dtype=jnp.float32) * s_c
        Wo = jax.random.normal(ks[5], (DIM, DIM), dtype=jnp.float32) * s_d
        return {'x': x, 'context': context, 'context_mask': context_mask, 'Wq': Wq, 'Wk': Wk, 'Wv': Wv, 'Wo': Wo}
    _L0_xattn_all = _L0_xattn_setup()
    _L0_xattn_in = {k: v for k, v in _L0_xattn_all.items() if k in ('Wq', 'Wk', 'Wv', 'Wo')}
    del _L0_xattn_all

    def _L0_ffn_setup():
        import jax, jax.numpy as jnp
        import numpy as np
        D = 256
        H = 1024
        E = 8
        B = 2
        T = 512
        LN_EPS = 1e-05

        def _layer_norm(r, gamma, beta):
            mu = jnp.mean(r, axis=-1, keepdims=True)
            var = jnp.mean(jnp.square(r - mu), axis=-1, keepdims=True)
            return (r - mu) * jax.lax.rsqrt(var + LN_EPS) * gamma + beta
        key = jax.random.key(seed)
        ks = jax.random.split(key, 9)
        s_in = 1.0 / np.sqrt(D)
        s_hid = 1.0 / np.sqrt(H)
        x = jax.random.normal(ks[0], (B, T, D), dtype=jnp.float32)
        Wg = jax.random.uniform(ks[1], (D, E), jnp.float32, -s_in, s_in)
        bg = jax.random.uniform(ks[2], (E,), jnp.float32, -s_in, s_in)
        W1 = jax.random.uniform(ks[3], (E, D, H), jnp.float32, -s_in, s_in)
        b1 = jax.random.uniform(ks[4], (E, H), jnp.float32, -s_in, s_in)
        W2 = jax.random.uniform(ks[5], (E, H, D), jnp.float32, -s_hid, s_hid)
        b2 = jax.random.uniform(ks[6], (E, D), jnp.float32, -s_hid, s_hid)
        gamma = jnp.ones((D,), jnp.float32)
        beta = jnp.zeros((D,), jnp.float32)
        return {'x': x, 'Wg': Wg, 'bg': bg, 'W1': W1, 'b1': b1, 'W2': W2, 'b2': b2, 'gamma': gamma, 'beta': beta}
    _L0_ffn_all = _L0_ffn_setup()
    _L0_ffn_in = {k: v for k, v in _L0_ffn_all.items() if k in ('Wg', 'bg', 'W1', 'b1', 'W2', 'b2', 'gamma', 'beta')}
    del _L0_ffn_all
    return {'x': x, 'ctx_768': ctx_768, 'mask_BxS2_bf1': mask_BxS2_bf1, 'L0_attn_norm1_w': _L0_attn_in['norm1_w'], 'L0_attn_norm2_w': _L0_attn_in['norm2_w'], 'L0_attn_in_proj_w': _L0_attn_in['in_proj_w'], 'L0_attn_in_proj_b': _L0_attn_in['in_proj_b'], 'L0_attn_conv_w': _L0_attn_in['conv_w'], 'L0_attn_conv_b': _L0_attn_in['conv_b'], 'L0_attn_x_proj_w': _L0_attn_in['x_proj_w'], 'L0_attn_dt_proj_w': _L0_attn_in['dt_proj_w'], 'L0_attn_dt_proj_b': _L0_attn_in['dt_proj_b'], 'L0_attn_A_log': _L0_attn_in['A_log'], 'L0_attn_D_ssm': _L0_attn_in['D_ssm'], 'L0_attn_out_proj_w': _L0_attn_in['out_proj_w'], 'L0_attn_out_proj_b': _L0_attn_in['out_proj_b'], 'L0_attn_proj_write_w': _L0_attn_in['proj_write_w'], 'L0_attn_proj_read_w': _L0_attn_in['proj_read_w'], 'L0_attn_decay': _L0_attn_in['decay'], 'L0_xattn_Wq': _L0_xattn_in['Wq'], 'L0_xattn_Wk': _L0_xattn_in['Wk'], 'L0_xattn_Wv': _L0_xattn_in['Wv'], 'L0_xattn_Wo': _L0_xattn_in['Wo'], 'L0_ffn_Wg': _L0_ffn_in['Wg'], 'L0_ffn_bg': _L0_ffn_in['bg'], 'L0_ffn_W1': _L0_ffn_in['W1'], 'L0_ffn_b1': _L0_ffn_in['b1'], 'L0_ffn_W2': _L0_ffn_in['W2'], 'L0_ffn_b2': _L0_ffn_in['b2'], 'L0_ffn_gamma': _L0_ffn_in['gamma'], 'L0_ffn_beta': _L0_ffn_in['beta']}

def reference(x, ctx_768, mask_BxS2_bf1, L0_attn_norm1_w, L0_attn_norm2_w, L0_attn_in_proj_w, L0_attn_in_proj_b, L0_attn_conv_w, L0_attn_conv_b, L0_attn_x_proj_w, L0_attn_dt_proj_w, L0_attn_dt_proj_b, L0_attn_A_log, L0_attn_D_ssm, L0_attn_out_proj_w, L0_attn_out_proj_b, L0_attn_proj_write_w, L0_attn_proj_read_w, L0_attn_decay, L0_xattn_Wq, L0_xattn_Wk, L0_xattn_Wv, L0_xattn_Wo, L0_ffn_Wg, L0_ffn_bg, L0_ffn_W1, L0_ffn_b1, L0_ffn_W2, L0_ffn_b2, L0_ffn_gamma, L0_ffn_beta):
    import jax
    import jax.numpy as jnp

    def _L0_attn_ref(x, norm1_w, norm2_w, in_proj_w, in_proj_b, conv_w, conv_b, x_proj_w, dt_proj_w, dt_proj_b, A_log, D_ssm, out_proj_w, out_proj_b, proj_write_w, proj_read_w, decay):
        import jax, jax.numpy as jnp
        import numpy as np
        D_MODEL, D_INNER, D_CONV, D_STATE, DT_RANK = (256, 512, 4, 16, 64)
        ALPHA, CHUNK = (0.1, 64)

        def rmsnorm(x, w, eps=1e-05):
            return x * jax.lax.rsqrt(jnp.mean(x * x, axis=-1, keepdims=True) + eps) * w

        def mamba_block(x, in_w, in_b, conv_w, conv_b, xp_w, dt_w, dt_b, A_log, D_ssm, out_w, out_b):
            B, T, _ = x.shape
            xz = x @ in_w.T + in_b
            xm, res = jnp.split(xz, 2, axis=-1)
            xc = jax.lax.conv_general_dilated(xm.transpose(0, 2, 1), conv_w, (1,), [(D_CONV - 1, 0)], dimension_numbers=('NCH', 'OIH', 'NCH'), feature_group_count=D_INNER)
            xm = jax.nn.silu(xc.transpose(0, 2, 1) + conv_b)
            x_dbl = xm @ xp_w.T
            delta = jax.nn.softplus(x_dbl[..., :DT_RANK] @ dt_w.T + dt_b)
            Bm = x_dbl[..., DT_RANK:DT_RANK + D_STATE]
            Cm = x_dbl[..., DT_RANK + D_STATE:]
            A = -jnp.exp(A_log)

            def step(h, ins):
                d_t, B_t, C_t, u_t = ins
                dA = jnp.exp(d_t[:, :, None] * A)
                h = h * dA + (d_t * u_t)[:, :, None] * B_t[:, None, :]
                y = jnp.einsum('bds,bs->bd', h, C_t)
                return (h, y)
            h0 = jnp.zeros((B, D_INNER, D_STATE), x.dtype)
            _, ys = jax.lax.scan(step, h0, (delta.transpose(1, 0, 2), Bm.transpose(1, 0, 2), Cm.transpose(1, 0, 2), xm.transpose(1, 0, 2)))
            y = ys.transpose(1, 0, 2) + xm * D_ssm
            y = y * jax.nn.silu(res)
            return y @ out_w.T + out_b

        def memory_attend(out, w_write, w_read, decay):
            B, T, D = out.shape
            C = CHUNK
            gamma = jax.nn.sigmoid(decay)
            log_gamma = jnp.log(gamma)
            v = out @ w_write.T
            wk = jnp.pad(out[:, :-1], ((0, 0), (1, 0), (0, 0)))
            rk = out
            n = T // C
            p = jnp.arange(C)
            diffs = jnp.clip(p[:, None] - 1 - p[None, :], 0, None).astype(out.dtype)
            causal = (p[:, None] > p[None, :]).astype(out.dtype)
            M = jnp.exp(diffs * log_gamma) * causal
            g_in = gamma ** p
            g_w = gamma ** (C - 1 - p)
            chunked = lambda a: a.reshape(B, n, C, D).transpose(1, 0, 2, 3)

            def step(W, ins):
                rk_c, wk_c, v_c = ins
                inter = jnp.einsum('bde,bce->bcd', W, rk_c) * g_in[None, :, None]
                S = jnp.einsum('bcd,bkd->bck', rk_c, wk_c)
                intra = jnp.einsum('bck,bkd->bcd', S * M, v_c)
                W_new = gamma ** C * W + jnp.einsum('bcd,bce->bde', v_c * g_w[None, :, None], wk_c)
                return (W_new, inter + intra)
            W0 = jnp.zeros((B, D, D), out.dtype)
            _, reads = jax.lax.scan(step, W0, (chunked(rk), chunked(wk), chunked(v)))
            reads = reads.transpose(1, 0, 2, 3).reshape(B, T, D)
            return out + ALPHA * (reads @ w_read.T)
        mb = lambda h: mamba_block(h, in_proj_w, in_proj_b, conv_w, conv_b, x_proj_w, dt_proj_w, dt_proj_b, A_log, D_ssm, out_proj_w, out_proj_b)
        out1 = mb(rmsnorm(x, norm1_w))
        x1 = x + out1
        out2 = mb(rmsnorm(x1, norm2_w))
        out2 = memory_attend(out2, proj_write_w, proj_read_w, decay)
        return x1 + out2

    def _L0_xattn_ref(x, context, context_mask, Wq, Wk, Wv, Wo):
        import jax, jax.numpy as jnp
        import numpy as np
        DIM = 256
        CTX_DIM = 192
        HEADS = 16
        B, N, _ = x.shape
        M = context.shape[1]
        hd = DIM // HEADS
        scale = hd ** (-0.5)
        q = (x @ Wq).reshape(B, N, HEADS, hd).transpose(0, 2, 1, 3)
        k = (context @ Wk).reshape(B, M, HEADS, hd).transpose(0, 2, 1, 3)
        v = (context @ Wv).reshape(B, M, HEADS, hd).transpose(0, 2, 1, 3)
        scores = jnp.einsum('bhid,bhjd->bhij', q, k) * scale
        max_neg = -jnp.finfo(scores.dtype).max
        scores = jnp.where(context_mask[:, None, None, :], scores, max_neg)
        attn = jax.nn.softmax(scores, axis=-1)
        out = jnp.einsum('bhij,bhjd->bhid', attn, v)
        out = out.transpose(0, 2, 1, 3).reshape(B, N, DIM)
        return out @ Wo

    def _L0_ffn_ref(x, Wg, bg, W1, b1, W2, b2, gamma, beta):
        import jax, jax.numpy as jnp
        import numpy as np
        D = 256
        H = 1024
        E = 8
        B = 2
        T = 512
        LN_EPS = 1e-05

        def _layer_norm(r, gamma, beta):
            mu = jnp.mean(r, axis=-1, keepdims=True)
            var = jnp.mean(jnp.square(r - mu), axis=-1, keepdims=True)
            return (r - mu) * jax.lax.rsqrt(var + LN_EPS) * gamma + beta
        logits = jnp.einsum('btd,de->bte', x, Wg) + bg
        top2_vals, top2_idx = jax.lax.top_k(logits, 2)
        scores = jax.nn.softmax(top2_vals, axis=-1)
        onehot = jax.nn.one_hot(top2_idx, E, dtype=x.dtype)
        combine = jnp.einsum('btk,btke->bte', scores, onehot)
        h = jnp.einsum('btd,edh->bteh', x, W1) + b1[None, None]
        h = jax.nn.gelu(h, approximate=False)
        y = jnp.einsum('bteh,ehd->bted', h, W2) + b2[None, None]
        out = jnp.einsum('bted,bte->btd', y, combine)
        return _layer_norm(x + out, gamma, beta)
    x = _layernorm(x + _L0_attn_ref(x, L0_attn_norm1_w, L0_attn_norm2_w, L0_attn_in_proj_w, L0_attn_in_proj_b, L0_attn_conv_w, L0_attn_conv_b, L0_attn_x_proj_w, L0_attn_dt_proj_w, L0_attn_dt_proj_b, L0_attn_A_log, L0_attn_D_ssm, L0_attn_out_proj_w, L0_attn_out_proj_b, L0_attn_proj_write_w, L0_attn_proj_read_w, L0_attn_decay), axis=-1)
    x = _layernorm(x + _L0_xattn_ref(x, ctx_768, mask_BxS2_bf1, L0_xattn_Wq, L0_xattn_Wk, L0_xattn_Wv, L0_xattn_Wo), axis=-1)
    x = _layernorm(x + _L0_ffn_ref(x, L0_ffn_Wg, L0_ffn_bg, L0_ffn_W1, L0_ffn_b1, L0_ffn_W2, L0_ffn_b2, L0_ffn_gamma, L0_ffn_beta), axis=-1)
    return x

_drawn_inputs = setup_inputs


def setup_inputs(seed=0):
    import zlib

    import numpy as np

    out = dict(_drawn_inputs(seed))
    spreads = {'L0_attn_norm1_w': (1.0, 0.6),
     'L0_attn_norm2_w': (1.0, 0.6),
     'L0_attn_in_proj_b': (0.0, 0.8),
     'L0_attn_conv_b': (0.0, 0.8),
     'L0_attn_D_ssm': (1.0, 0.6),
     'L0_attn_out_proj_b': (0.0, 0.1),
     'L0_ffn_gamma': (1.0, 0.2),
     'L0_ffn_beta': (0.0, 0.1)}
    factors = {'L0_attn_in_proj_w': 8.0,
     'L0_attn_conv_w': 8.0,
     'L0_attn_x_proj_w': 8.0,
     'L0_attn_dt_proj_w': 8.0,
     'L0_attn_dt_proj_b': 8.0,
     'L0_attn_A_log': 8.0,
     'L0_attn_out_proj_w': 8.0,
     'L0_ffn_bg': 4.066,
     'L0_ffn_b1': 8.0,
     'L0_ffn_b2': 8.0}
    for name, (base, spread) in spreads.items():
        noise = np.random.default_rng([zlib.crc32(name.encode()), seed]).standard_normal(out[name].shape)
        drawn = base * np.exp(spread * noise) if base else spread * noise
        out[name] = jnp.asarray(drawn.astype(out[name].dtype))
    for name, factor in factors.items():
        out[name] = (out[name] * factor).astype(out[name].dtype)
    return out
```

```python
from contextlib import ExitStack

import numpy as np

import concourse.bass as bass
from concourse import mybir

ALU = mybir.AluOpType
ACT = mybir.ActivationFunctionType
AX = mybir.AxisListType
F32 = mybir.dt.float32
I32 = mybir.dt.int32
U32 = mybir.dt.uint32
U8 = mybir.dt.uint8

P = 128
EPS = 1e-5
ALPHA = 0.1
MASKED = -1.0e30
SMALL_E = 2.0 ** -7
SHRINK = 2.0 ** -40
VAR_LIMIT = float(np.finfo(np.float32).max) * SHRINK ** 2
RING = 4
BANK = 512


def offsets(stages):
    at, first = 0, {}
    for name, count in stages:
        first[name] = at
        at += count
    return first, at


def decoder_layer(nc, x, ctxT, ctx_mask, norm1_w, norm2_w, in_wT, in_b, conv_w, conv_b, xp_wT, dt_wT, dt_b,
                  A_log, D_ssm, out_wT, out_b, write_wT, read_wT, decay, Wq, Wk, Wv, Wo,
                  Wg, bg, W1, b1, W2, b2, gamma, beta, out):
    B, T, D = x.shape
    DI = out_wT.shape[0]
    NS = A_log.shape[2]
    R = dt_wT.shape[0]
    TAPS = conv_w.shape[2]
    CD, M = ctxT.shape[1], ctxT.shape[2]
    HEADS = 16
    HD = D // HEADS
    E = Wg.shape[1]
    HID = W1.shape[2]
    TT = T // P
    KD = D // P
    KI = DI // P
    HALF = T // 2
    JT = HALF // P
    KH = HID // P
    CH = B * T // BANK
    NT = B * T // P
    CP = CD // 2
    VW = HD + 1
    assert HALF == BANK and M * 8 == BANK and KI * P == BANK

    MAMBA_A = [("xnT", 2 * KD), ("in", 4 * KI), ("rank", 2), ("bc", 2), ("uT", TT)]
    MAMBA_D = [("z", 2 * KI), ("y", 2 * KI), ("mo", TT // 2)]
    SEQ_A = [(f"{n}{m}", c) for m in range(2) for n, c in MAMBA_A] + [
        ("oT", 2 * KD), ("v", TT // 2), ("rT", 2 * KD),
        ("xaT", 2 * KD), ("qT", 2 * KD), ("probs", 3 * TT)]
    MEM_S = [(i, h) for i in range(TT) for h in range(2) if (h + 1) * JT > i]
    SEQ_D = [(f"{n}{m}", c) for m in range(2) for n, c in MAMBA_D] + [
        ("mem", len(MEM_S)), ("rp", TT // 2), ("score", 3 * TT), ("wo", TT // 2)]
    OFF_A, PER_A = offsets(SEQ_A)
    OFF_D, PER_D = offsets(SEQ_D)
    SETUP_D = 4
    assert PER_A % RING == 0 and PER_D % RING == 0 and all(v % RING == 0 for v in
           (OFF_A["uT1"], OFF_A["oT"], OFF_D["mem"]))

    def job_a(b, stage, j):
        return b * PER_A + (OFF_A[stage] + j)

    def job_d(b, stage, j):
        return b * PER_D + (SETUP_D + OFF_D[stage] + j)

    def bank_a(stage, j):
        return (OFF_A[stage] + j) % RING

    def bank_d(stage, j):
        return (OFF_D[stage] + j) % RING

    END_A, END_D = B * PER_A, SETUP_D + B * PER_D
    OFF_FA, PRE_FA = offsets([("x2T", KD * CH), ("combT", NT // 4)])
    OFF_FD, PRE_FD = offsets([("logits", 4), ("b2", NT // 2)])

    with ExitStack() as ctx:
        def sb(name, shape, dt=F32):
            return ctx.enter_context(nc.sbuf_tensor(name, shape, dt))

        def sem(name):
            return ctx.enter_context(nc.semaphore(name))

        psA = ctx.enter_context(nc.psum_tensor("psA", [P, RING, BANK], F32))
        psD = ctx.enter_context(nc.psum_tensor("psD", [P, RING, BANK], F32))

        x2_dram = nc.dram_tensor("x2_dram", (NT, P, D), F32, kind="Internal").ap()

        ident = sb("ident", [P, P])
        ones = sb("ones", [P, P])
        in_w_sb = sb("in_w_sb", [P, KD, 2 * DI])
        out_w_sb = sb("out_w_sb", [P, KI, D])
        xp_w_sb = sb("xp_w_sb", [P, KI, R + 2 * NS])
        dt_w_sb = sb("dt_w_sb", [R, DI])
        write_w_sb = sb("write_w_sb", [P, KD, D])
        read_w_sb = sb("read_w_sb", [P, KD, D])
        wq_sb = sb("wq_sb", [P, KD, D])
        wo_sb = sb("wo_sb", [P, KD, D])
        norm_sb = sb("norm_sb", [P, 2, KD])
        in_b_sb = sb("in_b_sb", [P, 2 * KI])
        conv_w_sb = sb("conv_w_sb", [P, KI, TAPS])
        conv_b_sb = sb("conv_b_sb", [P, KI])
        dt_b_sb = sb("dt_b_sb", [P, KI])
        d_sb = sb("d_sb", [P, KI])
        alog_sb = sb("alog_sb", [P, KI, NS])
        negA = sb("negA", [P, KI, NS])
        out_b_sb = sb("out_b_sb", [P, D])
        lng = sb("lng", [P, 8])
        strip = sb("strip", [P, T])
        kT = sb("kT", [P, KD, B, M])
        vdup = sb("vdup", [P, B, D])
        eps_sb = sb("eps_sb", [P, 2])
        headmask = sb("headmask", [P, 8])
        pairmask = sb("pairmask", [P, 2])
        mask_u8 = sb("mask_u8", [1, B, M], U8)
        mask_row = sb("mask_row", [1, B, M])
        ss = sb("ss", [P, TT])
        rt = sb("rt", [P, TT])
        rs = sb("rs", [P, TT])
        stats = sb("stats", [P, TT, 6])
        aggr = sb("aggr", [P, TT, 2])
        bc = sb("bc", [P, TT, 2 * NS])
        bcol = sb("bcol", [P, 2, JT])
        mx = sb("mx", [P, 2, 8])
        rsum = sb("rsum", [P, HEADS])

        WORDS = 41100
        arena = sb("arena", [P, WORDS])
        at = [0]

        def carve(n):
            at[0] += n
            assert at[0] <= WORDS, at
            return arena[:, at[0] - n:at[0]]

        xin = carve(TT * D).rearrange("p (t d) -> p t d", d=D)
        x1 = carve(TT * D).rearrange("p (t d) -> p t d", d=D)
        base = carve(TT * D).rearrange("p (t d) -> p t d", d=D)
        g_flat = carve(2 * JT * DI)
        g = g_flat.rearrange("p (u j d) -> p u j d", u=2, j=JT)
        xn = g_flat[:, 0:TT * D].rearrange("p (t d) -> p t d", d=D)
        rank_sb = g_flat[0:R, 0:T]
        xnT_flat = carve(KD * (T + 1))
        xnT = xnT_flat.rearrange("p (k t) -> p k t", k=KD)
        pre_flat = carve(KI * (T + TAPS - 1))
        pre = pre_flat.rearrange("p (k t) -> p k t", k=KI)
        uT = pre_flat[:, 0:TT * DI].rearrange("p (t d) -> p t d", d=DI)
        sm_flat = carve(2 * KI * T)
        xm = sm_flat[:, 0:KI * T].rearrange("p (k t) -> p k t", k=KI)
        gate = sm_flat[:, KI * T:2 * KI * T].rearrange("p (k t) -> p k t", k=KI)
        dt = carve(KI * T).rearrange("p (k t) -> p k t", k=KI)
        yT_flat = carve(TT * DI)
        yT = yT_flat.rearrange("p (t d) -> p t d", d=DI)
        h_flat = carve(2 * KI * HALF)
        h = h_flat.rearrange("p (u k t) -> p u k t", u=2, k=KI)
        dtu = h_flat.rearrange("p (k t) -> p k t", k=KI)
        da_flat = carve(2 * KI * HALF)
        da = da_flat.rearrange("p (u k t) -> p u k t", u=2, k=KI)
        soft_e = da_flat.rearrange("p (k t) -> p k t", k=KI)
        soft_ln = yT_flat.rearrange("p (k t) -> p k t", k=KI)
        series = dtu
        is_small = xnT_flat[:, 0:KI * T // 4].bitcast(U8).rearrange("p (k t) -> p k t", k=KI)
        y = da_flat.rearrange("p (k t) -> p k t", k=KI)
        o2 = x2_out = g_flat[:, 0:TT * D].rearrange("p (t d) -> p t d", d=D)
        oT = xnT
        v_sb = g_flat[:, TT * D:2 * TT * D].rearrange("p (t d) -> p t d", d=D)
        sm_first, sm_words = offsets([((i, hh), (hh + 1) * BANK - max(P * i, hh * BANK)) for i, hh in MEM_S])
        assert sm_words <= 2 * KI * T
        rT = yT_flat[:, 0:KD * T].rearrange("p (k t) -> p k t", k=KD)
        xa = x1
        xaT = yT_flat[:, KD * T:2 * KD * T].rearrange("p (k t) -> p k t", k=KD)
        qT = h_flat[:, 0:KD * T].rearrange("p (k t) -> p k t", k=KD)
        attT = h_flat[:, KD * T:2 * KD * T].rearrange("p (k t) -> p k t", k=KD)
        prob = da_flat[:, 0:2 * 2 * BANK].rearrange("p (u n c) -> p u n c", u=2, n=2)
        probT = da_flat[:, 2 * 2 * BANK:4 * 2 * BANK].rearrange("p (u n c) -> p u n c", u=2, n=2)
        att = pre_flat[:, 0:2 * D].rearrange("p (u d) -> p u d", u=2)
        kblk = pre_flat[:, 1024:1024 + KD * 8 * M].rearrange("p (k h m) -> p k h m", k=KD, h=8)
        vblk = pre_flat[:, 2048:2048 + HEADS * VW].rearrange("p (q r d) -> p q r d", r=2, d=VW)
        at[0] = 0
        x2 = carve(NT * D).rearrange("p (t d) -> p t d", d=D)
        acc = carve(NT * D).rearrange("p (t d) -> p t d", d=D)
        x2T = carve(NT * D).rearrange("p (k t) -> p k t", k=KD)
        w1_sb = carve(2 * KD * HID).rearrange("p (u k f) -> p u k f", u=2, k=KD)
        w2_flat = carve(2 * KH * D)
        w2_sb = w2_flat.rearrange("p (u k f) -> p u k f", u=2, k=KH)
        hT_flat = carve(KH * BANK)
        hT = hT_flat.rearrange("p (k t) -> p k t", k=KH)
        combT = hT_flat[0:E, 0:NT * P]
        small = in_w_sb[:, :, :].rearrange("p k f -> p (k f)")
        logit = small[:, 0:NT * E].rearrange("p (t e) -> p t e", e=E)
        top = small[:, NT * E:2 * NT * E].rearrange("p (t e) -> p t e", e=E)
        topi = small[:, 2 * NT * E:3 * NT * E].bitcast(U32).rearrange("p (t e) -> p t e", e=E)
        comb = small[:, 3 * NT * E:4 * NT * E].rearrange("p (t e) -> p t e", e=E)
        hot = small[:, 4 * NT * E:5 * NT * E].rearrange("p (t e) -> p t e", e=E)
        topf = small[:, 5 * NT * E:6 * NT * E].rearrange("p (t e) -> p t e", e=E)
        rest = small[:, 6 * NT * E:7 * NT * E].rearrange("p (k t) -> p k t", k=8)
        wg_sb = sb("wg_sb", [P, KD, E])
        bg_sb = sb("bg_sb", [P, E])
        b1_sb = sb("b1_sb", [P, E, KH])
        b2_sb = sb("b2_sb", [E, D])
        expert_id = sb("expert_id", [P, E])
        expert_i = sb("expert_i", [P, E], I32)
        gamma_sb = sb("gamma_sb", [P, D])
        beta_sb = sb("beta_sb", [P, D])
        fstats = sb("fstats", [P, 2, TT, 6])
        faggr = sb("faggr", [P, 2, TT, 2])
        frt = sb("frt", [P, 2, 2, TT])
        iota_i = base[:, 0:T // D, :].rearrange("p t d -> p (t d)").bitcast(I32)
        ctx_sb = gate[0:CP, 0, 0:2 * B * 2 * M].rearrange("p (c b m) -> p c b m", c=2, b=B)
        wk_sb = gate[0:CP, 1, 0:2 * D].rearrange("p (c d) -> p c d", c=2)
        wv_sb = gate[0:CP, 2, 0:2 * D].rearrange("p (c d) -> p c d", c=2)

        w_loaded = sem("w_loaded")
        x_loaded = sem("x_loaded")
        act_full, act_drained = sem("act_full"), sem("act_drained")
        dve_full, dve_drained = sem("dve_full"), sem("dve_drained")
        consts_step = sem("consts_step")
        consts_ready = sem("consts_ready")
        dve_setup = sem("dve_setup")
        act_setup = sem("act_setup")
        squares = sem("squares")
        root = sem("root")
        inverse = sem("inverse")
        normed = sem("normed")
        pads_zero = sem("pads_zero")
        conv_step = sem("conv_step")
        xm_ready = sem("xm_ready")
        soft_step = sem("soft_step")
        series_step = sem("series_step")
        dt_ready = sem("dt_ready")
        dtu_ready = sem("dtu_ready")
        y_zero = sem("y_zero")
        bcol_ready = sem("bcol_ready")
        g_ready = sem("g_ready")
        da_ready = sem("da_ready")
        dbu_full = sem("dbu_full")
        scanned = sem("scanned")
        hT_full = sem("hT_full")
        summed = sem("summed")
        gated = sem("gated")
        xb_ready = sem("xb_ready")
        sum01 = sem("sum01")
        base_ready = sem("base_ready")
        ln_stats = sem("ln_stats")
        ln_done = sem("ln_done")
        blocks_ready = sem("blocks_ready")
        score_max = sem("score_max")
        expo = sem("expo")
        sum_inv = sem("sum_inv")
        mix_ready = sem("mix_ready")
        route_step = sem("route_step")
        w1_loaded = [sem("w1_loaded0"), sem("w1_loaded1")]
        w2_loaded = [sem("w2_loaded0"), sem("w2_loaded1")]
        x2_stored = sem("x2_stored")
        x2_loaded = sem("x2_loaded")
        eps_ready = sem("eps_ready")
        expert_ready = sem("expert_ready")
        gap_exp = sem("gap_exp")
        fin_step = sem("fin_step")
        fin_root = sem("fin_root")
        fin_pool = sem("fin_pool")
        stored = sem("stored")
        waits_passed = sem("waits_passed")

        UNITS = 2 * NS

        def alone(engine):
            engine.sem_inc(waits_passed, 1)

        def unit(b, m, s, half):
            return b * (2 * UNITS) + s * 2 + (m * UNITS + half)

        def score_job(t, n):
            return n if t == 0 else 3 * t - 1 + n

        def out_job(t):
            return 3 * t + 4 if t + 1 < TT else 3 * TT - 1

        ROUTE_TOP = 2 * NT
        ROUTE_DIFF = ROUTE_TOP + 2
        ROUTE_ALL = ROUTE_DIFF + 5
        FIN_NORM = 3 * TT + 1
        FIN_PER = 2 * FIN_NORM + 3

        block = ctx.enter_context(nc.Block())

        loads = [
            (in_w_sb[:, :, :], in_wT.rearrange("(k p) f -> p k f", p=P)),
            (out_w_sb[:, :, :], out_wT.rearrange("(k p) f -> p k f", p=P)),
            (xp_w_sb[:, :, :], xp_wT.rearrange("(k p) f -> p k f", p=P)),
            (dt_w_sb[:, :], dt_wT),
            (write_w_sb[:, :, :], write_wT.rearrange("(k p) f -> p k f", p=P)),
            (read_w_sb[:, :, :], read_wT.rearrange("(k p) f -> p k f", p=P)),
            (wq_sb[:, :, :], Wq.rearrange("(k p) f -> p k f", p=P)),
            (wo_sb[:, :, :], Wo.rearrange("(k p) f -> p k f", p=P)),
            (norm_sb[:, 0, :], norm1_w),
            (norm_sb[:, 1, :], norm2_w),
            (in_b_sb[:, :], in_b),
            (conv_w_sb[:, :, :], conv_w),
            (conv_b_sb[:, :], conv_b),
            (dt_b_sb[:, :], dt_b),
            (d_sb[:, :], D_ssm),
            (alog_sb[:, :, :], A_log),
            (out_b_sb[:, :], out_b.rearrange("(a n) -> a n", a=1).broadcast_to([P, D])),
            (lng[:, 0:1], decay.rearrange("(a n) -> a n", a=1).broadcast_to([P, 1])),
            (mask_u8[:, :, :], ctx_mask.rearrange("(a b) m -> a b m", a=1)),
            (wk_sb[:, :, :], Wk.rearrange("(c p) f -> p c f", p=CP)),
            (wv_sb[:, :, :], Wv.rearrange("(c p) f -> p c f", p=CP)),
            (wg_sb[:, :, :], Wg.rearrange("(k p) f -> p k f", p=P)),
            (bg_sb[:, :], bg.rearrange("(a n) -> a n", a=1).broadcast_to([P, E])),
            (b2_sb[:, :], b2),
            (gamma_sb[:, :], gamma.rearrange("(a n) -> a n", a=1).broadcast_to([P, D])),
            (beta_sb[:, :], beta.rearrange("(a n) -> a n", a=1).broadcast_to([P, D])),
            (b1_sb[:, :, :], b1),
        ] + [(ctx_sb[:, :, b, r * M:(r + 1) * M], ctxT[b].rearrange("(c p) m -> p c m", p=CP))
             for b in range(B) for r in range(2)]
        LOADED = 16 * len(loads)

        @block.sync
        def _(sp):
            sp.sem_inc(x2_stored, 16)
            sp.dma_start(xin, x[0].rearrange("(t p) d -> p t d", p=P)).then_inc(x_loaded, 16)
            for dst, src in loads:
                sp.dma_start(dst, src).then_inc(w_loaded, 16)
            def keep_x2(b):
                sp.wait_ge(ln_done, b * (2 * TT) + 2 * TT)
                sp.dma_start(x2_dram[bass.ds(b * TT, TT)].rearrange("t p d -> p t d"), x2_out).then_inc(x2_stored, 16)

            with sp.Fori(0, B - 1) as b:
                sp.wait_ge(sum01, b + 1)
                sp.dma_start(xin, x[bass.ds(b + 1, 1)].rearrange("a (t p) d -> p (a t) d", p=P))\
                  .then_inc(x_loaded, 16)
                keep_x2(b)
            keep_x2(B - 1)
            for e in range(2):
                sp.dma_start(w1_sb[:, e, :, :], W1[e].rearrange("(k p) f -> p k f", p=P)).then_inc(w1_loaded[e], 16)
                sp.dma_start(w2_sb[:, e, :, :], W2[e].rearrange("(k p) f -> p k f", p=P)).then_inc(w2_loaded[e], 16)
            sp.wait_ge(x2_stored, 16 * B + 16)
            sp.dma_start(x2, x2_dram.rearrange("t p d -> p t d")).then_inc(x2_loaded, 16)
            with sp.Fori(1, E // 2) as pair:
                for r in range(2):
                    e = pair * 2
                    sp.wait_ge(dve_full, e * (CH * 2) + (END_D + PRE_FD + (r - 1) * CH * 2))
                    sp.dma_start(w1_sb[:, r, :, :], W1[bass.ds(e + r, 1)].rearrange("a (k p) f -> p (a k) f", p=P))\
                      .then_inc(w1_loaded[r], 16)
                    sp.dma_start(w2_sb[:, r, :, :], W2[bass.ds(e + r, 1)].rearrange("a (k p) f -> p (a k) f", p=P))\
                      .then_inc(w2_loaded[r], 16)
            out_v = out.rearrange("b (t p) d -> p (b t) d", p=P)
            for q in range(B):
                sp.wait_ge(fin_step, FIN_PER * (q + 1))
                sp.dma_start(out_v[:, q * TT:(q + 1) * TT, :], acc[:, q * TT:(q + 1) * TT, :]).then_inc(stored, 16)
            sp.wait_ge(stored, 16 * B)

        @block.gpsimd
        def _(pool):
            step = 0
            pool.memset(ident[:, :], 0.0).then_inc(consts_step, 1)
            pool.memset(ones[:, :], 1.0).then_inc(consts_ready, 1)
            pool.memset(headmask[:, :], 1.0 / float(HD) ** 0.5).then_inc(consts_step, 1)
            pool.memset(pairmask[:, :], 1.0).then_inc(consts_step, 1)
            pool.iota(iota_i, pattern=[[1, T]], base=-1, channel_multiplier=-1).then_inc(consts_ready, 1)
            pool.iota(expert_i[:, :], pattern=[[1, E]], base=0, channel_multiplier=0).then_inc(consts_ready, 1)
            pool.wait_ge(consts_step, 3)
            pool.affine_select(out=ident[:, :], in_=ident[:, :], compare_op=ALU.not_equal, fill=1.0, base=0,
                               pattern=[[-1, P]], channel_multiplier=1).then_inc(consts_ready, 1)
            pool.affine_select(out=headmask[:, :], in_=headmask[:, :], compare_op=ALU.is_ge, fill=0.0, base=0,
                               pattern=[[-HD, 8]], channel_multiplier=1).then_inc(consts_step, 1)
            pool.wait_ge(consts_step, 4)
            pool.affine_select(out=headmask[:, :], in_=headmask[:, :], compare_op=ALU.is_ge, fill=0.0, base=HD - 1,
                               pattern=[[HD, 8]], channel_multiplier=-1).then_inc(consts_ready, 1)
            pool.affine_select(out=pairmask[:, 0:1], in_=pairmask[:, 0:1], compare_op=ALU.is_ge, fill=0.0,
                               base=M - 1, pattern=[[0, 1]], channel_multiplier=-1).then_inc(consts_ready, 1)
            pool.affine_select(out=pairmask[:, 1:2], in_=pairmask[:, 1:2], compare_op=ALU.is_ge, fill=0.0,
                               base=-M, pattern=[[0, 1]], channel_multiplier=1).then_inc(consts_ready, 1)
            pool.wait_ge(act_setup, 5)
            pool.affine_select(out=strip[:, :], in_=strip[:, :], compare_op=ALU.is_ge, fill=0.0, base=-1,
                               pattern=[[1, T]], channel_multiplier=-1).then_inc(consts_ready, 1)
            pool.sem_inc(g_ready, JT + 1)
            with pool.Fori(0, B) as b:
                for m in range(2):
                    if m == 0:
                        pool.wait_ge(x2_stored, b * 16 + 16)
                        pool.wait_ge(x_loaded, b * 16 + 16)
                        pool.wait_ge(w_loaded, LOADED)
                        pool.tensor_tensor(base[:, :, :], xin[:, :, :],
                                           out_b_sb[:, :].unsqueeze(1).broadcast_to([P, TT, D]), ALU.add)\
                            .then_inc(xb_ready, 1)
                        pool.wait_ge(xb_ready, b + 1)
                    else:
                        pool.wait_ge(dve_drained, job_d(b, "mo0", TT // 2) + RING)
                        pool.tensor_tensor(base[:, :, :], xin[:, :, :], x1[:, :, :], ALU.add).then_inc(sum01, 1)
                    pool.wait_ge(dtu_ready, b * (2 * KI) + (m * KI + KI))
                    alone(pool)
                    pool.memset(yT_flat, 0.0).then_inc(y_zero, 1)
                    pool.wait_ge(act_drained, job_a(b, f"uT{m}", TT) + RING)
                    alone(pool)
                    with pool.Fori(0, NS) as s:
                        for half in range(2):
                            u = unit(b, m, s, half)
                            pool.wait_ge(bcol_ready, u + 1)
                            pool.wait_ge(dbu_full, u * KI + 1)
                            alone(pool)
                            for j in range(JT):
                                pool.tensor_scalar(g[:, half, j, :], uT[:, half * JT + j, :], bcol[:, half, j:j + 1],
                                                   1.0, ALU.mult, ALU.mult).then_inc(g_ready, 1)
                pool.wait_ge(dve_drained, job_d(b, "mo1", TT // 2) + RING)
                pool.wait_ge(sum01, b + 1)
                pool.tensor_tensor(base[:, :, :], base[:, :, :], o2[:, :, :], ALU.add).then_inc(base_ready, 1)
                pool.wait_ge(base_ready, b * 2 + 1)
                alone(pool)
                pool.tensor_scalar(base[:, :, :], base[:, :, :], SHRINK, 1.0, ALU.mult, ALU.mult).then_inc(base_ready, 1)

        @block.scalar
        def _(act):
            act.sem_inc(act_drained, RING)
            act.wait_ge(eps_ready, 2)
            act.wait_ge(w_loaded, LOADED)
            act.activation(lng[:, 1:2], lng[:, 0:1], ACT.Abs).then_inc(act_setup, 1)
            act.activation(alog_sb[:, :, :], alog_sb[:, :, :], ACT.Exp).then_inc(act_setup, 1)
            act.wait_ge(act_setup, 2)
            act.activation(lng[:, 2:3], lng[:, 1:2], ACT.Exp, scale=-1.0).then_inc(act_setup, 1)
            act.wait_ge(act_setup, 3)
            act.activation(lng[:, 3:4], lng[:, 2:3], ACT.Ln, bias=1.0).then_inc(act_setup, 1)
            act.wait_ge(dve_setup, 4)
            act.activation(strip[:, :], strip[:, :], ACT.Exp, scale=lng[:, 5:6]).then_inc(act_setup, 1)

            def drain(job, bank, dst, width=BANK, func=ACT.Copy, **kw):
                act.wait_ge(act_full, job + 1)
                act.activation(dst, psA[:, bank, 0:width], func, **kw).then_inc(act_drained, 1)

            def turned(b, stage, dst, scale=None, shift=0):
                for j in range(2 * KD):
                    k, half = j // 2, j % 2
                    kw = {} if scale is None else {"scale": scale[:, k:k + 1]}
                    drain(job_a(b, stage, j), bank_a(stage, j),
                          dst[:, k, shift + half * HALF:shift + (half + 1) * HALF], **kw)

            def root_of(dst, src, scale, ready, eps=0):
                act.wait_ge(*ready)
                act.activation(dst, src, ACT.Sqrt, scale=scale, bias=eps_sb[:, eps:eps + 1]).then_inc(root, 1)

            def mamba(b, m):
                blk = b * 2 + m
                src = xin if m == 0 else x1
                if m == 0:
                    act.wait_ge(x_loaded, b * 16 + 16)
                    act.wait_ge(x2_stored, b * 16 + 16)
                else:
                    act.wait_ge(dve_drained, job_d(b, "mo0", TT // 2) + RING)
                for t in range(TT):
                    act.activation(xn[:, t, :], src[:, t, :], ACT.Square, accum_out=ss[:, t:t + 1]).then_inc(squares, 1)
                root_of(rt[:, :], ss[:, :], 1.0 / D, (squares, blk * TT + TT))
                turned(b, f"xnT{m}", xnT, norm_sb[:, m, :])
                act.wait_ge(pads_zero, blk + 1)
                for j in range(4 * KI):
                    f, half = j // 2, j % 2
                    if f < KI:
                        drain(job_a(b, f"in{m}", j), bank_a(f"in{m}", j),
                              pre[:, f, TAPS - 1 + half * HALF:TAPS - 1 + (half + 1) * HALF],
                              func=ACT.Identity, bias=in_b_sb[:, f:f + 1])
                    else:
                        drain(job_a(b, f"in{m}", j), bank_a(f"in{m}", j),
                              gate[:, f - KI, half * HALF:(half + 1) * HALF],
                              func=ACT.Silu, bias=in_b_sb[:, f:f + 1])
                for f in range(KI):
                    act.wait_ge(conv_step, blk * (TAPS * KI) + TAPS * (f + 1))
                    act.activation(xm[:, f, :], xm[:, f, :], ACT.Silu).then_inc(xm_ready, 1)
                for j in range(2):
                    act.wait_ge(act_full, job_a(b, f"rank{m}", j) + 1)
                    act.activation(rank_sb[:, j * HALF:(j + 1) * HALF], psA[0:R, bank_a(f"rank{m}", j), :], ACT.Copy)\
                       .then_inc(act_drained, 1)
                for j in range(2):
                    act.wait_ge(act_full, job_a(b, f"bc{m}", j) + 1)
                    act.activation(bc[:, j * JT:(j + 1) * JT, :], psA[:, bank_a(f"bc{m}", j), 0:JT * 2 * NS]
                                   .rearrange("p (t c) -> p t c", t=JT), ACT.Copy).then_inc(act_drained, 1)
                for f in range(KI):
                    act.wait_ge(dve_drained, job_d(b, f"z{m}", 2 * f + 1) + 1 + RING)
                    act.activation(soft_e[:, f, :], dt[:, f, :], ACT.Abs).then_inc(soft_step, 1)
                for f in range(KI):
                    act.wait_ge(soft_step, blk * (4 * KI) + f + 1)
                    act.activation(soft_e[:, f, :], soft_e[:, f, :], ACT.Exp, scale=-1.0).then_inc(soft_step, 1)
                for f in range(KI):
                    act.wait_ge(soft_step, blk * (4 * KI) + KI + f + 1)
                    act.activation(series[:, f, :], soft_e[:, f, :], ACT.Copy, scale=1.0 / 3.0, bias=-0.5)\
                       .then_inc(soft_step, 1)
                    act.activation(soft_ln[:, f, :], soft_e[:, f, :], ACT.Ln, bias=1.0).then_inc(soft_step, 1)
                for j in range(TT):
                    drain(job_a(b, f"uT{m}", j), bank_a(f"uT{m}", j), uT[:, j, :])
                act.wait_ge(dt_ready, blk * KI + KI)
                with act.Fori(0, NS) as s:
                    for half in range(2):
                        u = unit(b, m, s, half)
                        act.wait_ge(g_ready, u * JT + 1)
                        act.activation(bcol[:, half, :], bc[:, half * JT:(half + 1) * JT, bass.ds(s, 1)]
                                       .rearrange("p t o -> p (t o)"), ACT.Copy).then_inc(bcol_ready, 1)
                        act.wait_ge(scanned, u * KI + 1)
                        alone(act)
                        for f in range(KI):
                            act.activation(da[:, half, f, :], dt[:, f, half * HALF:(half + 1) * HALF], ACT.Exp,
                                           scale=negA[:, f, bass.ds(s, 1)]).then_inc(da_ready, 1)

            with act.Fori(0, B) as b:
                for m in range(2):
                    mamba(b, m)
                turned(b, "oT", oT, shift=1)
                for j in range(TT // 2):
                    drain(job_a(b, "v", j), bank_a("v", j), v_sb[:, 2 * j:2 * j + 2, :].rearrange("p t d -> p (t d)"))
                turned(b, "rT", rT)
                root_of(rt[:, :], aggr[:, :, 1], 1.0, (ln_stats, b * (4 * TT) + 2 * TT), 1)
                turned(b, "xaT", xaT)
                turned(b, "qT", qT)

                def exps(t):
                    for n in range(2):
                        act.wait_ge(dve_drained, job_d(b, "score", score_job(t, n)) + 1 + RING)
                        act.activation(prob[:, t % 2, n, :], prob[:, t % 2, n, :], ACT.Exp).then_inc(expo, 1)

                def rest_of(t):
                    for n in range(2):
                        drain(job_a(b, "probs", 3 * t + n), bank_a("probs", 3 * t + n), probT[:, t % 2, n, :])
                    act.wait_ge(act_full, job_a(b, "probs", 3 * t + 2) + 1)
                    act.activation(attT[:, :, t * P:(t + 1) * P], psA[:, bank_a("probs", 3 * t + 2), 0:KD * P]
                                   .rearrange("p (k t) -> p k t", k=KD), ACT.Copy).then_inc(act_drained, 1)

                exps(0)
                for t in range(TT):
                    if t + 1 < TT:
                        exps(t + 1)
                    rest_of(t)
                root_of(rt[:, :], aggr[:, :, 1], 1.0, (ln_stats, b * (4 * TT) + 4 * TT))

            for j in range(KD * CH):
                k, c = j % KD, j // KD
                drain(END_A + j, j % RING, x2T[:, k, c * BANK:(c + 1) * BANK])
            act.wait_ge(route_step, ROUTE_DIFF)
            act.activation(rest[:, 1, :], rest[:, 0, :], ACT.Exp).then_inc(gap_exp, 1)
            for j in range(NT // 4):
                n = END_A + OFF_FA["combT"] + j
                act.wait_ge(act_full, n + 1)
                act.activation(combT[:, j * BANK:(j + 1) * BANK], psA[0:E, n % RING, :], ACT.Copy).then_inc(act_drained, 1)
            act.wait_ge(dve_full, END_D + PRE_FD)
            with act.Fori(0, E) as e:
                with act.Fori(0, CH) as c:
                    job = (e * CH + c) * KH + (END_A + PRE_FA)
                    act.wait_ge(dve_full, (e * CH + c) * 2 + (END_D + PRE_FD))
                    for k in range(KH):
                        act.wait_ge(act_full, job + (k + 1))
                        act.activation(hT[:, k, :], psA[:, k % RING, :], ACT.Gelu, bias=b1_sb[:, bass.ds(e, 1), k]
                                       ).then_inc(act_drained, 1)
            for q in range(B):
                for r in range(2):
                    act.wait_ge(fin_step, FIN_PER * q + r * (FIN_NORM + 3) + 2 * TT)
                    act.activation(frt[:, q % 2, r, :], faggr[:, q % 2, :, 1], ACT.Sqrt, bias=eps_sb[:, 0:1])\
                       .then_inc(fin_root, 1)

        @block.tensor
        def _(pe):
            def claim_a(job):
                pe.wait_ge(act_drained, job + 1)

            def claim_d(job):
                pe.wait_ge(dve_drained, job + 1)

            def turn(b, stage, src):
                for j in range(2 * KD):
                    k, half = j // 2, j % 2
                    claim_a(job_a(b, stage, j))
                    for t in range(JT):
                        mm = pe.transpose(psA[:, bank_a(stage, j), t * P:(t + 1) * P],
                                          src[:, half * JT + t, k * P:(k + 1) * P], ident[:, :])
                    mm.then_inc(act_full, 1)

            def product(out_ap, pairs):
                for i, (lhs, rhs) in enumerate(pairs):
                    mm = pe.matmul(out_ap, lhs, rhs, start=i == 0, stop=i == len(pairs) - 1)
                return mm

            def token_rows(bank, ps, t0, lhs, rhs, tiles):
                for r in range(2):
                    mm = product(ps[:, bank, r * D:(r + 1) * D],
                                 [(lhs[:, k, (t0 + r) * P:(t0 + r + 1) * P], rhs[:, k, :]) for k in range(tiles)])
                return mm

            pe.wait_ge(w_loaded, LOADED)
            pe.wait_ge(consts_ready, 8)
            for m in range(KD):
                claim_d(m)
                product(psD[:, m, 0:B * M].rearrange("p (b m) -> p b m", b=B), [(wk_sb[:, c, m * P:(m + 1) * P], ctx_sb[:, c, :, 0:M]) for c in range(2)])\
                    .then_inc(dve_full, 1)
            for j in range(B // 2):
                claim_d(KD + j)
                for r in range(2):
                    mm = product(psD[:, KD + j, r * D:(r + 1) * D],
                                 [(ctx_sb[:, c, 2 * j + r, :], wv_sb[:, c, :]) for c in range(2)])
                mm.then_inc(dve_full, 1)

            def mamba(b, m):
                blk = b * 2 + m
                pe.wait_ge(normed, blk * TT + TT)
                turn(b, f"xnT{m}", xn)
                pe.wait_ge(act_drained, job_a(b, f"xnT{m}", 2 * KD) + RING)
                for j in range(4 * KI):
                    f, half = j // 2, j % 2
                    claim_a(job_a(b, f"in{m}", j))
                    product(psA[:, bank_a(f"in{m}", j), :],
                            [(in_w_sb[:, k, f * P:(f + 1) * P], xnT[:, k, half * HALF:(half + 1) * HALF])
                             for k in range(KD)]).then_inc(act_full, 1)
                pe.wait_ge(xm_ready, blk * KI + KI)
                for j in range(2):
                    claim_a(job_a(b, f"rank{m}", j))
                    product(psA[0:R, bank_a(f"rank{m}", j), :],
                            [(xp_w_sb[:, k, 0:R], xm[:, k, j * HALF:(j + 1) * HALF]) for k in range(KI)])\
                        .then_inc(act_full, 1)
                for j in range(2):
                    claim_a(job_a(b, f"bc{m}", j))
                    for t in range(JT):
                        mm = product(psA[:, bank_a(f"bc{m}", j), t * 2 * NS:(t + 1) * 2 * NS],
                                     [(xm[:, k, (j * JT + t) * P:(j * JT + t + 1) * P], xp_w_sb[:, k, R:R + 2 * NS])
                                      for k in range(KI)])
                    mm.then_inc(act_full, 1)
                for j in range(2 * KI):
                    f, half = j // 2, j % 2
                    pe.wait_ge(act_drained, job_a(b, f"rank{m}", half) + 1 + RING)
                    claim_d(job_d(b, f"z{m}", j))
                    pe.matmul(psD[:, bank_d(f"z{m}", j), :], dt_w_sb[:, f * P:(f + 1) * P],
                              rank_sb[:, half * HALF:(half + 1) * HALF], start=True, stop=True).then_inc(dve_full, 1)
                pe.wait_ge(dtu_ready, blk * KI + KI)
                for j in range(TT):
                    claim_a(job_a(b, f"uT{m}", j))
                    for f in range(KI):
                        mm = pe.transpose(psA[:, bank_a(f"uT{m}", j), f * P:(f + 1) * P],
                                          dtu[:, f, j * P:(j + 1) * P], ident[:, :])
                    mm.then_inc(act_full, 1)
                pe.wait_ge(act_drained, job_a(b, f"uT{m}", TT) + RING)
                pe.wait_ge(dve_drained, job_d(b, f"z{m}", 2 * KI) + RING)

                def inputs(s, half):
                    u = unit(b, m, s, half)
                    pe.wait_ge(g_ready, u * JT + (2 * JT + 1))
                    for f in range(KI):
                        pe.wait_ge(scanned, u * KI + (f + 2))
                        for j in range(JT):
                            mm = pe.transpose(psD[:, f, j * P:(j + 1) * P], g[:, half, j, f * P:(f + 1) * P], ident[:, :])
                        mm.then_inc(dbu_full, 1)

                def states(s, half):
                    u = unit(b, m, s, half)
                    pe.wait_ge(scanned, u * KI + (2 * KI + 1))
                    for j in range(JT):
                        pe.wait_ge(summed, u * JT + (j + 2))
                        for f in range(KI):
                            mm = pe.transpose(psA[:, j, f * P:(f + 1) * P], h[:, half, f, j * P:(j + 1) * P], ident[:, :])
                        mm.then_inc(hT_full, 1)

                inputs(0, 0)
                with pe.Fori(0, NS - 1) as s:
                    inputs(s, 1)
                    states(s, 0)
                    inputs(s + 1, 0)
                    states(s, 1)
                inputs(NS - 1, 1)
                states(NS - 1, 0)
                states(NS - 1, 1)

                last = unit(b, m, NS - 1, 1)
                pe.wait_ge(summed, last * JT + (2 * JT + 1))
                for j in range(2 * KI):
                    f, half = j // 2, j % 2
                    claim_d(job_d(b, f"y{m}", j))
                    for t in range(JT):
                        mm = pe.transpose(psD[:, bank_d(f"y{m}", j), t * P:(t + 1) * P],
                                          yT[:, half * JT + t, f * P:(f + 1) * P], ident[:, :])
                    mm.then_inc(dve_full, 1)
                pe.wait_ge(gated, blk * KI + KI)
                for j in range(TT // 2):
                    claim_d(job_d(b, f"mo{m}", j))
                    token_rows(bank_d(f"mo{m}", j), psD, 2 * j, y, out_w_sb, KI).then_inc(dve_full, 1)

            pe.sem_inc(hT_full, JT + 1)
            pe.sem_inc(dbu_full, KI + 1)
            with pe.Fori(0, B) as b:
                for m in range(2):
                    mamba(b, m)
                pe.wait_ge(dve_drained, job_d(b, "mo1", TT // 2) + RING)
                turn(b, "oT", o2)
                pe.wait_ge(act_drained, job_a(b, "oT", 2 * KD) + RING)
                pe.wait_ge(blocks_ready, b * 3 + 1)
                for j in range(TT // 2):
                    claim_a(job_a(b, "v", j))
                    token_rows(bank_a("v", j), psA, 2 * j, oT[:, :, 1:T + 1], write_w_sb, KD).then_inc(act_full, 1)
                for j, (i, half) in enumerate(MEM_S):
                    lo, hi = max(P * i, half * HALF), (half + 1) * HALF
                    claim_d(job_d(b, "mem", j))
                    product(psD[:, bank_d("mem", j), 0:hi - lo],
                            [(oT[:, k, P * i:P * i + P], oT[:, k, 1 + lo:1 + hi]) for k in range(KD)]).then_inc(dve_full, 1)
                pe.wait_ge(act_drained, job_a(b, "v", TT // 2) + RING)
                pe.wait_ge(dve_drained, job_d(b, "mem", len(MEM_S)) + RING)
                for j in range(2 * KD):
                    k, half = j // 2, j % 2
                    claim_a(job_a(b, "rT", j))
                    tiles = [i for i in range(TT) if (i, half) in MEM_S]
                    for i in tiles:
                        lo, hi = max(P * i, half * HALF), (half + 1) * HALF
                        at0 = sm_first[(i, half)]
                        mm = pe.matmul(psA[:, bank_a("rT", j), lo - half * HALF:HALF], v_sb[:, i, k * P:(k + 1) * P],
                                       sm_flat[:, at0:at0 + hi - lo], start=i == 0, stop=i == tiles[-1])
                    mm.then_inc(act_full, 1)
                pe.wait_ge(act_drained, job_a(b, "rT", 2 * KD) + RING)
                for j in range(TT // 2):
                    claim_d(job_d(b, "rp", j))
                    token_rows(bank_d("rp", j), psD, 2 * j, rT, read_w_sb, KD).then_inc(dve_full, 1)

                pe.wait_ge(ln_done, b * (2 * TT) + TT)
                turn(b, "xaT", xa)
                pe.wait_ge(act_drained, job_a(b, "xaT", 2 * KD) + RING)
                for j in range(2 * KD):
                    f, half = j // 2, j % 2
                    claim_a(job_a(b, "qT", j))
                    product(psA[:, bank_a("qT", j), :], [(wq_sb[:, k, f * P:(f + 1) * P],
                            xaT[:, k, half * HALF:(half + 1) * HALF]) for k in range(KD)]).then_inc(act_full, 1)
                pe.wait_ge(act_drained, job_a(b, "qT", 2 * KD) + RING)
                pe.wait_ge(blocks_ready, b * 3 + 3)

                def scores(t):
                    for n in range(2):
                        j = score_job(t, n)
                        claim_d(job_d(b, "score", j))
                        bank = psD[:, bank_d("score", j), :]
                        pe.matmul(bank, qT[:, n, t * P:(t + 1) * P], kblk[:, n, :, :].rearrange("p h m -> p (h m)"),
                                  start=True, stop=False)
                        pe.matmul(bank.rearrange("p (h m) -> p h m", h=8), ones[0:1, :], mask_row[0:1, bass.ds(b, 1), :].broadcast_to([1, 8, M]),
                                  start=False, stop=True).then_inc(dve_full, 1)

                def weigh(t):
                    for n in range(2):
                        pe.wait_ge(expo, b * (2 * TT) + (2 * t + n + 1))
                        claim_a(job_a(b, "probs", 3 * t + n))
                        for q in range(4):
                            mm = pe.transpose(psA[:, bank_a("probs", 3 * t + n), q * P:(q + 1) * P],
                                              prob[:, t % 2, n, q * P:(q + 1) * P], ident[:, :])
                        mm.then_inc(act_full, 1)
                    claim_d(job_d(b, "score", out_job(t)))
                    pe.wait_ge(act_drained, job_a(b, "probs", 3 * t + 2) + RING)
                    for q in range(HEADS // 2):
                        mm = pe.matmul(psD[:, bank_d("score", out_job(t)), q * 2 * VW:(q + 1) * 2 * VW],
                                       probT[:, t % 2, q // 4, (q % 4) * P:(q % 4 + 1) * P],
                                       vblk[:, q, :, :].rearrange("p h d -> p (h d)"), start=True, stop=True)
                    mm.then_inc(dve_full, 1)

                def turn_heads(t):
                    pe.wait_ge(dve_drained, job_d(b, "score", out_job(t)) + 1 + RING)
                    claim_a(job_a(b, "probs", 3 * t + 2))
                    for k in range(KD):
                        mm = pe.transpose(psA[:, bank_a("probs", 3 * t + 2), k * P:(k + 1) * P],
                                          att[:, t % 2, k * P:(k + 1) * P], ident[:, :])
                    mm.then_inc(act_full, 1)

                scores(0)
                for t in range(TT):
                    if t + 1 < TT:
                        scores(t + 1)
                    weigh(t)
                    turn_heads(t)
                pe.wait_ge(act_drained, job_a(b, "probs", 3 * TT) + RING)
                for j in range(TT // 2):
                    claim_d(job_d(b, "wo", j))
                    token_rows(bank_d("wo", j), psD, 2 * j, attT, wo_sb, KD).then_inc(dve_full, 1)

            pe.wait_ge(x2_loaded, 16)
            for j in range(KD * CH):
                k, c = j % KD, j // KD
                claim_a(END_A + j)
                for t in range(4):
                    mm = pe.transpose(psA[:, j % RING, t * P:(t + 1) * P], x2[:, 4 * c + t, k * P:(k + 1) * P], ident[:, :])
                mm.then_inc(act_full, 1)
            pe.wait_ge(act_drained, END_A + KD * CH + RING)
            for j in range(4):
                claim_d(END_D + j)
                for t in range(8):
                    mm = product(psD[:, (END_D + j) % RING, t * E:(t + 1) * E],
                                 [(x2T[:, k, (8 * j + t) * P:(8 * j + t + 1) * P], wg_sb[:, k, :]) for k in range(KD)])
                mm.then_inc(dve_full, 1)
            pe.wait_ge(route_step, ROUTE_ALL)
            for j in range(NT // 4):
                n = END_A + OFF_FA["combT"] + j
                claim_a(n)
                for t in range(4):
                    mm = pe.transpose(psA[0:E, n % RING, t * P:(t + 1) * P], comb[:, 4 * j + t, :], ident[:, :])
                mm.then_inc(act_full, 1)
            pe.wait_ge(act_drained, END_A + PRE_FA + RING)
            for j in range(NT // 2):
                n = END_D + OFF_FD["b2"] + j
                claim_d(n)
                for r in range(2):
                    mm = pe.matmul(psD[:, n % RING, r * D:(r + 1) * D], combT[:, (2 * j + r) * P:(2 * j + r + 1) * P],
                                   b2_sb[:, :], start=True, stop=True)
                mm.then_inc(dve_full, 1)
            with pe.Fori(0, E // 2) as pair:
                for r in range(2):
                    e = pair * 2 + r
                    pe.wait_ge(w1_loaded[r], pair * 16 + 16)
                    pe.wait_ge(w2_loaded[r], pair * 16 + 16)
                    alone(pe)
                    with pe.Fori(0, CH // 2) as c2:
                        for q in range(2):
                            chunk = e * CH + (c2 * 2 + q)
                            job = chunk * KH + (END_A + PRE_FA)
                            for k in range(KH):
                                claim_a(job + k)
                                mm = product(psA[:, k % RING, :],
                                             [(w1_sb[:, r, i, k * P:(k + 1) * P], x2T[:, i, bass.ds((c2 * 2 + q) * BANK, BANK)])
                                              for i in range(KD)])
                                mm.then_inc(act_full, 1)
                            pe.wait_ge(act_drained, job + (KH + RING))
                            for j in range(2):
                                n = chunk * 2 + (END_D + PRE_FD + j)
                                claim_d(n)
                                token_rows((END_D + PRE_FD + 2 * q + j) % RING, psD, 2 * j, hT, w2_sb[:, r], KH)\
                                    .then_inc(dve_full, 1)

        @block.vector
        def _(dve):
            dve.sem_inc(dve_drained, RING)
            dve.sem_inc(scanned, KI + 1)
            dve.sem_inc(summed, JT + 1)
            dve.memset(eps_sb[:, 0:1], EPS).then_inc(eps_ready, 1)
            dve.memset(eps_sb[:, 1:2], EPS * SHRINK ** 2).then_inc(eps_ready, 1)
            dve.wait_ge(consts_ready, 3)
            dve.tensor_scalar(strip[:, :], iota_i, 0.0, None, ALU.max).then_inc(dve_setup, 1)
            dve.tensor_copy(expert_id[:, :], expert_i[:, :]).then_inc(expert_ready, 1)
            dve.wait_ge(w_loaded, LOADED)
            dve.tensor_scalar(lng[:, 4:5], lng[:, 0:1], -1.0, 0.0, ALU.mult, ALU.max).then_inc(dve_setup, 1)
            dve.wait_ge(act_setup, 4)
            dve.tensor_scalar(negA[:, :, :], alog_sb[:, :, :], -1.0, None, ALU.mult).then_inc(dve_setup, 1)
            dve.wait_ge(dve_setup, 3)
            dve.tensor_scalar(lng[:, 5:6], lng[:, 4:5], lng[:, 3:4], -1.0, ALU.add, ALU.mult).then_inc(dve_setup, 1)
            dve.tensor_scalar(mask_row[:, :, :], mask_u8[:, :, :], -1.0, -MASKED, ALU.add, ALU.mult).then_inc(dve_setup, 1)
            dve.wait_ge(expert_ready, 1)
            dve.wait_ge(consts_ready, 8)
            for m in range(KD):
                dve.wait_ge(dve_full, m + 1)
                dve.tensor_copy(kT[:, m, :, :].rearrange("p b m -> p (b m)"), psD[:, m, 0:B * M]).then_inc(dve_drained, 1)
            for j in range(B // 2):
                dve.wait_ge(dve_full, KD + j + 1)
                dve.tensor_copy(vdup[:, 2 * j:2 * j + 2, :].rearrange("p b d -> p (b d)"), psD[:, KD + j, :])\
                   .then_inc(dve_drained, 1)

            def mamba(b, m):
                blk = b * 2 + m
                src = xin if m == 0 else x1
                rb = b * 4 + m
                dve.wait_ge(root, rb + 1)
                dve.reciprocal(rs[:, :], rt[:, :]).then_inc(inverse, 1)
                dve.wait_ge(inverse, b * 5 + (m + 1))
                for t in range(TT):
                    dve.tensor_scalar(xn[:, t, :], src[:, t, :], rs[:, t:t + 1], None, ALU.mult).then_inc(normed, 1)
                dve.memset(pre[:, :, 0:TAPS - 1], 0.0).then_inc(pads_zero, 1)
                for f in range(KI):
                    dve.wait_ge(act_drained, job_a(b, f"in{m}", 2 * f + 1) + 1 + RING)
                    dve.tensor_scalar(xm[:, f, :], pre[:, f, 0:T], conv_w_sb[:, f, 0:1], conv_b_sb[:, f:f + 1],
                                      ALU.mult, ALU.add).then_inc(conv_step, 1)
                    for tap in range(1, TAPS):
                        dve.wait_ge(conv_step, blk * (TAPS * KI) + (TAPS * f + tap))
                        dve.scalar_tensor_tensor(xm[:, f, :], pre[:, f, tap:tap + T], conv_w_sb[:, f, tap:tap + 1],
                                                 xm[:, f, :], op0=ALU.mult, op1=ALU.add).then_inc(conv_step, 1)
                for j in range(2 * KI):
                    f, half = j // 2, j % 2
                    dve.wait_ge(dve_full, job_d(b, f"z{m}", j) + 1)
                    dve.tensor_scalar(dt[:, f, half * HALF:(half + 1) * HALF], psD[:, bank_d(f"z{m}", j), :],
                                      dt_b_sb[:, f:f + 1], None, ALU.add).then_inc(dve_drained, 1)
                for f in range(KI):
                    done = blk * (4 * KI) + 4 * f
                    dve.wait_ge(soft_step, blk * (4 * KI) + (2 * KI + 2 * f + 2))
                    dve.tensor_tensor(series[:, f, :], series[:, f, :], soft_e[:, f, :], ALU.mult).then_inc(series_step, 1)
                    dve.tensor_scalar(is_small[:, f, :], soft_e[:, f, :], SMALL_E, None, ALU.is_lt).then_inc(series_step, 1)
                    dve.wait_ge(series_step, done + 1)
                    dve.scalar_tensor_tensor(series[:, f, :], series[:, f, :], 1.0, soft_e[:, f, :],
                                             op0=ALU.add, op1=ALU.mult).then_inc(series_step, 1)
                    dve.wait_ge(series_step, done + 3)
                    alone(dve)
                    dve.copy_predicated(soft_ln[:, f, :], is_small[:, f, :], series[:, f, :]).then_inc(series_step, 1)
                    dve.wait_ge(series_step, done + 4)
                    dve.scalar_tensor_tensor(dt[:, f, :], dt[:, f, :], 0.0, soft_ln[:, f, :],
                                             op0=ALU.max, op1=ALU.add).then_inc(dt_ready, 1)
                for f in range(KI):
                    dve.wait_ge(dt_ready, blk * KI + f + 1)
                    dve.tensor_tensor(dtu[:, f, :], dt[:, f, :], xm[:, f, :], ALU.mult).then_inc(dtu_ready, 1)

                def scans(s, half):
                    u = unit(b, m, s, half)
                    dve.wait_ge(hT_full, u * JT + 1)
                    if half == 1:
                        dve.wait_ge(scanned, u * KI + (KI + 1))
                    for f in range(KI):
                        dve.wait_ge(da_ready, u * KI + (f + 1))
                        dve.wait_ge(dbu_full, u * KI + (KI + f + 2))
                        start = 0.0 if half == 0 else h[:, 0, f, HALF - 1:HALF]
                        dve.tensor_tensor_scan(h[:, half, f, :], da[:, half, f, :], psD[:, f, :], start,
                                               ALU.mult, ALU.add).then_inc(scanned, 1)

                def sums(s, half):
                    u = unit(b, m, s, half)
                    dve.wait_ge(summed, u * JT + 1)
                    for j in range(JT):
                        t = half * JT + j
                        dve.wait_ge(hT_full, u * JT + (JT + j + 2))
                        dve.scalar_tensor_tensor(yT[:, t, :], psA[:, j, :],
                                                 bc[:, t, bass.ds(s + NS, 1)], yT[:, t, :],
                                                 op0=ALU.mult, op1=ALU.add).then_inc(summed, 1)

                dve.wait_ge(y_zero, blk + 1)
                dve.wait_ge(act_drained, job_a(b, f"uT{m}", TT) + RING)
                scans(0, 0)
                with dve.Fori(0, NS - 1) as s:
                    scans(s, 1)
                    sums(s, 0)
                    scans(s + 1, 0)
                    sums(s, 1)
                scans(NS - 1, 1)
                sums(NS - 1, 0)
                sums(NS - 1, 1)

                for j in range(2 * KI):
                    f, half = j // 2, j % 2
                    dve.wait_ge(dve_full, job_d(b, f"y{m}", j) + 1)
                    dve.scalar_tensor_tensor(y[:, f, half * HALF:(half + 1) * HALF], xm[:, f, half * HALF:(half + 1) * HALF],
                                             d_sb[:, f:f + 1], psD[:, bank_d(f"y{m}", j), :],
                                             op0=ALU.mult, op1=ALU.add).then_inc(dve_drained, 1)
                for f in range(KI):
                    dve.wait_ge(dve_drained, job_d(b, f"y{m}", 2 * f + 1) + 1 + RING)
                    dve.tensor_tensor(y[:, f, :], y[:, f, :], gate[:, f, :], ALU.mult).then_inc(gated, 1)
                if m == 0:
                    dve.wait_ge(xb_ready, b + 1)
                for j in range(TT // 2):
                    dve.wait_ge(dve_full, job_d(b, f"mo{m}", j) + 1)
                    ps = psD[:, bank_d(f"mo{m}", j), :].rearrange("p (t d) -> p t d", t=2)
                    if m == 0:
                        dve.tensor_tensor(x1[:, 2 * j:2 * j + 2, :], ps, base[:, 2 * j:2 * j + 2, :], ALU.add)\
                           .then_inc(dve_drained, 1)
                    else:
                        dve.tensor_tensor(o2[:, 2 * j:2 * j + 2, :], ps,
                                          out_b_sb[:, :].unsqueeze(1).broadcast_to([P, 2, D]), ALU.add)\
                           .then_inc(dve_drained, 1)

            def layer_norm(b, n, z, dst):
                for t in range(TT):
                    dve.bn_stats(stats[:, t, :], z[:, t, :]).then_inc(ln_stats, 1)
                dve.wait_ge(ln_stats, b * (4 * TT) + (2 * TT * n + TT))
                alone(dve)
                for t in range(TT):
                    dve.bn_aggr(aggr[:, t, :], stats[:, t, :]).then_inc(ln_stats, 1)
                dve.wait_ge(root, b * 4 + (3 + n))
                dve.reciprocal(rs[:, :], rt[:, :]).then_inc(inverse, 1)
                dve.wait_ge(inverse, b * 5 + (3 + 2 * n))
                if n == 0:
                    dve.scalar_tensor_tensor(rs[:, :], aggr[:, :, 1], VAR_LIMIT / D, rs[:, :],
                                             op0=ALU.is_le, op1=ALU.mult).then_inc(inverse, 1)
                    dve.wait_ge(inverse, b * 5 + 4)
                for t in range(TT):
                    dve.tensor_scalar(dst[:, t, :], z[:, t, :], aggr[:, t, 0:1], rs[:, t:t + 1],
                                      ALU.subtract, ALU.mult).then_inc(ln_done, 1)

            with dve.Fori(0, B) as b:
                for m in range(2):
                    mamba(b, m)
                dve.memset(oT[:, :, 0:1], 0.0).then_inc(blocks_ready, 1)
                for j, (i, half) in enumerate(MEM_S):
                    lo, hi = max(P * i, half * HALF), (half + 1) * HALF
                    at0 = sm_first[(i, half)]
                    dve.wait_ge(dve_full, job_d(b, "mem", j) + 1)
                    dve.tensor_tensor(sm_flat[:, at0:at0 + hi - lo], psD[:, bank_d("mem", j), 0:hi - lo],
                                      strip[:, lo - P * i:hi - P * i], ALU.mult).then_inc(dve_drained, 1)
                for k in range(KD):
                    last = dve.tensor_tensor(kblk[:, k, :, :], kT[:, k, bass.ds(b, 1), :].broadcast_to([P, 8, M]),
                                             headmask[:, :].unsqueeze(2).broadcast_to([P, 8, M]), ALU.mult)
                last.then_inc(blocks_ready, 1)
                for r in range(2):
                    dve.tensor_scalar(vblk[:, :, r, 0:HD], vdup[:, bass.ds(b, 1), :].rearrange(
                        "p o (q r d) -> p (o q) r d", r=2, d=HD)[:, :, r, :], pairmask[:, r:r + 1], None, ALU.mult)
                    last = dve.tensor_copy(vblk[:, :, r, HD:VW], pairmask[:, r:r + 1].unsqueeze(1)
                                           .broadcast_to([P, HEADS // 2, 1]))
                last.then_inc(blocks_ready, 1)
                dve.wait_ge(base_ready, b * 2 + 2)
                for j in range(TT // 2):
                    dve.wait_ge(dve_full, job_d(b, "rp", j) + 1)
                    dve.scalar_tensor_tensor(base[:, 2 * j:2 * j + 2, :].rearrange("p t d -> p (t d)"),
                                             psD[:, bank_d("rp", j), :], ALPHA * SHRINK,
                                             base[:, 2 * j:2 * j + 2, :].rearrange("p t d -> p (t d)"),
                                             op0=ALU.mult, op1=ALU.add).then_inc(dve_drained, 1)
                dve.wait_ge(dve_drained, job_d(b, "rp", TT // 2) + RING)
                layer_norm(b, 0, base, xa)

                def less_max(t):
                    for n in range(2):
                        j = score_job(t, n)
                        bank = psD[:, bank_d("score", j), :].rearrange("p (h m) -> p h m", h=8)
                        dve.wait_ge(dve_full, job_d(b, "score", j) + 1)
                        dve.tensor_reduce(mx[:, n, :], bank, AX.X, ALU.max).then_inc(score_max, 1)
                        dve.wait_ge(score_max, b * (2 * TT) + (2 * t + n + 1))
                        if t >= 2:
                            dve.wait_ge(act_full, job_a(b, "probs", 3 * (t - 2) + n) + 1)
                        dve.tensor_tensor(prob[:, t % 2, n, :].rearrange("p (h m) -> p h m", h=8), bank,
                                          mx[:, n, :].unsqueeze(2).broadcast_to([P, 8, M]), ALU.subtract)\
                           .then_inc(dve_drained, 1)

                def normalise(t):
                    bank = psD[:, bank_d("score", out_job(t)), 0:HEADS * VW].rearrange("p (h d) -> p h d", h=HEADS)
                    dve.wait_ge(dve_full, job_d(b, "score", out_job(t)) + 1)
                    dve.reciprocal(rsum[:, :], bank[:, :, HD]).then_inc(sum_inv, 1)
                    dve.wait_ge(sum_inv, b * TT + (t + 1))
                    if t >= 2:
                        dve.wait_ge(act_full, job_a(b, "probs", 3 * (t - 2) + 2) + 1)
                    dve.tensor_tensor(att[:, t % 2, :].rearrange("p (h d) -> p h d", h=HEADS), bank[:, :, 0:HD],
                                      rsum[:, :].unsqueeze(2).broadcast_to([P, HEADS, HD]), ALU.mult)\
                       .then_inc(dve_drained, 1)

                less_max(0)
                for t in range(TT):
                    if t + 1 < TT:
                        less_max(t + 1)
                    normalise(t)
                for j in range(TT // 2):
                    dve.wait_ge(dve_full, job_d(b, "wo", j) + 1)
                    dve.tensor_tensor(base[:, 2 * j:2 * j + 2, :].rearrange("p t d -> p (t d)"),
                                      psD[:, bank_d("wo", j), :],
                                      xa[:, 2 * j:2 * j + 2, :].rearrange("p t d -> p (t d)"), ALU.add)\
                       .then_inc(dve_drained, 1)
                dve.wait_ge(dve_drained, job_d(b, "wo", TT // 2) + RING)
                layer_norm(b, 1, base, x2_out)

            for j in range(4):
                dve.wait_ge(dve_full, END_D + j + 1)
                dve.tensor_tensor(logit[:, 8 * j:8 * j + 8, :], psD[:, (END_D + j) % RING, 0:8 * E]
                                  .rearrange("p (t e) -> p t e", e=E),
                                  bg_sb[:, :].unsqueeze(1).broadcast_to([P, 8, E]), ALU.add).then_inc(dve_drained, 1)
            dve.wait_ge(dve_drained, END_D + 4 + RING)
            for t in range(NT):
                dve.max(top[:, t, :], logit[:, t, :]).then_inc(route_step, 1)
            for t in range(NT):
                dve.wait_ge(route_step, NT)
                dve.max_index(topi[:, t, :], top[:, t, :], logit[:, t, :]).then_inc(route_step, 1)
            dve.wait_ge(route_step, ROUTE_TOP)
            dve.tensor_copy(topf[:, :, 0:2], topi[:, :, 0:2]).then_inc(route_step, 1)
            dve.tensor_tensor(rest[:, 0, :], top[:, :, 1], top[:, :, 0], ALU.subtract).then_inc(route_step, 1)
            dve.wait_ge(gap_exp, 1)
            dve.tensor_scalar(rest[:, 2, :], rest[:, 1, :], 1.0, None, ALU.add).then_inc(route_step, 1)
            dve.wait_ge(route_step, ROUTE_DIFF + 1)
            dve.reciprocal(rest[:, 3, :], rest[:, 2, :]).then_inc(route_step, 1)
            dve.wait_ge(route_step, ROUTE_DIFF + 2)
            dve.tensor_tensor(rest[:, 4, :], rest[:, 1, :], rest[:, 3, :], ALU.mult).then_inc(mix_ready, 1)
            for r in range(2):
                dst = comb if r == 0 else hot
                dve.tensor_tensor(dst[:, :, :], topf[:, :, r:r + 1].broadcast_to([P, NT, E]),
                                  expert_id[:, :].unsqueeze(1).broadcast_to([P, NT, E]), ALU.is_equal)\
                   .then_inc(mix_ready, 1)
            dve.wait_ge(mix_ready, 3)
            dve.tensor_tensor(comb[:, :, :], comb[:, :, :], rest[:, 3, :].unsqueeze(2).broadcast_to([P, NT, E]),
                              ALU.mult).then_inc(route_step, 1)
            dve.tensor_tensor(hot[:, :, :], hot[:, :, :], rest[:, 4, :].unsqueeze(2).broadcast_to([P, NT, E]),
                              ALU.mult).then_inc(route_step, 1)
            dve.wait_ge(route_step, ROUTE_DIFF + 4)
            dve.tensor_tensor(comb[:, :, :], comb[:, :, :], hot[:, :, :], ALU.add).then_inc(route_step, 1)
            for j in range(NT // 2):
                n = END_D + OFF_FD["b2"] + j
                dve.wait_ge(dve_full, n + 1)
                dve.tensor_tensor(acc[:, 2 * j:2 * j + 2, :].rearrange("p t d -> p (t d)"), psD[:, n % RING, :],
                                  x2[:, 2 * j:2 * j + 2, :].rearrange("p t d -> p (t d)"), ALU.add).then_inc(dve_drained, 1)
            dve.wait_ge(dve_drained, END_D + PRE_FD + RING)
            with dve.Fori(0, E) as e:
                with dve.Fori(0, CH // 2) as c2:
                    for q in range(2):
                        for j in range(2):
                            n = (e * CH + c2 * 2) * 2 + (END_D + PRE_FD + 2 * q + j)
                            dve.wait_ge(dve_full, n + 1)
                            dve.wait_ge(dve_drained, n + 1)
                            bank = psD[:, (END_D + PRE_FD + 2 * q + j) % RING, :]
                            for r in range(2):
                                t = c2 * 8 + (4 * q + 2 * j + r)
                                last = dve.scalar_tensor_tensor(
                                    acc[:, bass.ds(t, 1), :].rearrange("p o d -> p (o d)"), bank[:, r * D:(r + 1) * D],
                                    comb[:, bass.ds(t, 1), bass.ds(e, 1)].rearrange("p o q -> p (o q)"),
                                    acc[:, bass.ds(t, 1), :].rearrange("p o d -> p (o d)"),
                                    op0=ALU.mult, op1=ALU.add)
                            last.then_inc(dve_drained, 1)

            dve.wait_ge(dve_drained, END_D + PRE_FD + E * CH * 2 + RING)
            n = 0

            def fin(ins):
                nonlocal n
                n += 1
                ins.then_inc(fin_step, 1)

            def norm(q, r):
                for t in range(TT):
                    fin(dve.bn_stats(fstats[:, q % 2, t, :], acc[:, q * TT + t, :]))
                dve.wait_ge(fin_step, n)
                for t in range(TT):
                    fin(dve.bn_aggr(faggr[:, q % 2, t, :], fstats[:, q % 2, t, :]))
                dve.wait_ge(fin_root, 2 * q + r + 1)
                fin(dve.reciprocal(frt[:, q % 2, r, :], frt[:, q % 2, r, :]))
                dve.wait_ge(fin_step, n)
                for t in range(TT):
                    fin(dve.tensor_scalar(acc[:, q * TT + t, :], acc[:, q * TT + t, :], faggr[:, q % 2, t, 0:1],
                                          frt[:, q % 2, r, t:t + 1], ALU.subtract, ALU.mult))
                dve.wait_ge(fin_step, n)

            for q in range(B):
                rows = acc[:, q * TT:(q + 1) * TT, :]
                norm(q, 0)
                fin(dve.tensor_tensor(rows, rows, gamma_sb[:, :].unsqueeze(1).broadcast_to([P, TT, D]), ALU.mult))
                dve.wait_ge(fin_step, n)
                fin(dve.tensor_tensor(rows, rows, beta_sb[:, :].unsqueeze(1).broadcast_to([P, TT, D]), ALU.add))
                dve.wait_ge(fin_step, n)
                fin(dve.tensor_tensor(rows, rows, x2[:, q * TT:(q + 1) * TT, :], ALU.add))
                dve.wait_ge(fin_step, n)
                norm(q, 1)
                assert n == FIN_PER * (q + 1)


def _layouts(np, a):
    def vec(v):
        return v.reshape(-1, 128).T

    def rows(v):
        return v.reshape(v.shape[0] // 128, 128, -1).transpose(1, 0, 2)

    return {
        "x": a["x"], "ctxT": a["ctx_768"].transpose(0, 2, 1), "ctx_mask": a["mask_BxS2_bf1"].view(np.uint8),
        "norm1_w": vec(a["L0_attn_norm1_w"]), "norm2_w": vec(a["L0_attn_norm2_w"]),
        "in_wT": a["L0_attn_in_proj_w"].T, "in_b": vec(a["L0_attn_in_proj_b"]),
        "conv_w": rows(a["L0_attn_conv_w"][:, 0, :]), "conv_b": vec(a["L0_attn_conv_b"]),
        "xp_wT": a["L0_attn_x_proj_w"].T, "dt_wT": a["L0_attn_dt_proj_w"].T, "dt_b": vec(a["L0_attn_dt_proj_b"]),
        "A_log": rows(a["L0_attn_A_log"]), "D_ssm": vec(a["L0_attn_D_ssm"]),
        "out_wT": a["L0_attn_out_proj_w"].T, "out_b": a["L0_attn_out_proj_b"],
        "write_wT": a["L0_attn_proj_write_w"].T, "read_wT": a["L0_attn_proj_read_w"].T,
        "decay": a["L0_attn_decay"].reshape(1),
        "Wq": a["L0_xattn_Wq"], "Wk": a["L0_xattn_Wk"], "Wv": a["L0_xattn_Wv"], "Wo": a["L0_xattn_Wo"],
        "Wg": a["L0_ffn_Wg"], "bg": a["L0_ffn_bg"], "W1": a["L0_ffn_W1"],
        "b1": a["L0_ffn_b1"].reshape(8, 8, 128).transpose(2, 0, 1),
        "W2": a["L0_ffn_W2"], "b2": a["L0_ffn_b2"], "gamma": a["L0_ffn_gamma"], "beta": a["L0_ffn_beta"],
    }


def kernel(**inputs):
    import numpy as _np
    import concourse.bacc as _bacc
    from concourse import mybir as _mybir
    from concourse.bass_utils import run_bass_kernel_spmd as _run

    nc = _bacc.Bacc("TRN2", target_bir_lowering=False, num_devices=1)
    arrays, args = {}, []
    for name, a in _layouts(_np, {k: _np.asarray(v) for k, v in inputs.items()}).items():
        a = _np.ascontiguousarray(a)
        arrays[f"in_{name}"] = a
        args.append(nc.dram_tensor(f"in_{name}", a.shape, _mybir.dt.from_np(a.dtype), kind="ExternalInput").ap())
    shape = tuple(inputs["x"].shape)
    args.append(nc.dram_tensor("out_0", shape, _mybir.dt.float32, kind="ExternalOutput").ap())
    decoder_layer(nc, *args)
    r = _run(nc, [arrays], core_ids=[0])
    return r.results[0]["out_0"]
```

```python
from contextlib import ExitStack

import numpy as np

import concourse.bass as bass
from concourse import mybir

ALU = mybir.AluOpType
ACT = mybir.ActivationFunctionType
AX = mybir.AxisListType
F32 = mybir.dt.float32
BF16 = mybir.dt.bfloat16
I32 = mybir.dt.int32
U32 = mybir.dt.uint32
U8 = mybir.dt.uint8

P = 128
EPS = 1e-5
ALPHA = 0.1
MASKED = -1.0e30
SMALL_E = 2.0 ** -7
SHRINK = 2.0 ** -40
VAR_LIMIT = float(np.finfo(np.float32).max) * SHRINK ** 2
RING = 4
BANK = 512


def offsets(stages):
    at, first = 0, {}
    for name, count in stages:
        first[name] = at
        at += count
    return first, at


def decoder_layer(nc, x, ctxT, ctx_mask, norm1_w, norm2_w, in_wT, in_b, conv_w, conv_b, xp_wT, dt_wT, dt_b,
                  A_log, D_ssm, out_wT, out_b, write_wT, read_wT, decay, Wq, Wk, Wv, Wo,
                  Wg, bg, W1, b1, W2, b2, gamma, beta, out):
    B, T, D = x.shape
    DI = out_wT.shape[0]
    NS = A_log.shape[2]
    R = dt_wT.shape[0]
    TAPS = conv_w.shape[2]
    CD, M = ctxT.shape[1], ctxT.shape[2]
    HEADS = 16
    HD = D // HEADS
    E = Wg.shape[1]
    HID = W1.shape[2]
    TT = T // P
    KD = D // P
    KI = DI // P
    HALF = T // 2
    JT = HALF // P
    KH = HID // P
    CH = B * T // BANK
    NT = B * T // P
    CP = CD // 2
    VW = HD + 1
    assert HALF == BANK and M * 8 == BANK and KI * P == BANK

    EARLY = 4
    MAMBA_A = [("xnT", 2 * KD), ("in", 2 * KI + EARLY), ("rank", 2), ("bc", 2), ("late", 2 * KI - EARLY), ("uT", TT)]
    MAMBA_D = [("z", 2 * KI), ("y", 2 * KI), ("mo", TT // 2)]
    SEQ_A = [(f"{n}{m}", c) for m in range(2) for n, c in MAMBA_A] + [
        ("oT", 2 * KD), ("v", TT // 2), ("rT", 2 * KD),
        ("xaT", 2 * KD), ("qT", 2 * KD), ("probs", 3 * TT)]
    MEM_S = [(i, h) for i in range(TT) for h in range(2) if (h + 1) * JT > i]
    SEQ_D = [(f"{n}{m}", c) for m in range(2) for n, c in MAMBA_D] + [
        ("mem", len(MEM_S)), ("rp", TT // 2), ("score", 3 * TT), ("wo", TT // 2)]
    OFF_A, PER_A = offsets(SEQ_A)
    OFF_D, PER_D = offsets(SEQ_D)
    SETUP_D = 4
    assert PER_A % RING == 0 and PER_D % RING == 0 and all(v % RING == 0 for v in
           (OFF_A["uT1"], OFF_A["oT"], OFF_D["mem"]))

    def job_a(b, stage, j):
        return b * PER_A + (OFF_A[stage] + j)

    def job_d(b, stage, j):
        return b * PER_D + (SETUP_D + OFF_D[stage] + j)

    def bank_a(stage, j):
        return (OFF_A[stage] + j) % RING

    def bank_d(stage, j):
        return (OFF_D[stage] + j) % RING

    END_A, END_D = B * PER_A, SETUP_D + B * PER_D
    TILES = 2 * B * T // P + E
    STEPS = B * T // P

    with ExitStack() as ctx:
        def sb(name, shape, dt=F32):
            return ctx.enter_context(nc.sbuf_tensor(name, shape, dt))

        def sem(name):
            return ctx.enter_context(nc.semaphore(name))

        psA = ctx.enter_context(nc.psum_tensor("psA", [P, RING, BANK], F32))
        psD = ctx.enter_context(nc.psum_tensor("psD", [P, RING, BANK], F32))

        x2_dram = nc.dram_tensor("x2_dram", (NT, P, D), F32, kind="Internal").ap()
        xs_dram = nc.dram_tensor("xs_dram", ((TILES + 1) * P, D), F32, kind="Internal").ap()
        ys_dram = nc.dram_tensor("ys_dram", (TILES * P, D), F32, kind="Internal").ap()

        ident = sb("ident", [P, P])
        ones = sb("ones", [P, P])
        in_w_sb = sb("in_w_sb", [P, KD, 2 * DI])
        out_w_sb = sb("out_w_sb", [P, KI, D])
        xp_w_sb = sb("xp_w_sb", [P, KI, R + 2 * NS])
        dt_w_sb = sb("dt_w_sb", [R, DI])
        write_w_sb = sb("write_w_sb", [P, KD, D])
        read_w_sb = sb("read_w_sb", [P, KD, D])
        wq_sb = sb("wq_sb", [P, KD, D])
        wo_sb = sb("wo_sb", [P, KD, D])
        norm_sb = sb("norm_sb", [P, 2, KD])
        in_b_sb = sb("in_b_sb", [P, 2 * KI])
        conv_w_sb = sb("conv_w_sb", [P, KI, TAPS])
        conv_b_sb = sb("conv_b_sb", [P, KI])
        dt_b_sb = sb("dt_b_sb", [P, KI])
        d_sb = sb("d_sb", [P, KI])
        alog_sb = sb("alog_sb", [P, KI, NS])
        negA = sb("negA", [P, KI, NS])
        out_b_sb = sb("out_b_sb", [P, D])
        lng = sb("lng", [P, 8])
        strip = sb("strip", [P, T])
        kT = sb("kT", [P, KD, B, M])
        vdup = sb("vdup", [P, B, D])
        eps_sb = sb("eps_sb", [P, 2])
        headmask = sb("headmask", [P, 8])
        pairmask = sb("pairmask", [P, 2])
        mask_u8 = sb("mask_u8", [1, B, M], U8)
        mask_row = sb("mask_row", [1, B, M], BF16)
        mask_ones = sb("mask_ones", [1, P], BF16)
        ss = sb("ss", [P, TT])
        rt = sb("rt", [P, TT])
        rs = sb("rs", [P, TT])
        stats = sb("stats", [P, TT, 6])
        aggr = sb("aggr", [P, TT, 2])
        bc = sb("bc", [P, TT, 2 * NS])
        bcol = sb("bcol", [P, 2, JT])
        mx = sb("mx", [P, 2, 8])
        rsum = sb("rsum", [P, 2, HEADS])

        WORDS = 41100
        arena = sb("arena", [P, WORDS])
        at = [0]

        def carve(n):
            at[0] += n
            assert at[0] <= WORDS, at
            return arena[:, at[0] - n:at[0]]

        xin = carve(TT * D).rearrange("p (t d) -> p t d", d=D)
        x1 = carve(TT * D).rearrange("p (t d) -> p t d", d=D)
        base = carve(TT * D).rearrange("p (t d) -> p t d", d=D)
        g_flat = carve(2 * JT * DI)
        g = g_flat.rearrange("p (u j d) -> p u j d", u=2, j=JT)
        xn = g_flat[:, 0:TT * D].rearrange("p (t d) -> p t d", d=D)
        rank_sb = g_flat[0:R, 0:T]
        xnT_flat = carve(KD * (T + 1))
        xnT = xnT_flat.rearrange("p (k t) -> p k t", k=KD)
        pre_flat = carve(KI * (T + TAPS - 1))
        pre = pre_flat.rearrange("p (k t) -> p k t", k=KI)
        uT = pre_flat[:, 0:TT * DI].rearrange("p (t d) -> p t d", d=DI)
        sm_flat = carve(2 * KI * T)
        xm = sm_flat[:, 0:KI * T].rearrange("p (k t) -> p k t", k=KI)
        gate = sm_flat[:, KI * T:2 * KI * T].rearrange("p (k t) -> p k t", k=KI)
        dt = carve(KI * T).rearrange("p (k t) -> p k t", k=KI)
        yT_flat = carve(TT * DI)
        yT = yT_flat.rearrange("p (t d) -> p t d", d=DI)
        h_flat = carve(2 * KI * HALF)
        h = h_flat.rearrange("p (u k t) -> p u k t", u=2, k=KI)
        dtu = h_flat.rearrange("p (k t) -> p k t", k=KI)
        da_flat = carve(2 * KI * HALF)
        da = da_flat.rearrange("p (u k t) -> p u k t", u=2, k=KI)
        soft_e = da_flat.rearrange("p (k t) -> p k t", k=KI)
        soft_ln = yT_flat.rearrange("p (k t) -> p k t", k=KI)
        series = dtu
        is_small = pre_flat[:, 0:KI * T // 4].bitcast(U8).rearrange("p (k t) -> p k t", k=KI)
        y = da_flat.rearrange("p (k t) -> p k t", k=KI)
        o2 = x2_out = g_flat[:, 0:TT * D].rearrange("p (t d) -> p t d", d=D)
        oT = xnT
        v_sb = g_flat[:, TT * D:2 * TT * D].rearrange("p (t d) -> p t d", d=D)
        sm_first, sm_words = offsets([((i, hh), (hh + 1) * BANK - max(P * i, hh * BANK)) for i, hh in MEM_S])
        assert sm_words <= 2 * KI * T
        rT = yT_flat[:, 0:KD * T].rearrange("p (k t) -> p k t", k=KD)
        xa = x1
        xaT = yT_flat[:, KD * T:2 * KD * T].rearrange("p (k t) -> p k t", k=KD)
        qT = h_flat[:, 0:KD * T].rearrange("p (k t) -> p k t", k=KD)
        attT = h_flat[:, KD * T:2 * KD * T].rearrange("p (k t) -> p k t", k=KD)
        prob = da_flat.rearrange("p (u n c) -> p u n c", u=4, n=2)
        probT = dt.rearrange("p k t -> p (k t)").rearrange("p (u n c) -> p u n c", u=4, n=2)
        att = pre_flat[:, 0:2 * D].rearrange("p (u d) -> p u d", u=2)
        kblk = pre_flat[:, 1024:1024 + KD * 8 * M].rearrange("p (k h m) -> p k h m", k=KD, h=8)
        vblk = pre_flat[:, 2048:2048 + HEADS * VW].rearrange("p (q r d) -> p q r d", r=2, d=VW)
        at[0] = 0
        x2 = carve(NT * D).rearrange("p (t d) -> p t d", d=D)
        ys = carve(TILES * D).rearrange("p (t d) -> p t d", d=D)
        ys_flat = ys.rearrange("p t d -> p (t d)")
        tile_in = carve(D)
        x2T = ys_flat[:, 0:NT * D].rearrange("p (k t) -> p k t", k=KD)
        picked = ys_flat[:, 0:2 * NT * D].rearrange("p (r t d) -> p r t d", r=2, d=D)
        w1_sb = carve(2 * KD * HID).rearrange("p (u k f) -> p u k f", u=2, k=KD)
        w2_sb = carve(2 * KH * D).rearrange("p (u k f) -> p u k f", u=2, k=KH)
        b1_sb = carve(2 * HID).rearrange("p (u f) -> p u f", u=2)
        b2_sb = carve(2 * D).rearrange("p (u f) -> p u f", u=2)
        hid = carve(HID)
        act_hid = carve(HID)
        hidT = carve(HID).rearrange("p (k t) -> p k t", k=KH)
        tileT = carve(KD * P).rearrange("p (k t) -> p k t", k=KD)
        small = in_w_sb[:, :, :].rearrange("p k f -> p (k f)")
        small2 = out_w_sb[:, :, :].rearrange("p k f -> p (k f)")

        def by_expert(words, n):
            return words[:, n * NT * E:(n + 1) * NT * E].rearrange("p (t e) -> p t e", e=E)

        logit, top, topf, sel1, sel2, sel, cum = (by_expert(small, n) for n in range(7))
        topi = by_expert(small, 7).bitcast(U32)
        place, total, weighed = (by_expert(small2, n) for n in range(3))
        rest = small2[:, 3 * NT * E:4 * NT * E].rearrange("p (k t) -> p k t", k=8)
        over = write_w_sb[:, 0, :].rearrange("p (e j) -> p e j", e=E)
        steps = write_w_sb[:, 1, :].rearrange("p (e j) -> p e j", e=E)
        steps_i = read_w_sb[:, 1, :].bitcast(I32).rearrange("p (e j) -> p e j", e=E)
        count = read_w_sb[:, 0, 0:E]
        ends = read_w_sb[:, 0, E:2 * E]
        firsts = read_w_sb[:, 0, 2 * E:3 * E]
        bound = sb("bound", [P, E + 1], I32)
        slot = sb("slot", [P, 2, NT], U32)
        below = sb("below", [P, P])
        wg_sb = sb("wg_sb", [P, KD, E])
        bg_sb = sb("bg_sb", [P, E])
        expert_id = sb("expert_id", [P, E])
        expert_i = sb("expert_i", [P, E], I32)
        gamma_sb = sb("gamma_sb", [P, D])
        beta_sb = sb("beta_sb", [P, D])
        fstats = sb("fstats", [P, 2, TT, 6])
        faggr = sb("faggr", [P, 2, TT, 2])
        frt = sb("frt", [P, 2, 2, TT])
        zeros = sb("zeros", [P, 4 * D])
        acc = picked[:, 0]
        iota_i = base[:, 0:T // D, :].rearrange("p t d -> p (t d)").bitcast(I32)
        ctx_sb = gate[0:CP, 0, 0:2 * B * 2 * M].rearrange("p (c b m) -> p c b m", c=2, b=B)
        wk_sb = gate[0:CP, 1, 0:2 * D].rearrange("p (c d) -> p c d", c=2)
        wv_sb = gate[0:CP, 2, 0:2 * D].rearrange("p (c d) -> p c d", c=2)

        w_loaded = sem("w_loaded")
        x_loaded = sem("x_loaded")
        act_full, act_drained = sem("act_full"), sem("act_drained")
        dve_full, dve_drained = sem("dve_full"), sem("dve_drained")
        consts_step = sem("consts_step")
        consts_ready = sem("consts_ready")
        dve_setup = sem("dve_setup")
        act_setup = sem("act_setup")
        squares = sem("squares")
        root = sem("root")
        inverse = sem("inverse")
        normed = sem("normed")
        pads_zero = sem("pads_zero")
        tap0_ready = sem("tap0_ready")
        conv_step = sem("conv_step")
        xm_ready = sem("xm_ready")
        soft_abs = sem("soft_abs")
        soft_exp = sem("soft_exp")
        soft_log = sem("soft_log")
        small_found = sem("small_found")
        cubic_step = sem("cubic_step")
        series_step = sem("series_step")
        gate_ready = sem("gate_ready")
        dt_ready = sem("dt_ready")
        dtu_ready = sem("dtu_ready")
        y_zero = sem("y_zero")
        bcol_ready = sem("bcol_ready")
        g_ready = sem("g_ready")
        da_ready = sem("da_ready")
        dbu_full = sem("dbu_full")
        scanned = sem("scanned")
        hT_full = sem("hT_full")
        summed = sem("summed")
        gated = sem("gated")
        xb_ready = sem("xb_ready")
        sum01 = sem("sum01")
        base_ready = sem("base_ready")
        ln_stats = sem("ln_stats")
        ln_done = sem("ln_done")
        blocks_ready = sem("blocks_ready")
        score_max = sem("score_max")
        expo = sem("expo")
        sum_inv = sem("sum_inv")
        route_step = sem("route_step")
        gap_exp = sem("gap_exp")
        routed = sem("routed")
        steps_ready = sem("steps_ready")
        xs_zeroed = sem("xs_zeroed")
        xs_sorted = sem("xs_sorted")
        xs_loaded = sem("xs_loaded")
        w_ready = [sem("w_ready0"), sem("w_ready1")]
        tileT_full = sem("tileT_full")
        tileT_ready = sem("tileT_ready")
        hid_full = sem("hid_full")
        hid_ready = sem("hid_ready")
        gelu_ready = sem("gelu_ready")
        turn_full = sem("turn_full")
        hidT_ready = sem("hidT_ready")
        y_full = sem("y_full")
        y_ready = sem("y_ready")
        y_stored = sem("y_stored")
        picked_in = [sem(f"picked_in{q}") for q in range(B)]
        x2_stored = sem("x2_stored")
        x2_loaded = sem("x2_loaded")
        eps_ready = sem("eps_ready")
        expert_ready = sem("expert_ready")
        fin_step = sem("fin_step")
        fin_root = sem("fin_root")
        fin_pool = sem("fin_pool")
        stored = sem("stored")
        waits_passed = sem("waits_passed")

        CONSTS = 10
        UNITS = 2 * NS

        def alone(engine):
            engine.sem_inc(waits_passed, 1)

        def unit(b, m, s, half):
            return b * (2 * UNITS) + s * 2 + (m * UNITS + half)

        order_d = [("score", 0, 0), ("score", 0, 1), ("score", 1, 0), ("score", 1, 1)]
        order_a = []
        for t in range(TT + 2):
            order_d += [("score", t + 2, n) for n in range(2) if t + 2 < TT]
            order_d += [("out", t - 1, 0)] if 1 <= t <= TT else []
            order_a += [("probs", t, n) for n in range(2) if t < TT]
            order_a += [("heads", t - 2, 0)] if t >= 2 else []
        assert len(order_d) == len(order_a) == 3 * TT

        def score_job(t, n):
            return order_d.index(("score", t, n))

        def out_job(t):
            return order_d.index(("out", t, 0))

        def probs_job(t, n):
            return order_a.index(("probs", t, n))

        def heads_job(t):
            return order_a.index(("heads", t, 0))

        GAP_STEP = NT + 1
        SEL_STEP = GAP_STEP + NT + 4
        FIN_NORM = 3 * TT + 1
        FIN_PER = TT + TT + 2 * FIN_NORM + 3

        block = ctx.enter_context(nc.Block())

        loads = [
            (in_w_sb[:, :, :], in_wT.rearrange("(k p) f -> p k f", p=P)),
            (out_w_sb[:, :, :], out_wT.rearrange("(k p) f -> p k f", p=P)),
            (xp_w_sb[:, :, :], xp_wT.rearrange("(k p) f -> p k f", p=P)),
            (dt_w_sb[:, :], dt_wT),
            (write_w_sb[:, :, :], write_wT.rearrange("(k p) f -> p k f", p=P)),
            (read_w_sb[:, :, :], read_wT.rearrange("(k p) f -> p k f", p=P)),
            (wq_sb[:, :, :], Wq.rearrange("(k p) f -> p k f", p=P)),
            (wo_sb[:, :, :], Wo.rearrange("(k p) f -> p k f", p=P)),
            (norm_sb[:, 0, :], norm1_w),
            (norm_sb[:, 1, :], norm2_w),
            (in_b_sb[:, :], in_b),
            (conv_w_sb[:, :, :], conv_w),
            (conv_b_sb[:, :], conv_b),
            (dt_b_sb[:, :], dt_b),
            (d_sb[:, :], D_ssm),
            (alog_sb[:, :, :], A_log),
            (out_b_sb[:, :], out_b.rearrange("(a n) -> a n", a=1).broadcast_to([P, D])),
            (lng[:, 0:1], decay.rearrange("(a n) -> a n", a=1).broadcast_to([P, 1])),
            (mask_u8[:, :, :], ctx_mask.rearrange("(a b) m -> a b m", a=1)),
            (wk_sb[:, :, :], Wk.rearrange("(c p) f -> p c f", p=CP)),
            (wv_sb[:, :, :], Wv.rearrange("(c p) f -> p c f", p=CP)),
            (wg_sb[:, :, :], Wg.rearrange("(k p) f -> p k f", p=P)),
            (bg_sb[:, :], bg.rearrange("(a n) -> a n", a=1).broadcast_to([P, E])),
            (gamma_sb[:, :], gamma.rearrange("(a n) -> a n", a=1).broadcast_to([P, D])),
            (beta_sb[:, :], beta.rearrange("(a n) -> a n", a=1).broadcast_to([P, D])),
        ] + [(ctx_sb[:, :, b, r * M:(r + 1) * M], ctxT[b].rearrange("(c p) m -> p c m", p=CP))
             for b in range(B) for r in range(2)]
        LOADED = 16 * len(loads)

        def load_expert(engine, e, r):
            one = bass.ds(e, 1)
            engine.dma_start(w1_sb[:, r, :, :], W1[one].rearrange("a (k p) f -> p (a k) f", p=P)).then_inc(w_ready[r], 16)
            engine.dma_start(w2_sb[:, r, :, :], W2[one].rearrange("a (k p) f -> p (a k) f", p=P)).then_inc(w_ready[r], 16)
            engine.dma_start(b1_sb[:, r, :], b1[one, :].broadcast_to([P, HID])).then_inc(w_ready[r], 16)
            engine.dma_start(b2_sb[:, r, :], b2[one, :].broadcast_to([P, D])).then_inc(w_ready[r], 16)

        def expert_tiles(engine, e):
            return (engine.value_load(bound[0:1, bass.ds(e, 1)], min_val=0, max_val=TILES - 1),
                    engine.value_load(bound[0:1, bass.ds(e + 1, 1)], min_val=1, max_val=TILES))

        @block.sync
        def _(sp):
            sp.sem_inc(x2_stored, 16)
            sp.dma_start(xin, x[0].rearrange("(t p) d -> p t d", p=P)).then_inc(x_loaded, 16)
            for dst, src in loads:
                sp.dma_start(dst, src).then_inc(w_loaded, 16)
            def keep_x2(b):
                sp.wait_ge(ln_done, b * (2 * TT) + 2 * TT)
                sp.dma_start(x2_dram[bass.ds(b * TT, TT)].rearrange("t p d -> p t d"), x2_out).then_inc(x2_stored, 16)

            sp.wait_ge(consts_ready, 1)
            rows = xs_dram.rearrange("(p r) d -> p (r d)", p=P)
            for c in range(-(-(TILES + 1) // 4)):
                lo, hi = c * 4 * D, min((c + 1) * 4 * D, (TILES + 1) * D)
                sp.dma_start(rows[:, lo:hi], zeros[:, 0:hi - lo]).then_inc(xs_zeroed, 16)
            rows = ys_dram[(TILES - E) * P:TILES * P, :].rearrange("(p r) d -> p (r d)", p=P)
            for c in range(E // 4):
                sp.dma_start(rows[:, c * 4 * D:(c + 1) * 4 * D], zeros[:, :]).then_inc(xs_zeroed, 16)
            with sp.Fori(0, B - 1) as b:
                sp.wait_ge(sum01, b + 1)
                sp.dma_start(xin, x[bass.ds(b + 1, 1)].rearrange("a (t p) d -> p (a t) d", p=P))\
                  .then_inc(x_loaded, 16)
                keep_x2(b)
            keep_x2(B - 1)
            sp.wait_ge(x2_stored, 16 * B + 16)
            sp.dma_start(x2, x2_dram.rearrange("t p d -> p t d")).then_inc(x2_loaded, 16)
            sp.wait_ge(xs_sorted, 16 * 2 * NT)
            sp.wait_ge(routed, 1)
            sp.dma_start(tile_in, xs_dram[0:P, :]).then_inc(xs_loaded, 16)
            tiles = sp.value_load(bound[0:1, E:E + 1], min_val=E, max_val=TILES)
            with sp.Fori(0, tiles) as i:
                sp.wait_ge(tileT_full, i + 2)
                sp.wait_ge(xs_loaded, i * 16 + 16)
                alone(sp)
                sp.dma_start(tile_in, xs_dram[bass.ds(i * P + P, P), :]).then_inc(xs_loaded, 16)
            out_v = out.rearrange("b (t p) d -> p (b t) d", p=P)
            for q in range(B):
                sp.wait_ge(fin_step, FIN_PER * (q + 1))
                sp.dma_start(out_v[:, q * TT:(q + 1) * TT, :], acc[:, q * TT:(q + 1) * TT, :]).then_inc(stored, 16)
            sp.wait_ge(stored, 16 * B)

        @block.gpsimd
        def _(pool):
            pool.memset(zeros[:, :], 0.0).then_inc(consts_ready, 1)
            pool.memset(ident[:, :], 0.0).then_inc(consts_step, 1)
            pool.memset(ones[:, :], 1.0).then_inc(consts_ready, 1)
            pool.memset(headmask[:, :], 1.0 / float(HD) ** 0.5).then_inc(consts_step, 1)
            pool.memset(pairmask[:, :], 1.0).then_inc(consts_step, 1)
            pool.memset(below[:, :], 1.0).then_inc(consts_step, 1)
            pool.iota(iota_i, pattern=[[1, T]], base=-1, channel_multiplier=-1).then_inc(consts_ready, 1)
            pool.iota(expert_i[:, :], pattern=[[1, E]], base=0, channel_multiplier=0).then_inc(consts_ready, 1)
            pool.wait_ge(consts_step, 4)
            pool.affine_select(out=below[:, :], in_=below[:, :], compare_op=ALU.is_ge, fill=0.0, base=-1,
                               pattern=[[1, P]], channel_multiplier=-1).then_inc(consts_ready, 1)
            pool.affine_select(out=ident[:, :], in_=ident[:, :], compare_op=ALU.not_equal, fill=1.0, base=0,
                               pattern=[[-1, P]], channel_multiplier=1).then_inc(consts_ready, 1)
            pool.affine_select(out=headmask[:, :], in_=headmask[:, :], compare_op=ALU.is_ge, fill=0.0, base=0,
                               pattern=[[-HD, 8]], channel_multiplier=1).then_inc(consts_step, 1)
            pool.wait_ge(consts_step, 5)
            pool.affine_select(out=headmask[:, :], in_=headmask[:, :], compare_op=ALU.is_ge, fill=0.0, base=HD - 1,
                               pattern=[[HD, 8]], channel_multiplier=-1).then_inc(consts_ready, 1)
            pool.affine_select(out=pairmask[:, 0:1], in_=pairmask[:, 0:1], compare_op=ALU.is_ge, fill=0.0,
                               base=M - 1, pattern=[[0, 1]], channel_multiplier=-1).then_inc(consts_ready, 1)
            pool.affine_select(out=pairmask[:, 1:2], in_=pairmask[:, 1:2], compare_op=ALU.is_ge, fill=0.0,
                               base=-M, pattern=[[0, 1]], channel_multiplier=1).then_inc(consts_ready, 1)
            pool.wait_ge(act_setup, 5)
            pool.affine_select(out=strip[:, :], in_=strip[:, :], compare_op=ALU.is_ge, fill=0.0, base=-1,
                               pattern=[[1, T]], channel_multiplier=-1).then_inc(consts_ready, 1)
            pool.sem_inc(g_ready, JT + 1)
            with pool.Fori(0, B) as b:
                for m in range(2):
                    if m == 0:
                        pool.wait_ge(x2_stored, b * 16 + 16)
                        pool.wait_ge(x_loaded, b * 16 + 16)
                        pool.wait_ge(w_loaded, LOADED)
                        pool.tensor_tensor(base[:, :, :], xin[:, :, :],
                                           out_b_sb[:, :].unsqueeze(1).broadcast_to([P, TT, D]), ALU.add)\
                            .then_inc(xb_ready, 1)
                        pool.wait_ge(xb_ready, b + 1)
                    else:
                        pool.wait_ge(dve_drained, job_d(b, "mo0", TT // 2) + RING)
                        pool.tensor_tensor(base[:, :, :], xin[:, :, :], x1[:, :, :], ALU.add).then_inc(sum01, 1)
                    blk = b * 2 + m
                    for f in range(KI):
                        pool.wait_ge(soft_exp, blk * KI + f + 1)
                        alone(pool)
                        pool.tensor_scalar(series[:, f, :], soft_e[:, f, :], 1.0 / 3.0, -0.5, ALU.mult, ALU.add)\
                            .then_inc(cubic_step, 1)
                        pool.tensor_scalar(is_small[:, f, :], soft_e[:, f, :], SMALL_E, None, ALU.is_lt)\
                            .then_inc(small_found, 1)
                        pool.wait_ge(cubic_step, blk * (2 * KI) + (2 * f + 1))
                        pool.tensor_tensor(series[:, f, :], series[:, f, :], soft_e[:, f, :], ALU.mult)\
                            .then_inc(cubic_step, 1)
                    pool.wait_ge(dtu_ready, b * (2 * KI) + (m * KI + KI))
                    alone(pool)
                    pool.memset(yT_flat, 0.0).then_inc(y_zero, 1)
                    pool.wait_ge(act_drained, job_a(b, f"uT{m}", TT) + RING)
                    alone(pool)
                    with pool.Fori(0, NS) as s:
                        for half in range(2):
                            u = unit(b, m, s, half)
                            pool.wait_ge(bcol_ready, u + 1)
                            pool.wait_ge(dbu_full, u * KI + 1)
                            alone(pool)
                            for j in range(JT):
                                pool.tensor_scalar(g[:, half, j, :], uT[:, half * JT + j, :], bcol[:, half, j:j + 1],
                                                   1.0, ALU.mult, ALU.mult).then_inc(g_ready, 1)
                pool.wait_ge(dve_drained, job_d(b, "mo1", TT // 2) + RING)
                pool.wait_ge(sum01, b + 1)
                pool.tensor_tensor(base[:, :, :], base[:, :, :], o2[:, :, :], ALU.add).then_inc(base_ready, 1)
                pool.wait_ge(base_ready, b * 2 + 1)
                alone(pool)
                pool.tensor_scalar(base[:, :, :], base[:, :, :], SHRINK, 1.0, ALU.mult, ALU.mult).then_inc(base_ready, 1)

            pool.wait_ge(xs_zeroed, 16 * (-(-(TILES + 1) // 4) + E // 4))
            pool.wait_ge(x2_loaded, 16)
            pool.iota(steps_i, pattern=[[0, E], [P, STEPS]], base=0, channel_multiplier=0).then_inc(steps_ready, 1)
            for e in range(2):
                load_expert(pool, e, e)
            pool.wait_ge(routed, 1)
            for r in range(2):
                for t in range(NT):
                    pool.indirect_dma_start(xs_dram, bass.IndirectOffsetOnAxis(slot[:, r, t:t + 1], 0), x2[:, t, :], None)\
                        .then_inc(xs_sorted, 16)

            def keep_results(e):
                first, end = expert_tiles(pool, e)
                with pool.Fori(first, end) as i:
                    pool.wait_ge(y_ready, i + 2)
                    alone(pool)
                    pool.dma_start(ys_dram[bass.ds(i * P, P), :], ys[:, bass.ds(i, 1), :].rearrange("p o d -> p (o d)"))\
                        .then_inc(y_stored, 16)
                return end

            with pool.Fori(0, E // 2 - 1) as pair:
                for r in range(2):
                    end = keep_results(pair * 2 + r)
                    pool.wait_ge(y_ready, end + 1)
                    alone(pool)
                    load_expert(pool, pair * 2 + (r + 2), r)
            for e in range(E - 2, E):
                tiles = keep_results(e)
            pool.wait_ge(y_stored, tiles * 16)
            alone(pool)
            for t in range(NT):
                for r in range(2):
                    pool.indirect_dma_start(picked[:, r, t, :], None, ys_dram, bass.IndirectOffsetOnAxis(slot[:, r, t:t + 1], 0))\
                        .then_inc(picked_in[t // TT], 16)

        @block.scalar
        def _(act):
            act.sem_inc(act_drained, RING)
            act.wait_ge(eps_ready, 2)
            act.wait_ge(w_loaded, LOADED)
            act.activation(lng[:, 1:2], lng[:, 0:1], ACT.Abs).then_inc(act_setup, 1)
            act.activation(alog_sb[:, :, :], alog_sb[:, :, :], ACT.Exp).then_inc(act_setup, 1)
            act.wait_ge(act_setup, 2)
            act.activation(lng[:, 2:3], lng[:, 1:2], ACT.Exp, scale=-1.0).then_inc(act_setup, 1)
            act.wait_ge(act_setup, 3)
            act.activation(lng[:, 3:4], lng[:, 2:3], ACT.Ln, bias=1.0).then_inc(act_setup, 1)
            act.wait_ge(dve_setup, 4)
            act.activation(strip[:, :], strip[:, :], ACT.Exp, scale=lng[:, 5:6]).then_inc(act_setup, 1)

            def drain(job, bank, dst, width=BANK, func=ACT.Copy, **kw):
                act.wait_ge(act_full, job + 1)
                act.activation(dst, psA[:, bank, 0:width], func, **kw).then_inc(act_drained, 1)

            def turned(b, stage, dst, scale=None, shift=0):
                for j in range(2 * KD):
                    k, half = j // 2, j % 2
                    kw = {} if scale is None else {"scale": scale[:, k:k + 1]}
                    drain(job_a(b, stage, j), bank_a(stage, j),
                          dst[:, k, shift + half * HALF:shift + (half + 1) * HALF], **kw)

            def root_of(dst, src, scale, ready, eps=0):
                act.wait_ge(*ready)
                act.activation(dst, src, ACT.Sqrt, scale=scale, bias=eps_sb[:, eps:eps + 1]).then_inc(root, 1)

            def mamba(b, m):
                blk = b * 2 + m
                src = xin if m == 0 else x1
                if m == 0:
                    act.wait_ge(x_loaded, b * 16 + 16)
                    act.wait_ge(x2_stored, b * 16 + 16)
                for t in range(TT):
                    if m == 1 and t % 2 == 0:
                        act.wait_ge(dve_drained, job_d(b, "mo0", t // 2) + 1 + RING)
                    act.activation(xn[:, t, :], src[:, t, :], ACT.Square, accum_out=ss[:, t:t + 1]).then_inc(squares, 1)
                root_of(rt[:, :], ss[:, :], 1.0 / D, (squares, blk * TT + TT))
                turned(b, f"xnT{m}", xnT, norm_sb[:, m, :])
                act.wait_ge(pads_zero, blk + 1)

                def drain_in(stage, j, n):
                    f, half = n // 2, n % 2
                    dst = (pre[:, f, TAPS - 1 + half * HALF:TAPS - 1 + (half + 1) * HALF] if f < KI
                           else gate[:, f - KI, half * HALF:(half + 1) * HALF])
                    drain(job_a(b, stage, j), bank_a(stage, j), dst, func=ACT.Identity, bias=in_b_sb[:, f:f + 1])

                def silu_conv(f):
                    act.wait_ge(conv_step, blk * ((TAPS - 1) * KI) + (TAPS - 1) * (f + 1))
                    act.activation(xm[:, f, :], xm[:, f, :], ACT.Silu).then_inc(xm_ready, 1)

                for f in range(KI):
                    for half in range(2):
                        drain_in(f"in{m}", 2 * f + half, 2 * f + half)
                    act.wait_ge(act_drained, job_a(b, f"in{m}", 2 * f + 1) + 1 + RING)
                    act.activation(xm[:, f, :], pre[:, f, 0:T], ACT.Identity, scale=conv_w_sb[:, f, 0:1],
                                   bias=conv_b_sb[:, f:f + 1]).then_inc(tap0_ready, 1)
                    if f >= 1:
                        silu_conv(f - 1)
                for j in range(2 * KI, 2 * KI + EARLY):
                    drain_in(f"in{m}", j, j)
                    if j == 2 * KI + 1:
                        silu_conv(KI - 1)
                for j in range(2):
                    act.wait_ge(act_full, job_a(b, f"rank{m}", j) + 1)
                    act.activation(rank_sb[:, j * HALF:(j + 1) * HALF], psA[0:R, bank_a(f"rank{m}", j), :], ACT.Copy)\
                       .then_inc(act_drained, 1)

                def absolute(f):
                    act.wait_ge(dve_drained, job_d(b, f"z{m}", 2 * f + 1) + 1 + RING)
                    act.activation(soft_e[:, f, :], dt[:, f, :], ACT.Abs).then_inc(soft_abs, 1)

                absolute(0)
                for f in range(KI):
                    if f + 1 < KI:
                        absolute(f + 1)
                    act.wait_ge(soft_abs, blk * KI + f + 1)
                    act.activation(soft_e[:, f, :], soft_e[:, f, :], ACT.Exp, scale=-1.0).then_inc(soft_exp, 1)
                for f in range(KI):
                    act.wait_ge(soft_exp, blk * KI + f + 1)
                    act.activation(soft_ln[:, f, :], soft_e[:, f, :], ACT.Ln, bias=1.0).then_inc(soft_log, 1)
                for j in range(2):
                    act.wait_ge(act_full, job_a(b, f"bc{m}", j) + 1)
                    act.activation(bc[:, j * JT:(j + 1) * JT, :], psA[:, bank_a(f"bc{m}", j), 0:JT * 2 * NS]
                                   .rearrange("p (t c) -> p t c", t=JT), ACT.Copy).then_inc(act_drained, 1)
                for j in range(2 * KI - EARLY):
                    drain_in(f"late{m}", j, 2 * KI + EARLY + j)
                for j in range(TT):
                    drain(job_a(b, f"uT{m}", j), bank_a(f"uT{m}", j), uT[:, j, :])
                act.wait_ge(dt_ready, blk * KI + KI)
                with act.Fori(0, NS) as s:
                    for half in range(2):
                        u = unit(b, m, s, half)
                        act.wait_ge(g_ready, u * JT + 1)
                        act.activation(bcol[:, half, :], bc[:, half * JT:(half + 1) * JT, bass.ds(s, 1)]
                                       .rearrange("p t o -> p (t o)"), ACT.Copy).then_inc(bcol_ready, 1)
                        act.wait_ge(scanned, u * KI + 1)
                        alone(act)
                        for f in range(KI):
                            act.activation(da[:, half, f, :], dt[:, f, half * HALF:(half + 1) * HALF], ACT.Exp,
                                           scale=negA[:, f, bass.ds(s, 1)]).then_inc(da_ready, 1)
                act.wait_ge(act_drained, job_a(b, f"late{m}", 2 * KI - EARLY) + RING)
                for f in range(KI):
                    act.activation(gate[:, f, :], gate[:, f, :], ACT.Silu).then_inc(gate_ready, 1)

            with act.Fori(0, B) as b:
                for m in range(2):
                    mamba(b, m)
                turned(b, "oT", oT, shift=1)
                for j in range(TT // 2):
                    drain(job_a(b, "v", j), bank_a("v", j), v_sb[:, 2 * j:2 * j + 2, :].rearrange("p t d -> p (t d)"))
                turned(b, "rT", rT)
                root_of(rt[:, :], aggr[:, :, 1], 1.0, (ln_stats, b * (4 * TT) + 2 * TT), 1)
                turned(b, "xaT", xaT)
                turned(b, "qT", qT)

                def exps(t):
                    for n in range(2):
                        act.wait_ge(dve_drained, job_d(b, "score", score_job(t, n)) + 1 + RING)
                        act.activation(prob[:, t % 4, n, :], prob[:, t % 4, n, :], ACT.Exp).then_inc(expo, 1)

                exps(0)
                exps(1)
                for t in range(TT + 2):
                    if t < TT:
                        for n in range(2):
                            j = probs_job(t, n)
                            drain(job_a(b, "probs", j), bank_a("probs", j), probT[:, t % 4, n, :])
                    if t + 2 < TT:
                        exps(t + 2)
                    if t >= 2:
                        j = heads_job(t - 2)
                        act.wait_ge(act_full, job_a(b, "probs", j) + 1)
                        act.activation(attT[:, :, (t - 2) * P:(t - 1) * P], psA[:, bank_a("probs", j), 0:KD * P]
                                       .rearrange("p (k t) -> p k t", k=KD), ACT.Copy).then_inc(act_drained, 1)
                root_of(rt[:, :], aggr[:, :, 1], 1.0, (ln_stats, b * (4 * TT) + 4 * TT))

            for j in range(KD * CH):
                k, c = j % KD, j // KD
                drain(END_A + j, j % RING, x2T[:, k, c * BANK:(c + 1) * BANK])
            act.wait_ge(route_step, GAP_STEP)
            act.activation(rest[:, 1, :], rest[:, 0, :], ACT.Exp).then_inc(gap_exp, 1)
            act.sem_inc(tileT_ready, 1)

            def tile_turned(i):
                act.wait_ge(tileT_full, i + 2)
                act.activation(tileT, psA[:, 0, 0:KD * P].rearrange("p (k t) -> p k t", k=KD), ACT.Copy)\
                   .then_inc(tileT_ready, 1)

            tile_turned(0)
            act.wait_ge(routed, 1)
            with act.Fori(0, E // 2) as pair:
                for r in range(2):
                    first, end = expert_tiles(act, pair * 2 + r)
                    with act.Fori(first, end) as i:
                        for n in range(2):
                            act.wait_ge(hid_ready, i * 2 + (n + 3))
                            act.activation(act_hid[:, n * BANK:(n + 1) * BANK], hid[:, n * BANK:(n + 1) * BANK], ACT.Gelu)\
                               .then_inc(gelu_ready, 1)
                        tile_turned(i + 1)
            for q in range(B):
                for r in range(2):
                    act.wait_ge(fin_step, FIN_PER * q + 2 * TT + r * (FIN_NORM + 3) + 2 * TT)
                    act.activation(frt[:, q % 2, r, :], faggr[:, q % 2, :, 1], ACT.Sqrt, bias=eps_sb[:, 0:1])\
                       .then_inc(fin_root, 1)

        @block.tensor
        def _(pe):
            def claim_a(job):
                pe.wait_ge(act_drained, job + 1)

            def claim_d(job):
                pe.wait_ge(dve_drained, job + 1)

            def turn(b, stage, src):
                for j in range(2 * KD):
                    k, half = j // 2, j % 2
                    claim_a(job_a(b, stage, j))
                    for t in range(JT):
                        mm = pe.transpose(psA[:, bank_a(stage, j), t * P:(t + 1) * P],
                                          src[:, half * JT + t, k * P:(k + 1) * P], ident[:, :])
                    mm.then_inc(act_full, 1)

            def product(out_ap, pairs):
                for i, (lhs, rhs) in enumerate(pairs):
                    mm = pe.matmul(out_ap, lhs, rhs, start=i == 0, stop=i == len(pairs) - 1)
                return mm

            def token_rows(bank, ps, t0, lhs, rhs, tiles):
                for r in range(2):
                    mm = product(ps[:, bank, r * D:(r + 1) * D],
                                 [(lhs[:, k, (t0 + r) * P:(t0 + r + 1) * P], rhs[:, k, :]) for k in range(tiles)])
                return mm

            pe.wait_ge(w_loaded, LOADED)
            pe.wait_ge(consts_ready, CONSTS)
            for m in range(KD):
                claim_d(m)
                product(psD[:, m, 0:B * M].rearrange("p (b m) -> p b m", b=B), [(wk_sb[:, c, m * P:(m + 1) * P], ctx_sb[:, c, :, 0:M]) for c in range(2)])\
                    .then_inc(dve_full, 1)
            for j in range(B // 2):
                claim_d(KD + j)
                for r in range(2):
                    mm = product(psD[:, KD + j, r * D:(r + 1) * D],
                                 [(ctx_sb[:, c, 2 * j + r, :], wv_sb[:, c, :]) for c in range(2)])
                mm.then_inc(dve_full, 1)

            def mamba(b, m):
                blk = b * 2 + m
                pe.wait_ge(normed, blk * TT + TT)
                turn(b, f"xnT{m}", xn)
                pe.wait_ge(act_drained, job_a(b, f"xnT{m}", 2 * KD) + RING)

                def project_in(stage, j, n):
                    f, half = n // 2, n % 2
                    claim_a(job_a(b, stage, j))
                    product(psA[:, bank_a(stage, j), :],
                            [(in_w_sb[:, k, f * P:(f + 1) * P], xnT[:, k, half * HALF:(half + 1) * HALF])
                             for k in range(KD)]).then_inc(act_full, 1)

                for j in range(2 * KI + EARLY):
                    project_in(f"in{m}", j, j)
                for j in range(2):
                    claim_a(job_a(b, f"rank{m}", j))
                    for k in range(KI):
                        if j == 0:
                            pe.wait_ge(xm_ready, blk * KI + k + 1)
                        mm = pe.matmul(psA[0:R, bank_a(f"rank{m}", j), :], xp_w_sb[:, k, 0:R],
                                       xm[:, k, j * HALF:(j + 1) * HALF], start=k == 0, stop=k == KI - 1)
                    mm.then_inc(act_full, 1)
                for j in range(2 * KI):
                    f, half = j // 2, j % 2
                    pe.wait_ge(act_drained, job_a(b, f"rank{m}", half) + 1 + RING)
                    claim_d(job_d(b, f"z{m}", j))
                    pe.matmul(psD[:, bank_d(f"z{m}", j), :], dt_w_sb[:, f * P:(f + 1) * P],
                              rank_sb[:, half * HALF:(half + 1) * HALF], start=True, stop=True).then_inc(dve_full, 1)
                for j in range(2):
                    claim_a(job_a(b, f"bc{m}", j))
                    for t in range(JT):
                        mm = product(psA[:, bank_a(f"bc{m}", j), t * 2 * NS:(t + 1) * 2 * NS],
                                     [(xm[:, k, (j * JT + t) * P:(j * JT + t + 1) * P], xp_w_sb[:, k, R:R + 2 * NS])
                                      for k in range(KI)])
                    mm.then_inc(act_full, 1)
                for j in range(2 * KI - EARLY):
                    project_in(f"late{m}", j, 2 * KI + EARLY + j)
                pe.wait_ge(dtu_ready, blk * KI + KI)
                for j in range(TT):
                    claim_a(job_a(b, f"uT{m}", j))
                    for f in range(KI):
                        mm = pe.transpose(psA[:, bank_a(f"uT{m}", j), f * P:(f + 1) * P],
                                          dtu[:, f, j * P:(j + 1) * P], ident[:, :])
                    mm.then_inc(act_full, 1)
                pe.wait_ge(act_drained, job_a(b, f"uT{m}", TT) + RING)
                pe.wait_ge(dve_drained, job_d(b, f"z{m}", 2 * KI) + RING)

                def inputs(s, half):
                    u = unit(b, m, s, half)
                    pe.wait_ge(g_ready, u * JT + (2 * JT + 1))
                    for f in range(KI):
                        pe.wait_ge(scanned, u * KI + (f + 2))
                        for j in range(JT):
                            mm = pe.transpose(psD[:, f, j * P:(j + 1) * P], g[:, half, j, f * P:(f + 1) * P], ident[:, :])
                        mm.then_inc(dbu_full, 1)

                def states(s, half):
                    u = unit(b, m, s, half)
                    pe.wait_ge(scanned, u * KI + (2 * KI + 1))
                    for j in range(JT):
                        pe.wait_ge(summed, u * JT + (j + 2))
                        for f in range(KI):
                            mm = pe.transpose(psA[:, j, f * P:(f + 1) * P], h[:, half, f, j * P:(j + 1) * P], ident[:, :])
                        mm.then_inc(hT_full, 1)

                inputs(0, 0)
                with pe.Fori(0, NS - 1) as s:
                    inputs(s, 1)
                    states(s, 0)
                    inputs(s + 1, 0)
                    states(s, 1)
                inputs(NS - 1, 1)
                states(NS - 1, 0)
                states(NS - 1, 1)

                last = unit(b, m, NS - 1, 1)
                pe.wait_ge(summed, last * JT + (2 * JT + 1))
                for j in range(2 * KI):
                    f, half = j // 2, j % 2
                    claim_d(job_d(b, f"y{m}", j))
                    for t in range(JT):
                        mm = pe.transpose(psD[:, bank_d(f"y{m}", j), t * P:(t + 1) * P],
                                          yT[:, half * JT + t, f * P:(f + 1) * P], ident[:, :])
                    mm.then_inc(dve_full, 1)
                pe.wait_ge(gated, blk * KI + KI)
                for j in range(TT // 2):
                    claim_d(job_d(b, f"mo{m}", j))
                    token_rows(bank_d(f"mo{m}", j), psD, 2 * j, y, out_w_sb, KI).then_inc(dve_full, 1)

            pe.sem_inc(hT_full, JT + 1)
            pe.sem_inc(dbu_full, KI + 1)
            with pe.Fori(0, B) as b:
                for m in range(2):
                    mamba(b, m)
                pe.wait_ge(dve_drained, job_d(b, "mo1", TT // 2) + RING)
                turn(b, "oT", o2)
                pe.wait_ge(act_drained, job_a(b, "oT", 2 * KD) + RING)
                pe.wait_ge(blocks_ready, b * 3 + 1)
                for j in range(TT // 2):
                    claim_a(job_a(b, "v", j))
                    token_rows(bank_a("v", j), psA, 2 * j, oT[:, :, 1:T + 1], write_w_sb, KD).then_inc(act_full, 1)
                for j, (i, half) in enumerate(MEM_S):
                    lo, hi = max(P * i, half * HALF), (half + 1) * HALF
                    claim_d(job_d(b, "mem", j))
                    product(psD[:, bank_d("mem", j), 0:hi - lo],
                            [(oT[:, k, P * i:P * i + P], oT[:, k, 1 + lo:1 + hi]) for k in range(KD)]).then_inc(dve_full, 1)
                pe.wait_ge(act_drained, job_a(b, "v", TT // 2) + RING)
                pe.wait_ge(dve_drained, job_d(b, "mem", len(MEM_S)) + RING)
                for j in range(2 * KD):
                    k, half = j // 2, j % 2
                    claim_a(job_a(b, "rT", j))
                    tiles = [i for i in range(TT) if (i, half) in MEM_S]
                    for i in tiles:
                        lo, hi = max(P * i, half * HALF), (half + 1) * HALF
                        at0 = sm_first[(i, half)]
                        mm = pe.matmul(psA[:, bank_a("rT", j), lo - half * HALF:HALF], v_sb[:, i, k * P:(k + 1) * P],
                                       sm_flat[:, at0:at0 + hi - lo], start=i == 0, stop=i == tiles[-1])
                    mm.then_inc(act_full, 1)
                pe.wait_ge(act_drained, job_a(b, "rT", 2 * KD) + RING)
                for j in range(TT // 2):
                    claim_d(job_d(b, "rp", j))
                    token_rows(bank_d("rp", j), psD, 2 * j, rT, read_w_sb, KD).then_inc(dve_full, 1)

                pe.wait_ge(ln_done, b * (2 * TT) + TT)
                turn(b, "xaT", xa)
                pe.wait_ge(act_drained, job_a(b, "xaT", 2 * KD) + RING)
                for j in range(2 * KD):
                    f, half = j // 2, j % 2
                    claim_a(job_a(b, "qT", j))
                    product(psA[:, bank_a("qT", j), :], [(wq_sb[:, k, f * P:(f + 1) * P],
                            xaT[:, k, half * HALF:(half + 1) * HALF]) for k in range(KD)]).then_inc(act_full, 1)
                pe.wait_ge(act_drained, job_a(b, "qT", 2 * KD) + RING)
                pe.wait_ge(blocks_ready, b * 3 + 3)

                def scores(t):
                    for n in range(2):
                        j = score_job(t, n)
                        claim_d(job_d(b, "score", j))
                        bank = psD[:, bank_d("score", j), :]
                        pe.matmul(bank, qT[:, n, t * P:(t + 1) * P], kblk[:, n, :, :].rearrange("p h m -> p (h m)"),
                                  start=True, stop=False)
                        pe.matmul(bank.rearrange("p (h m) -> p h m", h=8), mask_ones[:, :], mask_row[0:1, bass.ds(b, 1), :].broadcast_to([1, 8, M]),
                                  start=False, stop=True).then_inc(dve_full, 1)

                def turn_probs(t):
                    for n in range(2):
                        j = probs_job(t, n)
                        pe.wait_ge(expo, b * (2 * TT) + (2 * t + n + 1))
                        claim_a(job_a(b, "probs", j))
                        for q in range(4):
                            mm = pe.transpose(psA[:, bank_a("probs", j), q * P:(q + 1) * P],
                                              prob[:, t % 4, n, q * P:(q + 1) * P], ident[:, :])
                        mm.then_inc(act_full, 1)

                def weigh(t):
                    j = out_job(t)
                    claim_d(job_d(b, "score", j))
                    pe.wait_ge(act_drained, job_a(b, "probs", probs_job(t, 1)) + 1 + RING)
                    for q in range(HEADS // 2):
                        mm = pe.matmul(psD[:, bank_d("score", j), q * 2 * VW:(q + 1) * 2 * VW],
                                       probT[:, t % 4, q // 4, (q % 4) * P:(q % 4 + 1) * P],
                                       vblk[:, q, :, :].rearrange("p h d -> p (h d)"), start=True, stop=True)
                    mm.then_inc(dve_full, 1)

                def turn_heads(t):
                    j = heads_job(t)
                    pe.wait_ge(dve_drained, job_d(b, "score", out_job(t)) + 1 + RING)
                    claim_a(job_a(b, "probs", j))
                    for k in range(KD):
                        mm = pe.transpose(psA[:, bank_a("probs", j), k * P:(k + 1) * P],
                                          att[:, t % 2, k * P:(k + 1) * P], ident[:, :])
                    mm.then_inc(act_full, 1)

                scores(0)
                scores(1)
                for t in range(TT + 2):
                    if t + 2 < TT:
                        scores(t + 2)
                    if t < TT:
                        turn_probs(t)
                    if 1 <= t <= TT:
                        weigh(t - 1)
                    if t >= 2:
                        turn_heads(t - 2)
                pe.wait_ge(act_drained, job_a(b, "probs", 3 * TT) + RING)
                for j in range(TT // 2):
                    claim_d(job_d(b, "wo", j))
                    token_rows(bank_d("wo", j), psD, 2 * j, attT, wo_sb, KD).then_inc(dve_full, 1)

            pe.wait_ge(x2_loaded, 16)
            for j in range(KD * CH):
                k, c = j % KD, j // KD
                claim_a(END_A + j)
                for t in range(4):
                    mm = pe.transpose(psA[:, j % RING, t * P:(t + 1) * P], x2[:, 4 * c + t, k * P:(k + 1) * P], ident[:, :])
                mm.then_inc(act_full, 1)
            pe.wait_ge(act_drained, END_A + KD * CH + RING)
            for j in range(4):
                claim_d(END_D + j)
                for t in range(8):
                    mm = product(psD[:, (END_D + j) % RING, t * E:(t + 1) * E],
                                 [(x2T[:, k, (8 * j + t) * P:(8 * j + t + 1) * P], wg_sb[:, k, :]) for k in range(KD)])
                mm.then_inc(dve_full, 1)
            pe.wait_ge(route_step, SEL_STEP)
            for j, lhs in enumerate((below, ones)):
                claim_d(END_D + 4 + j)
                pe.matmul(psD[:, (END_D + 4 + j) % RING, 0:NT * E], lhs[:, :], sel.rearrange("p t e -> p (t e)"),
                          start=True, stop=True).then_inc(dve_full, 1)

            def turn_tile(i):
                pe.wait_ge(xs_loaded, i * 16 + 16)
                pe.wait_ge(tileT_ready, i + 1)
                for k in range(KD):
                    mm = pe.transpose(psA[:, 0, k * P:(k + 1) * P],
                                      tile_in[:, k * P:(k + 1) * P], ident[:, :])
                mm.then_inc(tileT_full, 1)

            pe.sem_inc(tileT_full, 1)
            pe.wait_ge(dve_drained, END_D + 6 + RING)
            pe.wait_ge(act_drained, END_A + KD * CH + RING)
            turn_tile(0)
            with pe.Fori(0, E // 2) as pair:
                for r in range(2):
                    first, end = expert_tiles(pe, pair * 2 + r)
                    pe.wait_ge(w_ready[r], pair * 64 + 64)
                    alone(pe)
                    with pe.Fori(first, end) as i:
                        pe.wait_ge(tileT_ready, i + 2)
                        for n in range(2):
                            pe.wait_ge(hid_ready, i * 2 + (n + 1))
                            product(psD[:, n, :], [(tileT[:, k, :], w1_sb[:, r, k, n * BANK:(n + 1) * BANK])
                                                   for k in range(KD)]).then_inc(hid_full, 1)
                        turn_tile(i + 1)
                        pe.wait_ge(y_ready, i + 1)
                        for n in range(2):
                            pe.wait_ge(gelu_ready, i * 2 + (n + 1))
                            pe.wait_ge(hidT_ready, i * 2 + (n + 1))
                            for k in range(4):
                                mm = pe.transpose(psA[:, 1 + n, k * P:(k + 1) * P],
                                                  act_hid[:, (4 * n + k) * P:(4 * n + k + 1) * P], ident[:, :])
                            mm.then_inc(turn_full, 1)
                            pe.wait_ge(hidT_ready, i * 2 + (n + 3))
                            for k in range(4 * n, 4 * n + 4):
                                mm = pe.matmul(psD[:, 2, 0:D], hidT[:, k, :], w2_sb[:, r, k, :],
                                               start=k == 0, stop=k == KH - 1)
                        mm.then_inc(y_full, 1)

        @block.vector
        def _(dve):
            dve.sem_inc(dve_drained, RING)
            dve.sem_inc(scanned, KI + 1)
            dve.sem_inc(summed, JT + 1)
            dve.memset(eps_sb[:, 0:1], EPS).then_inc(eps_ready, 1)
            dve.memset(eps_sb[:, 1:2], EPS * SHRINK ** 2).then_inc(eps_ready, 1)
            dve.wait_ge(consts_ready, 4)
            dve.tensor_scalar(strip[:, :], iota_i, 0.0, None, ALU.max).then_inc(dve_setup, 1)
            dve.tensor_copy(expert_id[:, :], expert_i[:, :]).then_inc(expert_ready, 1)
            dve.wait_ge(w_loaded, LOADED)
            dve.tensor_scalar(lng[:, 4:5], lng[:, 0:1], -1.0, 0.0, ALU.mult, ALU.max).then_inc(dve_setup, 1)
            dve.wait_ge(act_setup, 4)
            dve.tensor_scalar(negA[:, :, :], alog_sb[:, :, :], -1.0, None, ALU.mult).then_inc(dve_setup, 1)
            dve.wait_ge(dve_setup, 3)
            dve.tensor_scalar(lng[:, 5:6], lng[:, 4:5], lng[:, 3:4], -1.0, ALU.add, ALU.mult).then_inc(dve_setup, 1)
            dve.tensor_scalar(mask_row[:, :, :], mask_u8[:, :, :], -1.0, -MASKED, ALU.add, ALU.mult).then_inc(dve_setup, 1)
            dve.memset(mask_ones[:, :], 1.0).then_inc(dve_setup, 1)
            dve.wait_ge(expert_ready, 1)
            dve.wait_ge(consts_ready, CONSTS)
            for m in range(KD):
                dve.wait_ge(dve_full, m + 1)
                dve.tensor_copy(kT[:, m, :, :].rearrange("p b m -> p (b m)"), psD[:, m, 0:B * M]).then_inc(dve_drained, 1)
            for j in range(B // 2):
                dve.wait_ge(dve_full, KD + j + 1)
                dve.tensor_copy(vdup[:, 2 * j:2 * j + 2, :].rearrange("p b d -> p (b d)"), psD[:, KD + j, :])\
                   .then_inc(dve_drained, 1)

            def mamba(b, m):
                blk = b * 2 + m
                src = xin if m == 0 else x1
                rb = b * 4 + m
                dve.wait_ge(root, rb + 1)
                dve.reciprocal(rs[:, :], rt[:, :]).then_inc(inverse, 1)
                dve.wait_ge(inverse, b * 5 + (m + 1))
                for t in range(TT):
                    dve.tensor_scalar(xn[:, t, :], src[:, t, :], rs[:, t:t + 1], None, ALU.mult).then_inc(normed, 1)
                dve.memset(pre[:, :, 0:TAPS - 1], 0.0).then_inc(pads_zero, 1)
                for f in range(KI):
                    dve.wait_ge(tap0_ready, blk * KI + f + 1)
                    for tap in range(1, TAPS):
                        if tap > 1:
                            dve.wait_ge(conv_step, blk * ((TAPS - 1) * KI) + ((TAPS - 1) * f + tap - 1))
                        dve.scalar_tensor_tensor(xm[:, f, :], pre[:, f, tap:tap + T], conv_w_sb[:, f, tap:tap + 1],
                                                 xm[:, f, :], op0=ALU.mult, op1=ALU.add).then_inc(conv_step, 1)
                for j in range(2 * KI):
                    f, half = j // 2, j % 2
                    dve.wait_ge(dve_full, job_d(b, f"z{m}", j) + 1)
                    dve.tensor_scalar(dt[:, f, half * HALF:(half + 1) * HALF], psD[:, bank_d(f"z{m}", j), :],
                                      dt_b_sb[:, f:f + 1], None, ALU.add).then_inc(dve_drained, 1)

                def times_u(f):
                    dve.wait_ge(dt_ready, blk * KI + f + 1)
                    dve.tensor_tensor(dtu[:, f, :], dt[:, f, :], xm[:, f, :], ALU.mult).then_inc(dtu_ready, 1)

                for f in range(KI):
                    done = blk * (2 * KI) + 2 * f
                    dve.wait_ge(cubic_step, done + 2)
                    dve.scalar_tensor_tensor(series[:, f, :], series[:, f, :], 1.0, soft_e[:, f, :],
                                             op0=ALU.add, op1=ALU.mult).then_inc(series_step, 1)
                    if f >= 1:
                        times_u(f - 1)
                    dve.wait_ge(small_found, blk * KI + f + 1)
                    dve.wait_ge(soft_log, blk * KI + f + 1)
                    dve.wait_ge(series_step, done + 1)
                    alone(dve)
                    dve.copy_predicated(soft_ln[:, f, :], is_small[:, f, :], series[:, f, :]).then_inc(series_step, 1)
                    dve.wait_ge(series_step, done + 2)
                    dve.scalar_tensor_tensor(dt[:, f, :], dt[:, f, :], 0.0, soft_ln[:, f, :],
                                             op0=ALU.max, op1=ALU.add).then_inc(dt_ready, 1)
                times_u(KI - 1)

                def scans(s, half):
                    u = unit(b, m, s, half)
                    dve.wait_ge(hT_full, u * JT + 1)
                    if half == 1:
                        dve.wait_ge(scanned, u * KI + (KI + 1))
                    for f in range(KI):
                        dve.wait_ge(da_ready, u * KI + (f + 1))
                        dve.wait_ge(dbu_full, u * KI + (KI + f + 2))
                        start = 0.0 if half == 0 else h[:, 0, f, HALF - 1:HALF]
                        dve.tensor_tensor_scan(h[:, half, f, :], da[:, half, f, :], psD[:, f, :], start,
                                               ALU.mult, ALU.add).then_inc(scanned, 1)

                def sums(s, half):
                    u = unit(b, m, s, half)
                    dve.wait_ge(summed, u * JT + 1)
                    for j in range(JT):
                        t = half * JT + j
                        dve.wait_ge(hT_full, u * JT + (JT + j + 2))
                        dve.scalar_tensor_tensor(yT[:, t, :], psA[:, j, :],
                                                 bc[:, t, bass.ds(s + NS, 1)], yT[:, t, :],
                                                 op0=ALU.mult, op1=ALU.add).then_inc(summed, 1)

                dve.wait_ge(y_zero, blk + 1)
                dve.wait_ge(act_drained, job_a(b, f"uT{m}", TT) + RING)
                scans(0, 0)
                with dve.Fori(0, NS - 1) as s:
                    scans(s, 1)
                    sums(s, 0)
                    scans(s + 1, 0)
                    sums(s, 1)
                scans(NS - 1, 1)
                sums(NS - 1, 0)
                sums(NS - 1, 1)

                for j in range(2 * KI):
                    f, half = j // 2, j % 2
                    dve.wait_ge(dve_full, job_d(b, f"y{m}", j) + 1)
                    dve.scalar_tensor_tensor(y[:, f, half * HALF:(half + 1) * HALF], xm[:, f, half * HALF:(half + 1) * HALF],
                                             d_sb[:, f:f + 1], psD[:, bank_d(f"y{m}", j), :],
                                             op0=ALU.mult, op1=ALU.add).then_inc(dve_drained, 1)
                for f in range(KI):
                    dve.wait_ge(dve_drained, job_d(b, f"y{m}", 2 * f + 1) + 1 + RING)
                    dve.wait_ge(gate_ready, blk * KI + f + 1)
                    dve.tensor_tensor(y[:, f, :], y[:, f, :], gate[:, f, :], ALU.mult).then_inc(gated, 1)
                if m == 0:
                    dve.wait_ge(xb_ready, b + 1)
                for j in range(TT // 2):
                    dve.wait_ge(dve_full, job_d(b, f"mo{m}", j) + 1)
                    ps = psD[:, bank_d(f"mo{m}", j), :].rearrange("p (t d) -> p t d", t=2)
                    if m == 0:
                        dve.tensor_tensor(x1[:, 2 * j:2 * j + 2, :], ps, base[:, 2 * j:2 * j + 2, :], ALU.add)\
                           .then_inc(dve_drained, 1)
                    else:
                        dve.tensor_tensor(o2[:, 2 * j:2 * j + 2, :], ps,
                                          out_b_sb[:, :].unsqueeze(1).broadcast_to([P, 2, D]), ALU.add)\
                           .then_inc(dve_drained, 1)

            def layer_norm(b, n, z, dst):
                for t in range(TT):
                    dve.bn_stats(stats[:, t, :], z[:, t, :]).then_inc(ln_stats, 1)
                dve.wait_ge(ln_stats, b * (4 * TT) + (2 * TT * n + TT))
                alone(dve)
                for t in range(TT):
                    dve.bn_aggr(aggr[:, t, :], stats[:, t, :]).then_inc(ln_stats, 1)
                dve.wait_ge(root, b * 4 + (3 + n))
                dve.reciprocal(rs[:, :], rt[:, :]).then_inc(inverse, 1)
                dve.wait_ge(inverse, b * 5 + (3 + 2 * n))
                if n == 0:
                    dve.scalar_tensor_tensor(rs[:, :], aggr[:, :, 1], VAR_LIMIT / D, rs[:, :],
                                             op0=ALU.is_le, op1=ALU.mult).then_inc(inverse, 1)
                    dve.wait_ge(inverse, b * 5 + 4)
                for t in range(TT):
                    dve.tensor_scalar(dst[:, t, :], z[:, t, :], aggr[:, t, 0:1], rs[:, t:t + 1],
                                      ALU.subtract, ALU.mult).then_inc(ln_done, 1)

            with dve.Fori(0, B) as b:
                for m in range(2):
                    mamba(b, m)
                dve.memset(oT[:, :, 0:1], 0.0).then_inc(blocks_ready, 1)
                for j, (i, half) in enumerate(MEM_S):
                    lo, hi = max(P * i, half * HALF), (half + 1) * HALF
                    at0 = sm_first[(i, half)]
                    dve.wait_ge(dve_full, job_d(b, "mem", j) + 1)
                    dve.tensor_tensor(sm_flat[:, at0:at0 + hi - lo], psD[:, bank_d("mem", j), 0:hi - lo],
                                      strip[:, lo - P * i:hi - P * i], ALU.mult).then_inc(dve_drained, 1)
                for k in range(KD):
                    last = dve.tensor_tensor(kblk[:, k, :, :], kT[:, k, bass.ds(b, 1), :].broadcast_to([P, 8, M]),
                                             headmask[:, :].unsqueeze(2).broadcast_to([P, 8, M]), ALU.mult)
                last.then_inc(blocks_ready, 1)
                for r in range(2):
                    dve.tensor_scalar(vblk[:, :, r, 0:HD], vdup[:, bass.ds(b, 1), :].rearrange(
                        "p o (q r d) -> p (o q) r d", r=2, d=HD)[:, :, r, :], pairmask[:, r:r + 1], None, ALU.mult)
                    last = dve.tensor_copy(vblk[:, :, r, HD:VW], pairmask[:, r:r + 1].unsqueeze(1)
                                           .broadcast_to([P, HEADS // 2, 1]))
                last.then_inc(blocks_ready, 1)
                dve.wait_ge(base_ready, b * 2 + 2)
                for j in range(TT // 2):
                    dve.wait_ge(dve_full, job_d(b, "rp", j) + 1)
                    dve.scalar_tensor_tensor(base[:, 2 * j:2 * j + 2, :].rearrange("p t d -> p (t d)"),
                                             psD[:, bank_d("rp", j), :], ALPHA * SHRINK,
                                             base[:, 2 * j:2 * j + 2, :].rearrange("p t d -> p (t d)"),
                                             op0=ALU.mult, op1=ALU.add).then_inc(dve_drained, 1)
                dve.wait_ge(dve_drained, job_d(b, "rp", TT // 2) + RING)
                layer_norm(b, 0, base, xa)

                def less_max(t):
                    for n in range(2):
                        j = score_job(t, n)
                        bank = psD[:, bank_d("score", j), :].rearrange("p (h m) -> p h m", h=8)
                        dve.wait_ge(dve_full, job_d(b, "score", j) + 1)
                        dve.tensor_reduce(mx[:, n, :], bank, AX.X, ALU.max).then_inc(score_max, 1)
                        dve.wait_ge(score_max, b * (2 * TT) + (2 * t + n + 1))
                        if t >= 4:
                            dve.wait_ge(act_full, job_a(b, "probs", probs_job(t - 4, n)) + 1)
                        dve.tensor_tensor(prob[:, t % 4, n, :].rearrange("p (h m) -> p h m", h=8), bank,
                                          mx[:, n, :].unsqueeze(2).broadcast_to([P, 8, M]), ALU.subtract)\
                           .then_inc(dve_drained, 1)

                def normalise(t):
                    bank = psD[:, bank_d("score", out_job(t)), 0:HEADS * VW].rearrange("p (h d) -> p h d", h=HEADS)
                    dve.wait_ge(dve_full, job_d(b, "score", out_job(t)) + 1)
                    dve.reciprocal(rsum[:, t % 2, :], bank[:, :, HD]).then_inc(sum_inv, 1)
                    dve.wait_ge(sum_inv, b * TT + (t + 1))
                    if t >= 2:
                        dve.wait_ge(act_full, job_a(b, "probs", heads_job(t - 2)) + 1)
                    dve.tensor_tensor(att[:, t % 2, :].rearrange("p (h d) -> p h d", h=HEADS), bank[:, :, 0:HD],
                                      rsum[:, t % 2, :].unsqueeze(2).broadcast_to([P, HEADS, HD]), ALU.mult)\
                       .then_inc(dve_drained, 1)

                less_max(0)
                less_max(1)
                for t in range(TT + 1):
                    if t + 2 < TT:
                        less_max(t + 2)
                    if t >= 1:
                        normalise(t - 1)
                for j in range(TT // 2):
                    dve.wait_ge(dve_full, job_d(b, "wo", j) + 1)
                    dve.tensor_tensor(base[:, 2 * j:2 * j + 2, :].rearrange("p t d -> p (t d)"),
                                      psD[:, bank_d("wo", j), :],
                                      xa[:, 2 * j:2 * j + 2, :].rearrange("p t d -> p (t d)"), ALU.add)\
                       .then_inc(dve_drained, 1)
                dve.wait_ge(dve_drained, job_d(b, "wo", TT // 2) + RING)
                layer_norm(b, 1, base, x2_out)

            for j in range(4):
                dve.wait_ge(dve_full, END_D + j + 1)
                dve.tensor_tensor(logit[:, 8 * j:8 * j + 8, :], psD[:, (END_D + j) % RING, 0:8 * E]
                                  .rearrange("p (t e) -> p t e", e=E),
                                  bg_sb[:, :].unsqueeze(1).broadcast_to([P, 8, E]), ALU.add).then_inc(dve_drained, 1)
            dve.wait_ge(dve_drained, END_D + 4 + RING)
            route = 0

            def link(ins, wait=True):
                nonlocal route
                route += 1
                ins.then_inc(route_step, 1)
                if wait:
                    dve.wait_ge(route_step, route)

            for t in range(NT):
                link(dve.max(top[:, t, :], logit[:, t, :]), wait=t == NT - 1)
            link(dve.tensor_tensor(rest[:, 0, :], top[:, :, 1], top[:, :, 0], ALU.subtract), wait=False)
            assert route == GAP_STEP
            for t in range(NT):
                link(dve.max_index(topi[:, t, :], top[:, t, :], logit[:, t, :]), wait=t == NT - 1)
            link(dve.tensor_copy(topf[:, :, 0:2], topi[:, :, 0:2]))
            for r, dst in enumerate((sel1, sel2)):
                link(dve.tensor_tensor(dst, topf[:, :, r:r + 1].broadcast_to([P, NT, E]),
                                       expert_id[:, :].unsqueeze(1).broadcast_to([P, NT, E]), ALU.is_equal))
            link(dve.tensor_tensor(sel, sel1, sel2, ALU.add))
            assert route == SEL_STEP
            dve.wait_ge(gap_exp, 1)
            link(dve.tensor_scalar(rest[:, 2, :], rest[:, 1, :], 1.0, None, ALU.add))
            link(dve.reciprocal(rest[:, 3, :], rest[:, 2, :]))
            link(dve.tensor_tensor(rest[:, 4, :], rest[:, 1, :], rest[:, 3, :], ALU.mult))
            dve.wait_ge(steps_ready, 1)
            link(dve.tensor_copy(steps, steps_i))
            for j, dst in enumerate((place, total)):
                dve.wait_ge(dve_full, END_D + 5 + j)
                dve.tensor_copy(dst.rearrange("p t e -> p (t e)"), psD[:, (END_D + 4 + j) % RING, 0:NT * E])\
                   .then_inc(dve_drained, 1)
            dve.wait_ge(dve_drained, END_D + 6 + RING)
            for e in range(E):
                link(dve.tensor_tensor_scan(cum[:, :, e], ones[:, 0:NT], total[:, :, e], 0.0, ALU.mult, ALU.add),
                     wait=e == E - 1)
            link(dve.tensor_tensor(place, place, cum, ALU.add))
            link(dve.tensor_tensor(place, place, total, ALU.subtract))
            link(dve.tensor_tensor(over, cum[:, NT - 1, :].unsqueeze(2).broadcast_to([P, E, STEPS]), steps, ALU.is_gt))
            link(dve.tensor_reduce(count, over, AX.X, ALU.add))
            link(dve.tensor_scalar(count, count, 1.0, None, ALU.max))
            link(dve.tensor_tensor_scan(ends, ones[:, 0:E], count, 0.0, ALU.mult, ALU.add))
            link(dve.tensor_tensor(firsts, ends, count, ALU.subtract))
            link(dve.tensor_copy(bound[:, 0:E], firsts), wait=False)
            link(dve.tensor_copy(bound[:, E:E + 1], ends[:, E - 1:E]), wait=False)
            link(dve.tensor_scalar(firsts, firsts, float(P), None, ALU.mult))
            link(dve.tensor_tensor(place, place, firsts.unsqueeze(1).broadcast_to([P, NT, E]), ALU.add))
            for r, which in enumerate((sel1, sel2)):
                link(dve.tensor_tensor(weighed, which, place, ALU.mult))
                link(dve.tensor_reduce(rest[:, 5 + r, :], weighed, AX.X, ALU.add))
            dve.tensor_copy(slot[:, :, :], rest[:, 5:7, :]).then_inc(routed, 1)

            dve.sem_inc(hid_ready, 2)
            dve.sem_inc(hidT_ready, 2)
            dve.sem_inc(y_ready, 1)
            dve.wait_ge(routed, 1)
            with dve.Fori(0, E // 2) as pair:
                for r in range(2):
                    first, end = expert_tiles(dve, pair * 2 + r)
                    dve.wait_ge(w_ready[r], pair * 64 + 64)
                    alone(dve)
                    with dve.Fori(first, end) as i:
                        for n in range(2):
                            dve.wait_ge(hid_full, i * 2 + (n + 1))
                            dve.tensor_tensor(hid[:, n * BANK:(n + 1) * BANK], psD[:, n, :],
                                              b1_sb[:, r, n * BANK:(n + 1) * BANK], ALU.add).then_inc(hid_ready, 1)
                        for n in range(2):
                            dve.wait_ge(turn_full, i * 2 + (n + 1))
                            dve.tensor_copy(hidT[:, 4 * n:4 * n + 4, :].rearrange("p k t -> p (k t)"), psA[:, 1 + n, :])\
                               .then_inc(hidT_ready, 1)
                        dve.wait_ge(y_full, i + 1)
                        dve.tensor_tensor(ys[:, bass.ds(i, 1), :].rearrange("p o d -> p (o d)"), psD[:, 2, 0:D],
                                          b2_sb[:, r, :], ALU.add).then_inc(y_ready, 1)

            n = 0

            def fin(ins):
                nonlocal n
                n += 1
                ins.then_inc(fin_step, 1)

            def norm(q, r):
                for t in range(TT):
                    fin(dve.bn_stats(fstats[:, q % 2, t, :], acc[:, q * TT + t, :]))
                dve.wait_ge(fin_step, n)
                for t in range(TT):
                    fin(dve.bn_aggr(faggr[:, q % 2, t, :], fstats[:, q % 2, t, :]))
                dve.wait_ge(fin_root, 2 * q + r + 1)
                fin(dve.reciprocal(frt[:, q % 2, r, :], frt[:, q % 2, r, :]))
                dve.wait_ge(fin_step, n)
                for t in range(TT):
                    fin(dve.tensor_scalar(acc[:, q * TT + t, :], acc[:, q * TT + t, :], faggr[:, q % 2, t, 0:1],
                                          frt[:, q % 2, r, t:t + 1], ALU.subtract, ALU.mult))
                dve.wait_ge(fin_step, n)

            for q in range(B):
                rows = acc[:, q * TT:(q + 1) * TT, :]
                dve.wait_ge(picked_in[q], 2 * TT * 16)
                for r in range(2):
                    for t in range(q * TT, (q + 1) * TT):
                        fin(dve.scalar_tensor_tensor(acc[:, t, :], picked[:, r, t, :], rest[:, 3 + r, t:t + 1],
                                                     (x2 if r == 0 else acc)[:, t, :], op0=ALU.mult, op1=ALU.add))
                    dve.wait_ge(fin_step, n)
                norm(q, 0)
                fin(dve.tensor_tensor(rows, rows, gamma_sb[:, :].unsqueeze(1).broadcast_to([P, TT, D]), ALU.mult))
                dve.wait_ge(fin_step, n)
                fin(dve.tensor_tensor(rows, rows, beta_sb[:, :].unsqueeze(1).broadcast_to([P, TT, D]), ALU.add))
                dve.wait_ge(fin_step, n)
                fin(dve.tensor_tensor(rows, rows, x2[:, q * TT:(q + 1) * TT, :], ALU.add))
                dve.wait_ge(fin_step, n)
                norm(q, 1)
                assert n == FIN_PER * (q + 1)


def _layouts(np, a):
    def vec(v):
        return v.reshape(-1, 128).T

    def rows(v):
        return v.reshape(v.shape[0] // 128, 128, -1).transpose(1, 0, 2)

    return {
        "x": a["x"], "ctxT": a["ctx_768"].transpose(0, 2, 1), "ctx_mask": a["mask_BxS2_bf1"].view(np.uint8),
        "norm1_w": vec(a["L0_attn_norm1_w"]), "norm2_w": vec(a["L0_attn_norm2_w"]),
        "in_wT": a["L0_attn_in_proj_w"].T, "in_b": vec(a["L0_attn_in_proj_b"]),
        "conv_w": rows(a["L0_attn_conv_w"][:, 0, :]), "conv_b": vec(a["L0_attn_conv_b"]),
        "xp_wT": a["L0_attn_x_proj_w"].T, "dt_wT": a["L0_attn_dt_proj_w"].T, "dt_b": vec(a["L0_attn_dt_proj_b"]),
        "A_log": rows(a["L0_attn_A_log"]), "D_ssm": vec(a["L0_attn_D_ssm"]),
        "out_wT": a["L0_attn_out_proj_w"].T, "out_b": a["L0_attn_out_proj_b"],
        "write_wT": a["L0_attn_proj_write_w"].T, "read_wT": a["L0_attn_proj_read_w"].T,
        "decay": a["L0_attn_decay"].reshape(1),
        "Wq": a["L0_xattn_Wq"], "Wk": a["L0_xattn_Wk"], "Wv": a["L0_xattn_Wv"], "Wo": a["L0_xattn_Wo"],
        "Wg": a["L0_ffn_Wg"], "bg": a["L0_ffn_bg"], "W1": a["L0_ffn_W1"],
        "b1": a["L0_ffn_b1"],
        "W2": a["L0_ffn_W2"], "b2": a["L0_ffn_b2"], "gamma": a["L0_ffn_gamma"], "beta": a["L0_ffn_beta"],
    }


def kernel(**inputs):
    import numpy as _np
    import concourse.bacc as _bacc
    from concourse import mybir as _mybir
    from concourse.bass_utils import run_bass_kernel_spmd as _run

    nc = _bacc.Bacc("TRN2", target_bir_lowering=False, num_devices=1)
    arrays, args = {}, []
    for name, a in _layouts(_np, {k: _np.asarray(v) for k, v in inputs.items()}).items():
        a = _np.ascontiguousarray(a)
        arrays[f"in_{name}"] = a
        args.append(nc.dram_tensor(f"in_{name}", a.shape, _mybir.dt.from_np(a.dtype), kind="ExternalInput").ap())
    shape = tuple(inputs["x"].shape)
    args.append(nc.dram_tensor("out_0", shape, _mybir.dt.float32, kind="ExternalOutput").ap())
    decoder_layer(nc, *args)
    r = _run(nc, [arrays], core_ids=[0])
    return r.results[0]["out_0"]
```

```python
from contextlib import ExitStack

import numpy as np

import concourse.bass as bass
from concourse import mybir

ALU = mybir.AluOpType
ACT = mybir.ActivationFunctionType
AX = mybir.AxisListType
F32 = mybir.dt.float32
BF16 = mybir.dt.bfloat16
I32 = mybir.dt.int32
U32 = mybir.dt.uint32
U8 = mybir.dt.uint8

P = 128
EPS = 1e-5
ALPHA = 0.1
MASKED = -1.0e30
SMALL_E = 2.0 ** -7
SHRINK = 2.0 ** -40
VAR_LIMIT = float(np.finfo(np.float32).max) * SHRINK ** 2
RING = 4
BANK = 512


def offsets(stages):
    at, first = 0, {}
    for name, count in stages:
        first[name] = at
        at += count
    return first, at


def decoder_layer(nc, x, ctxT, ctx_mask, norm1_w, norm2_w, in_wT, in_b, conv_w, conv_b, xp_wT, dt_wT, dt_b,
                  A_log, D_ssm, out_wT, out_b, write_wT, read_wT, decay, Wq, Wk, Wv, Wo,
                  Wg, bg, W1, b1, W2, b2, gamma, beta, out):
    B, T, D = x.shape
    DI = out_wT.shape[0]
    NS = A_log.shape[2]
    R = dt_wT.shape[0]
    TAPS = conv_w.shape[2]
    CD, M = ctxT.shape[1], ctxT.shape[2]
    HEADS = 16
    HD = D // HEADS
    E = Wg.shape[1]
    HID = W1.shape[2]
    TT = T // P
    KD = D // P
    KI = DI // P
    HALF = T // 2
    JT = HALF // P
    JS = JT - 1
    KH = HID // P
    CH = B * T // BANK
    NT = B * T // P
    CP = CD // 2
    VW = HD + 1
    assert HALF == BANK and M * 8 == BANK and KI * P == BANK

    EARLY = 4
    MAMBA_A = [("xnT", 2 * KD), ("in", 2 * KI + EARLY), ("rank", 2), ("bc", 2), ("late", 2 * KI - EARLY), ("uT", 2 * KI)]
    MAMBA_D = [("z", 2 * KI), ("y", 2 * KI), ("mo", TT // 2)]
    SEQ_A = [(f"{n}{m}", c) for m in range(2) for n, c in MAMBA_A] + [
        ("oT", 2 * KD), ("v", TT // 2), ("rT", 2 * KD),
        ("xaT", 2 * KD), ("qT", 2 * KD), ("probs", 3 * TT)]
    MEM_S = [(i, h) for i in range(TT) for h in range(2) if (h + 1) * JT > i]
    SEQ_D = [(f"{n}{m}", c) for m in range(2) for n, c in MAMBA_D] + [
        ("mem", len(MEM_S)), ("rp", TT // 2), ("score", 3 * TT), ("wo", TT // 2)]
    OFF_A, PER_A = offsets(SEQ_A)
    OFF_D, PER_D = offsets(SEQ_D)
    SETUP_D = 4
    assert PER_A % RING == 0 and PER_D % RING == 0 and all(v % RING == 0 for v in
           (OFF_A["uT1"], OFF_A["oT"], OFF_D["mem"]))

    def job_a(b, stage, j):
        return b * PER_A + (OFF_A[stage] + j)

    def job_d(b, stage, j):
        return b * PER_D + (SETUP_D + OFF_D[stage] + j)

    def bank_a(stage, j):
        return (OFF_A[stage] + j) % RING

    def bank_d(stage, j):
        return (OFF_D[stage] + j) % RING

    END_A, END_D = B * PER_A, SETUP_D + B * PER_D
    FEWEST = 2 * B * T // P
    TILES = FEWEST + 2 * E
    STEPS = B * T // P

    with ExitStack() as ctx:
        def sb(name, shape, dt=F32):
            return ctx.enter_context(nc.sbuf_tensor(name, shape, dt))

        def sem(name):
            return ctx.enter_context(nc.semaphore(name))

        psA = ctx.enter_context(nc.psum_tensor("psA", [P, RING, BANK], F32))
        psD = ctx.enter_context(nc.psum_tensor("psD", [P, RING, BANK], F32))

        x2_dram = nc.dram_tensor("x2_dram", (NT - TT, P, D), F32, kind="Internal").ap()
        xs_dram = nc.dram_tensor("xs_dram", ((TILES + 1) * P, D), F32, kind="Internal").ap()
        ys_dram = nc.dram_tensor("ys_dram", (TILES * P, D), F32, kind="Internal").ap()

        ident = sb("ident", [P, P])
        ones = sb("ones", [P, P])
        in_w_sb = sb("in_w_sb", [P, KD, 2 * DI])
        out_w_sb = sb("out_w_sb", [P, KI, D])
        xp_w_sb = sb("xp_w_sb", [P, KI, R + 2 * NS])
        dt_w_sb = sb("dt_w_sb", [R, DI])
        write_w_sb = sb("write_w_sb", [P, KD, D])
        read_w_sb = sb("read_w_sb", [P, KD, D])
        wq_sb = sb("wq_sb", [P, KD, D])
        wo_sb = sb("wo_sb", [P, KD, D])
        norm_sb = sb("norm_sb", [P, 2, KD])
        in_b_sb = sb("in_b_sb", [P, 2 * KI])
        conv_w_sb = sb("conv_w_sb", [P, KI, TAPS])
        conv_b_sb = sb("conv_b_sb", [P, KI])
        dt_b_sb = sb("dt_b_sb", [P, KI])
        d_sb = sb("d_sb", [P, KI])
        alog_sb = sb("alog_sb", [P, KI, NS])
        negA = sb("negA", [P, KI, NS])
        out_b_sb = sb("out_b_sb", [P, D])
        lng = sb("lng", [P, 8])
        strip = sb("strip", [P, T])
        kT = sb("kT", [P, KD, B, M])
        vdup = sb("vdup", [P, B, D])
        eps_sb = sb("eps_sb", [P, 2])
        headmask = sb("headmask", [P, 8])
        pairmask = sb("pairmask", [P, 2])
        mask_u8 = sb("mask_u8", [1, B, M], U8)
        mask_row = sb("mask_row", [1, B, M], BF16)
        mask_ones = sb("mask_ones", [1, P], BF16)
        ss = sb("ss", [P, TT])
        rt = sb("rt", [P, TT])
        rs = sb("rs", [P, TT])
        stats = sb("stats", [P, TT, 6])
        aggr = sb("aggr", [P, TT, 2])
        bc = sb("bc", [P, TT, 2 * NS])
        bcol = sb("bcol", [P, 2, JT])
        mx = sb("mx", [P, 2, 8])
        rsum = sb("rsum", [P, 2, HEADS])

        WORDS = 41100
        arena = sb("arena", [P, WORDS])
        at = [0]

        def carve(n):
            at[0] += n
            assert at[0] <= WORDS, at
            return arena[:, at[0] - n:at[0]]

        xin = carve(TT * D).rearrange("p (t d) -> p t d", d=D)
        x1 = carve(TT * D).rearrange("p (t d) -> p t d", d=D)
        base = carve(TT * D).rearrange("p (t d) -> p t d", d=D)
        g_flat = carve(2 * JT * DI)
        g = g_flat.rearrange("p (u j d) -> p u j d", u=2, j=JT)
        xn = g_flat[:, 0:TT * D].rearrange("p (t d) -> p t d", d=D)
        rank_sb = g_flat[0:R, 0:T]
        xnT_flat = carve(KD * (T + 1))
        xnT = xnT_flat.rearrange("p (k t) -> p k t", k=KD)
        pre_flat = carve(KI * (T + TAPS - 1))
        pre = pre_flat.rearrange("p (k t) -> p k t", k=KI)
        uT = pre_flat[:, 0:TT * DI].rearrange("p (t d) -> p t d", d=DI)
        sm_flat = carve(2 * KI * T)
        xm = sm_flat[:, 0:KI * T].rearrange("p (k t) -> p k t", k=KI)
        gate = sm_flat[:, KI * T:2 * KI * T].rearrange("p (k t) -> p k t", k=KI)
        dt = carve(KI * T).rearrange("p (k t) -> p k t", k=KI)
        yT_flat = carve(TT * DI)
        yT = yT_flat.rearrange("p (t d) -> p t d", d=DI)
        h_flat = carve(2 * KI * HALF)
        h = h_flat.rearrange("p (u k t) -> p u k t", u=2, k=KI)
        dtu = h_flat.rearrange("p (k t) -> p k t", k=KI)
        da_flat = carve(2 * KI * HALF)
        da = da_flat.rearrange("p (u k t) -> p u k t", u=2, k=KI)
        squares_out = da_flat[:, 0:TT * D].rearrange("p (t d) -> p t d", d=D)
        soft_e = da_flat.rearrange("p (k t) -> p k t", k=KI)
        soft_ln = yT_flat.rearrange("p (k t) -> p k t", k=KI)
        series = dtu
        is_small = g_flat[:, T:T + KI * T // 4].bitcast(U8).rearrange("p (k t) -> p k t", k=KI)
        y = da_flat.rearrange("p (k t) -> p k t", k=KI)
        o2 = x2_out = g_flat[:, 0:TT * D].rearrange("p (t d) -> p t d", d=D)
        oT = xnT
        v_sb = g_flat[:, TT * D:2 * TT * D].rearrange("p (t d) -> p t d", d=D)
        sm_first, sm_words = offsets([((i, hh), (hh + 1) * BANK - max(P * i, hh * BANK)) for i, hh in MEM_S])
        assert sm_words <= 2 * KI * T
        rT = yT_flat[:, 0:KD * T].rearrange("p (k t) -> p k t", k=KD)
        xa = x1
        xaT = yT_flat[:, KD * T:2 * KD * T].rearrange("p (k t) -> p k t", k=KD)
        qT = h_flat[:, 0:KD * T].rearrange("p (k t) -> p k t", k=KD)
        attT = h_flat[:, KD * T:2 * KD * T].rearrange("p (k t) -> p k t", k=KD)
        prob = da_flat.rearrange("p (u n c) -> p u n c", u=4, n=2)
        probT = dt.rearrange("p k t -> p (k t)").rearrange("p (u n c) -> p u n c", u=4, n=2)
        att = pre_flat[:, 0:2 * D].rearrange("p (u d) -> p u d", u=2)
        kblk = pre_flat[:, 1024:1024 + KD * 8 * M].rearrange("p (k h m) -> p k h m", k=KD, h=8)
        vblk = pre_flat[:, 2048:2048 + HEADS * VW].rearrange("p (q r d) -> p q r d", r=2, d=VW)
        at[0] = 0
        x2 = carve(NT * D).rearrange("p (t d) -> p t d", d=D)
        ys = carve(TILES * D).rearrange("p (t d) -> p t d", d=D)
        ys_flat = ys.rearrange("p t d -> p (t d)")
        tile_in = carve(D)
        x2T = ys_flat[:, 0:NT * D].rearrange("p (k t) -> p k t", k=KD)
        picked = ys_flat[:, 0:2 * NT * D].rearrange("p (r t d) -> p r t d", r=2, d=D)
        w1_sb = carve(2 * KD * HID).rearrange("p (u k f) -> p u k f", u=2, k=KD)
        w2_sb = carve(2 * KH * D).rearrange("p (u k f) -> p u k f", u=2, k=KH)
        b1_sb = carve(2 * HID).rearrange("p (u f) -> p u f", u=2)
        b2_sb = carve(2 * D).rearrange("p (u f) -> p u f", u=2)
        hidT = carve(HID).rearrange("p (k t) -> p k t", k=KH)
        tileT = carve(KD * P).rearrange("p (k t) -> p k t", k=KD)
        small = in_w_sb[:, :, :].rearrange("p k f -> p (k f)")
        small2 = out_w_sb[:, :, :].rearrange("p k f -> p (k f)")

        hid, act_hid = small[:, 0:HID], small[:, HID:2 * HID]

        def by_expert(words, n):
            return words[:, n * NT * E:(n + 1) * NT * E].rearrange("p (t e) -> p t e", e=E)

        logit, top, topf, sel1, sel2, sel, cum = (by_expert(small, n) for n in range(7))
        topi = by_expert(small, 7).bitcast(U32)
        place, total, weighed = (by_expert(small2, n) for n in range(3))
        rest = small2[:, 3 * NT * E:4 * NT * E].rearrange("p (k t) -> p k t", k=8)
        over = write_w_sb[:, 0, :].rearrange("p (e j) -> p e j", e=E)
        steps = write_w_sb[:, 1, :].rearrange("p (e j) -> p e j", e=E)
        steps_i = read_w_sb[:, 1, :].bitcast(I32).rearrange("p (e j) -> p e j", e=E)
        count = read_w_sb[:, 0, 0:E]
        ends = read_w_sb[:, 0, E:2 * E]
        firsts = read_w_sb[:, 0, 2 * E:3 * E]
        bound = sb("bound", [P, E + 1], I32)
        slot = sb("slot", [P, 2, NT], U32)
        below = sb("below", [P, P])
        wg_sb = sb("wg_sb", [P, KD, E])
        bg_sb = sb("bg_sb", [P, E])
        expert_id = sb("expert_id", [P, E])
        expert_i = sb("expert_i", [P, E], I32)
        gamma_sb = sb("gamma_sb", [P, D])
        beta_sb = sb("beta_sb", [P, D])
        fstats = sb("fstats", [P, 2, TT, 6])
        faggr = sb("faggr", [P, 2, TT, 2])
        frt = sb("frt", [P, 2, 2, TT])
        zeros = sb("zeros", [P, 4 * D])
        weighed_h = zeros[:, :].rearrange("p (u d) -> p u d", u=2)
        acc = picked[:, 0]
        iota_i = base[:, 0:T // D, :].rearrange("p t d -> p (t d)").bitcast(I32)
        ctx_sb = gate[0:CP, 0, 0:2 * B * 2 * M].rearrange("p (c b m) -> p c b m", c=2, b=B)
        wk_sb = gate[0:CP, 1, 0:2 * D].rearrange("p (c d) -> p c d", c=2)
        wv_sb = gate[0:CP, 2, 0:2 * D].rearrange("p (c d) -> p c d", c=2)

        w_loaded = sem("w_loaded")
        x_loaded = sem("x_loaded")
        act_full, act_drained = sem("act_full"), sem("act_drained")
        dve_full, dve_drained = sem("dve_full"), sem("dve_drained")
        consts_step = sem("consts_step")
        consts_ready = sem("consts_ready")
        dve_setup = sem("dve_setup")
        act_setup = sem("act_setup")
        squares = sem("squares")
        root = sem("root")
        inverse = sem("inverse")
        normed = sem("normed")
        pads_zero = sem("pads_zero")
        tap0_ready = sem("tap0_ready")
        conv_step = sem("conv_step")
        xm_ready = sem("xm_ready")
        soft_abs = sem("soft_abs")
        soft_exp = sem("soft_exp")
        soft_log = sem("soft_log")
        small_found = sem("small_found")
        small_first = sem("small_first")
        slope_ready = sem("slope_ready")
        cubic_step = sem("cubic_step")
        series_step = sem("series_step")
        gate_ready = sem("gate_ready")
        dt_ready = sem("dt_ready")
        dtu_ready = sem("dtu_ready")
        y_zero = sem("y_zero")
        bcol_ready = sem("bcol_ready")
        g_ready = sem("g_ready")
        da_ready = sem("da_ready")
        dbu_full = sem("dbu_full")
        scanned = sem("scanned")
        hT_full = sem("hT_full")
        summed = sem("summed")
        c_weighed = sem("c_weighed")
        c_added = sem("c_added")
        gated = sem("gated")
        xb_ready = sem("xb_ready")
        sum01 = sem("sum01")
        base_ready = sem("base_ready")
        ln_stats = sem("ln_stats")
        ln_done = sem("ln_done")
        blocks_ready = sem("blocks_ready")
        score_max = sem("score_max")
        expo = sem("expo")
        sum_inv = sem("sum_inv")
        route_step = sem("route_step")
        gap_exp = sem("gap_exp")
        routed = sem("routed")
        steps_ready = sem("steps_ready")
        xs_zeroed = sem("xs_zeroed")
        xs_sorted = sem("xs_sorted")
        xs_loaded = sem("xs_loaded")
        w_ready = [sem("w_ready0"), sem("w_ready1")]
        tileT_full = sem("tileT_full")
        tileT_ready = sem("tileT_ready")
        hid_full = sem("hid_full")
        hid_ready = sem("hid_ready")
        gelu_ready = sem("gelu_ready")
        turn_full = sem("turn_full")
        hidT_ready = sem("hidT_ready")
        y_full = sem("y_full")
        y_ready = sem("y_ready")
        y_stored = sem("y_stored")
        picked_in = [sem(f"picked_in{q}") for q in range(B)]
        x2_stored = sem("x2_stored")
        x2_first = sem("x2_first")
        x2_middle = sem("x2_middle")
        eps_ready = sem("eps_ready")
        expert_ready = sem("expert_ready")
        fin_step = sem("fin_step")
        fin_root = sem("fin_root")
        stored = sem("stored")
        waits_passed = sem("waits_passed")

        CONSTS = 10
        UNITS = 2 * NS

        def alone(engine):
            engine.sem_inc(waits_passed, 1)

        def unit(b, m, s, half):
            return b * (2 * UNITS) + s * 2 + (m * UNITS + half)

        order_d = [("score", 0, 0), ("score", 0, 1), ("score", 1, 0), ("score", 1, 1)]
        order_a = []
        for t in range(TT + 2):
            order_d += [("score", t + 2, n) for n in range(2) if t + 2 < TT]
            order_d += [("out", t - 1, 0)] if 1 <= t <= TT else []
            order_a += [("probs", t, n) for n in range(2) if t < TT]
            order_a += [("heads", t - 2, 0)] if t >= 2 else []
        assert len(order_d) == len(order_a) == 3 * TT

        def score_job(t, n):
            return order_d.index(("score", t, n))

        def out_job(t):
            return order_d.index(("out", t, 0))

        def probs_job(t, n):
            return order_a.index(("probs", t, n))

        def heads_job(t):
            return order_a.index(("heads", t, 0))

        GAP_STEP = NT + 1
        SEL_STEP = GAP_STEP + NT + 4
        FIN_NORM = 3 * TT + 1
        FIN_PER = TT + TT + 2 * FIN_NORM + 3

        batch_order = [0, B - 1] + list(range(1, B - 1))
        turn_order = [(k, 2 * q + half) for q in batch_order for half in range(2) for k in range(KD)]
        assert CH == 2 * B and x2_out.offset == x2[:, NT - TT:NT, :].offset

        block = ctx.enter_context(nc.Block())

        loads = [
            (in_w_sb[:, :, :], in_wT.rearrange("(k p) f -> p k f", p=P)),
            (out_w_sb[:, :, :], out_wT.rearrange("(k p) f -> p k f", p=P)),
            (xp_w_sb[:, :, :], xp_wT.rearrange("(k p) f -> p k f", p=P)),
            (dt_w_sb[:, :], dt_wT),
            (write_w_sb[:, :, :], write_wT.rearrange("(k p) f -> p k f", p=P)),
            (read_w_sb[:, :, :], read_wT.rearrange("(k p) f -> p k f", p=P)),
            (wq_sb[:, :, :], Wq.rearrange("(k p) f -> p k f", p=P)),
            (wo_sb[:, :, :], Wo.rearrange("(k p) f -> p k f", p=P)),
            (norm_sb[:, 0, :], norm1_w),
            (norm_sb[:, 1, :], norm2_w),
            (in_b_sb[:, :], in_b),
            (conv_w_sb[:, :, :], conv_w),
            (conv_b_sb[:, :], conv_b),
            (dt_b_sb[:, :], dt_b),
            (d_sb[:, :], D_ssm),
            (alog_sb[:, :, :], A_log),
            (out_b_sb[:, :], out_b.rearrange("(a n) -> a n", a=1).broadcast_to([P, D])),
            (lng[:, 0:1], decay.rearrange("(a n) -> a n", a=1).broadcast_to([P, 1])),
            (mask_u8[:, :, :], ctx_mask.rearrange("(a b) m -> a b m", a=1)),
            (wk_sb[:, :, :], Wk.rearrange("(c p) f -> p c f", p=CP)),
            (wv_sb[:, :, :], Wv.rearrange("(c p) f -> p c f", p=CP)),
            (wg_sb[:, :, :], Wg.rearrange("(k p) f -> p k f", p=P)),
            (bg_sb[:, :], bg.rearrange("(a n) -> a n", a=1).broadcast_to([P, E])),
            (gamma_sb[:, :], gamma.rearrange("(a n) -> a n", a=1).broadcast_to([P, D])),
            (beta_sb[:, :], beta.rearrange("(a n) -> a n", a=1).broadcast_to([P, D])),
        ] + [(ctx_sb[:, :, b, r * M:(r + 1) * M], ctxT[b].rearrange("(c p) m -> p c m", p=CP))
             for b in range(B) for r in range(2)]
        LOADED = 16 * len(loads)
        ZEROED = 16 * (-(-(TILES + 1) // 4) + (TILES - FEWEST) // 4)

        def load_expert(engine, e, r):
            one = bass.ds(e, 1)
            engine.dma_start(w1_sb[:, r, :, :], W1[one].rearrange("a (k p) f -> p (a k) f", p=P)).then_inc(w_ready[r], 16)
            engine.dma_start(w2_sb[:, r, :, :], W2[one].rearrange("a (k p) f -> p (a k) f", p=P)).then_inc(w_ready[r], 16)
            engine.dma_start(b1_sb[:, r, :], b1[one, :].broadcast_to([P, HID])).then_inc(w_ready[r], 16)
            engine.dma_start(b2_sb[:, r, :], b2[one, :].broadcast_to([P, D])).then_inc(w_ready[r], 16)

        def expert_tiles(engine, e):
            return (engine.value_load(bound[0:1, bass.ds(e, 1)], min_val=0, max_val=TILES - 1),
                    engine.value_load(bound[0:1, bass.ds(e + 1, 1)], min_val=2, max_val=TILES))

        @block.sync
        def _(sp):
            sp.sem_inc(x2_stored, 16)
            sp.dma_start(xin, x[0].rearrange("(t p) d -> p t d", p=P)).then_inc(x_loaded, 16)
            for dst, src in loads[0::2]:
                sp.dma_start(dst, src).then_inc(w_loaded, 16)

            def keep_x2(b):
                sp.wait_ge(ln_done, b * (2 * TT) + 2 * TT)
                sp.dma_start(x2_dram[bass.ds(b * TT, TT)].rearrange("t p d -> p t d"), x2_out).then_inc(x2_stored, 16)

            sp.wait_ge(consts_ready, 1)
            rows = xs_dram.rearrange("(p r) d -> p (r d)", p=P)
            for c in range(-(-(TILES + 1) // 4)):
                lo, hi = c * 4 * D, min((c + 1) * 4 * D, (TILES + 1) * D)
                sp.dma_start(rows[:, lo:hi], zeros[:, 0:hi - lo]).then_inc(xs_zeroed, 16)
            rows = ys_dram[FEWEST * P:TILES * P, :].rearrange("(p r) d -> p (r d)", p=P)
            for c in range((TILES - FEWEST) // 4):
                sp.dma_start(rows[:, c * 4 * D:(c + 1) * 4 * D], zeros[:, :]).then_inc(xs_zeroed, 16)
            with sp.Fori(0, B - 1) as b:
                sp.wait_ge(sum01, b + 1)
                sp.dma_start(xin, x[bass.ds(b + 1, 1)].rearrange("a (t p) d -> p (a t) d", p=P))\
                  .then_inc(x_loaded, 16)
                keep_x2(b)
            sp.wait_ge(x2_stored, 16 * B)
            sp.wait_ge(sum01, B)
            sp.dma_start(x2[:, 0:TT, :], x2_dram[0:TT].rearrange("t p d -> p t d")).then_inc(x2_first, 16)
            sp.wait_ge(ln_done, B * 2 * TT)
            sp.dma_start(x2[:, TT:NT - TT, :], x2_dram[TT:NT - TT].rearrange("t p d -> p t d")).then_inc(x2_middle, 16)
            sp.wait_ge(xs_sorted, 16 * 2 * NT)
            sp.wait_ge(routed, 1)
            sp.dma_start(tile_in, xs_dram[0:P, :]).then_inc(xs_loaded, 16)
            tiles = sp.value_load(bound[0:1, E:E + 1], min_val=FEWEST, max_val=TILES)
            with sp.Fori(0, tiles) as i:
                sp.wait_ge(tileT_full, i + 2)
                sp.wait_ge(xs_loaded, i * 16 + 16)
                alone(sp)
                sp.dma_start(tile_in, xs_dram[bass.ds(i * P + P, P), :]).then_inc(xs_loaded, 16)
            out_v = out.rearrange("b (t p) d -> p (b t) d", p=P)
            for q in range(B):
                sp.wait_ge(fin_step, FIN_PER * (q + 1))
                sp.dma_start(out_v[:, q * TT:(q + 1) * TT, :], acc[:, q * TT:(q + 1) * TT, :]).then_inc(stored, 16)
            sp.wait_ge(stored, 16 * B)

        @block.gpsimd
        def _(pool):
            pool.memset(zeros[:, :], 0.0).then_inc(consts_ready, 1)
            pool.memset(ident[:, :], 0.0).then_inc(consts_step, 1)
            pool.memset(ones[:, :], 1.0).then_inc(consts_ready, 1)
            pool.memset(headmask[:, :], 1.0 / float(HD) ** 0.5).then_inc(consts_step, 1)
            pool.memset(pairmask[:, :], 1.0).then_inc(consts_step, 1)
            pool.memset(below[:, :], 1.0).then_inc(consts_step, 1)
            pool.iota(iota_i, pattern=[[1, T]], base=-1, channel_multiplier=-1).then_inc(consts_ready, 1)
            pool.iota(expert_i[:, :], pattern=[[1, E]], base=0, channel_multiplier=0).then_inc(consts_ready, 1)
            pool.wait_ge(consts_step, 4)
            pool.affine_select(out=below[:, :], in_=below[:, :], compare_op=ALU.is_ge, fill=0.0, base=-1,
                               pattern=[[1, P]], channel_multiplier=-1).then_inc(consts_ready, 1)
            pool.affine_select(out=ident[:, :], in_=ident[:, :], compare_op=ALU.not_equal, fill=1.0, base=0,
                               pattern=[[-1, P]], channel_multiplier=1).then_inc(consts_ready, 1)
            pool.affine_select(out=headmask[:, :], in_=headmask[:, :], compare_op=ALU.is_ge, fill=0.0, base=0,
                               pattern=[[-HD, 8]], channel_multiplier=1).then_inc(consts_step, 1)
            pool.wait_ge(consts_step, 5)
            pool.affine_select(out=headmask[:, :], in_=headmask[:, :], compare_op=ALU.is_ge, fill=0.0, base=HD - 1,
                               pattern=[[HD, 8]], channel_multiplier=-1).then_inc(consts_ready, 1)
            pool.affine_select(out=pairmask[:, 0:1], in_=pairmask[:, 0:1], compare_op=ALU.is_ge, fill=0.0,
                               base=M - 1, pattern=[[0, 1]], channel_multiplier=-1).then_inc(consts_ready, 1)
            pool.affine_select(out=pairmask[:, 1:2], in_=pairmask[:, 1:2], compare_op=ALU.is_ge, fill=0.0,
                               base=-M, pattern=[[0, 1]], channel_multiplier=1).then_inc(consts_ready, 1)
            pool.wait_ge(act_setup, 5)
            pool.affine_select(out=strip[:, :], in_=strip[:, :], compare_op=ALU.is_ge, fill=0.0, base=-1,
                               pattern=[[1, T]], channel_multiplier=-1).then_inc(consts_ready, 1)
            pool.sem_inc(g_ready, JT + 1)
            pool.sem_inc(c_added, 2)
            with pool.Fori(0, B) as b:
                for m in range(2):
                    if m == 0:
                        pool.wait_ge(x2_stored, b * 16 + 16)
                        pool.wait_ge(x_loaded, b * 16 + 16)
                        pool.wait_ge(w_loaded, LOADED)
                        pool.tensor_tensor(base[:, :, :], xin[:, :, :],
                                           out_b_sb[:, :].unsqueeze(1).broadcast_to([P, TT, D]), ALU.add)\
                            .then_inc(xb_ready, 1)
                        pool.wait_ge(xb_ready, b + 1)
                    else:
                        pool.wait_ge(dve_drained, job_d(b, "mo0", TT // 2) + RING)
                        pool.tensor_tensor(base[:, :, :], xin[:, :, :], x1[:, :, :], ALU.add).then_inc(sum01, 1)
                    blk = b * 2 + m
                    for f in range(KI):
                        if f >= 2:
                            pool.wait_ge(soft_exp, blk * KI + f + 1)
                            alone(pool)
                            pool.tensor_scalar(is_small[:, f, :], soft_e[:, f, :], SMALL_E, None, ALU.is_lt)\
                                .then_inc(small_found, 1)
                        pool.wait_ge(slope_ready, blk * KI + f + 1)
                        alone(pool)
                        pool.tensor_tensor(series[:, f, :], series[:, f, :], soft_e[:, f, :], ALU.mult)\
                            .then_inc(cubic_step, 1)
                    pool.wait_ge(y_zero, blk + 1)
                    alone(pool)

                    def scale_b(s, half):
                        u = unit(b, m, s, half)
                        pool.wait_ge(bcol_ready, u + 1)
                        pool.wait_ge(dbu_full, u * KI + 1)
                        alone(pool)
                        for j in range(JT):
                            pool.tensor_scalar(g[:, half, j, :], uT[:, half * JT + j, :], bcol[:, half, j:j + 1],
                                               1.0, ALU.mult, ALU.mult).then_inc(g_ready, 1)

                    def add_last(s, half):
                        u = unit(b, m, s, half)
                        t = half * JT + JS
                        pool.wait_ge(c_weighed, u + 2)
                        pool.wait_ge(c_added, u + 1)
                        alone(pool)
                        pool.tensor_tensor(yT[:, t, :], yT[:, t, :], weighed_h[:, half, :], ALU.add)\
                            .then_inc(c_added, 1)

                    for half in range(2):
                        pool.wait_ge(act_drained, job_a(b, f"uT{m}", 2 * KI - 1 + half) + RING)
                        scale_b(0, half)
                    with pool.Fori(0, NS - 1) as s:
                        for half in range(2):
                            scale_b(s + 1, half)
                            add_last(s, half)
                    for half in range(2):
                        add_last(NS - 1, half)
                pool.wait_ge(dve_drained, job_d(b, "mo1", TT // 2) + RING)
                pool.wait_ge(sum01, b + 1)
                pool.tensor_tensor(base[:, :, :], base[:, :, :], o2[:, :, :], ALU.add).then_inc(base_ready, 1)
                pool.wait_ge(base_ready, b * 2 + 1)
                alone(pool)
                pool.tensor_scalar(base[:, :, :], base[:, :, :], SHRINK, 1.0, ALU.mult, ALU.mult).then_inc(base_ready, 1)

            pool.wait_ge(xs_zeroed, ZEROED)
            pool.wait_ge(ln_done, B * 2 * TT)
            pool.iota(steps_i, pattern=[[0, E], [P, STEPS]], base=0, channel_multiplier=0).then_inc(steps_ready, 1)
            for e in range(2):
                load_expert(pool, e, e)
            pool.wait_ge(x2_first, 16)
            pool.wait_ge(x2_middle, 16)
            pool.wait_ge(routed, 1)
            for r in range(2):
                for t in range(NT):
                    pool.indirect_dma_start(xs_dram, bass.IndirectOffsetOnAxis(slot[:, r, t:t + 1], 0), x2[:, t, :], None)\
                        .then_inc(xs_sorted, 16)

            def keep_results(e):
                first, end = expert_tiles(pool, e)
                with pool.Fori(first, end) as i:
                    pool.wait_ge(y_ready, i + 2)
                    alone(pool)
                    pool.dma_start(ys_dram[bass.ds(i * P, P), :], ys[:, bass.ds(i, 1), :].rearrange("p o d -> p (o d)"))\
                        .then_inc(y_stored, 16)
                return end

            with pool.Fori(0, E // 2 - 1) as pair:
                for r in range(2):
                    end = keep_results(pair * 2 + r)
                    pool.wait_ge(y_ready, end + 1)
                    alone(pool)
                    load_expert(pool, pair * 2 + (r + 2), r)
            for e in range(E - 2, E):
                tiles = keep_results(e)
            pool.wait_ge(y_stored, tiles * 16)
            alone(pool)
            for t in range(NT):
                for r in range(2):
                    pool.indirect_dma_start(picked[:, r, t, :], None, ys_dram, bass.IndirectOffsetOnAxis(slot[:, r, t:t + 1], 0))\
                        .then_inc(picked_in[t // TT], 16)

        @block.scalar
        def _(act):
            for dst, src in loads[1::2]:
                act.dma_start(dst, src).then_inc(w_loaded, 16)
            act.sem_inc(act_drained, RING)
            act.wait_ge(eps_ready, 2)
            act.wait_ge(w_loaded, LOADED)
            act.activation(lng[:, 1:2], lng[:, 0:1], ACT.Abs).then_inc(act_setup, 1)
            act.activation(alog_sb[:, :, :], alog_sb[:, :, :], ACT.Exp).then_inc(act_setup, 1)
            act.wait_ge(act_setup, 2)
            act.activation(lng[:, 2:3], lng[:, 1:2], ACT.Exp, scale=-1.0).then_inc(act_setup, 1)
            act.wait_ge(act_setup, 3)
            act.activation(lng[:, 3:4], lng[:, 2:3], ACT.Ln, bias=1.0).then_inc(act_setup, 1)
            act.wait_ge(dve_setup, 4)
            act.activation(strip[:, :], strip[:, :], ACT.Exp, scale=lng[:, 5:6]).then_inc(act_setup, 1)

            def drain(job, bank, dst, width=BANK, func=ACT.Copy, **kw):
                act.wait_ge(act_full, job + 1)
                act.activation(dst, psA[:, bank, 0:width], func, **kw).then_inc(act_drained, 1)

            def turned(b, stage, dst, scale=None, shift=0, halves_first=True):
                for j in range(2 * KD):
                    k, half = (j % KD, j // KD) if halves_first else (j // 2, j % 2)
                    kw = {} if scale is None else {"scale": scale[:, k:k + 1]}
                    drain(job_a(b, stage, j), bank_a(stage, j),
                          dst[:, k, shift + half * HALF:shift + (half + 1) * HALF], **kw)

            def root_of(dst, src, scale, ready, eps=0):
                act.wait_ge(*ready)
                act.activation(dst, src, ACT.Sqrt, scale=scale, bias=eps_sb[:, eps:eps + 1]).then_inc(root, 1)

            def mamba(b, m):
                blk = b * 2 + m
                src, unused = (xin, squares_out) if m == 0 else (x1, xn)
                if m == 0:
                    act.wait_ge(x_loaded, b * 16 + 16)
                for t in range(TT):
                    if m == 1 and t % 2 == 0:
                        act.wait_ge(dve_drained, job_d(b, "mo0", t // 2) + 1 + RING)
                    act.activation(unused[:, t, :], src[:, t, :], ACT.Square, accum_out=ss[:, t:t + 1]).then_inc(squares, 1)
                if m == 0:
                    act.wait_ge(inverse, b * 5 + 1)
                root_of(rt[:, :], ss[:, :], 1.0 / D, (squares, blk * TT + TT))
                turned(b, f"xnT{m}", xnT, norm_sb[:, m, :])
                act.wait_ge(pads_zero, blk + 1)

                def drain_in(stage, j, n):
                    f, half = n // 2, n % 2
                    dst = (pre[:, f, TAPS - 1 + half * HALF:TAPS - 1 + (half + 1) * HALF] if f < KI
                           else gate[:, f - KI, half * HALF:(half + 1) * HALF])
                    drain(job_a(b, stage, j), bank_a(stage, j), dst, func=ACT.Identity, bias=in_b_sb[:, f:f + 1])

                def silu_conv(f):
                    act.wait_ge(conv_step, blk * ((TAPS - 1) * KI) + (TAPS - 1) * (f + 1))
                    act.activation(xm[:, f, :], xm[:, f, :], ACT.Silu).then_inc(xm_ready, 1)

                for f in range(KI):
                    for half in range(2):
                        drain_in(f"in{m}", 2 * f + half, 2 * f + half)
                    act.wait_ge(act_drained, job_a(b, f"in{m}", 2 * f + 1) + 1 + RING)
                    act.activation(xm[:, f, :], pre[:, f, 0:T], ACT.Identity, scale=conv_w_sb[:, f, 0:1],
                                   bias=conv_b_sb[:, f:f + 1]).then_inc(tap0_ready, 1)
                    if f >= 1:
                        silu_conv(f - 1)
                for j in range(2 * KI, 2 * KI + EARLY):
                    drain_in(f"in{m}", j, j)
                    if j == 2 * KI + 1:
                        silu_conv(KI - 1)
                for j in range(2):
                    act.wait_ge(act_full, job_a(b, f"rank{m}", j) + 1)
                    act.activation(rank_sb[:, j * HALF:(j + 1) * HALF], psA[0:R, bank_a(f"rank{m}", j), :], ACT.Copy)\
                       .then_inc(act_drained, 1)

                def absolute(f):
                    act.wait_ge(dve_drained, job_d(b, f"z{m}", 2 * f + 1) + 1 + RING)
                    act.activation(soft_e[:, f, :], dt[:, f, :], ACT.Abs).then_inc(soft_abs, 1)

                def slope(f):
                    act.wait_ge(soft_exp, blk * KI + f + 1)
                    act.activation(series[:, f, :], soft_e[:, f, :], ACT.Copy, scale=1.0 / 3.0, bias=-0.5)\
                       .then_inc(slope_ready, 1)

                absolute(0)
                for f in range(KI):
                    if f + 1 < KI:
                        absolute(f + 1)
                    act.wait_ge(soft_abs, blk * KI + f + 1)
                    act.activation(soft_e[:, f, :], soft_e[:, f, :], ACT.Exp, scale=-1.0).then_inc(soft_exp, 1)
                    if 1 <= f <= 2:
                        slope(f - 1)
                for f in range(KI):
                    act.wait_ge(soft_exp, blk * KI + f + 1)
                    act.activation(soft_ln[:, f, :], soft_e[:, f, :], ACT.Ln, bias=1.0).then_inc(soft_log, 1)
                    if f + 2 < KI:
                        slope(f + 2)
                for j in range(2):
                    act.wait_ge(act_full, job_a(b, f"bc{m}", j) + 1)
                    act.activation(bc[:, j * JT:(j + 1) * JT, :], psA[:, bank_a(f"bc{m}", j), 0:JT * 2 * NS]
                                   .rearrange("p (t c) -> p t c", t=JT), ACT.Copy).then_inc(act_drained, 1)
                for j in range(2 * KI - EARLY):
                    drain_in(f"late{m}", j, 2 * KI + EARLY + j)
                def column(s, half):
                    act.wait_ge(g_ready, unit(b, m, s, half) * JT + 1)
                    act.activation(bcol[:, half, :], bc[:, half * JT:(half + 1) * JT, bass.ds(s, 1)]
                                   .rearrange("p t o -> p (t o)"), ACT.Copy).then_inc(bcol_ready, 1)

                def decays(s, half):
                    act.wait_ge(scanned, unit(b, m, s, half) * KI + 1)
                    alone(act)
                    for f in range(KI):
                        act.activation(da[:, half, f, :], dt[:, f, half * HALF:(half + 1) * HALF], ACT.Exp,
                                       scale=negA[:, f, bass.ds(s, 1)]).then_inc(da_ready, 1)

                def weigh_last(s, half):
                    u = unit(b, m, s, half)
                    act.wait_ge(hT_full, u * JT + (2 * JT + 1))
                    act.wait_ge(c_added, u + 1)
                    alone(act)
                    act.activation(weighed_h[:, half, :], psA[:, JS, :], ACT.Copy,
                                   scale=bc[:, half * JT + JS, bass.ds(s + NS, 1)]).then_inc(c_weighed, 1)

                def drain_u(f):
                    for half in range(2):
                        j = 2 * f + half
                        act.wait_ge(act_full, job_a(b, f"uT{m}", j) + 1)
                        act.activation(uT[:, half * JT:(half + 1) * JT, f * P:(f + 1) * P],
                                       psA[:, bank_a(f"uT{m}", j), :].rearrange("p (t c) -> p t c", t=JT), ACT.Copy)\
                           .then_inc(act_drained, 1)

                act.wait_ge(act_drained, job_a(b, f"late{m}", 2 * KI - EARLY) + RING)
                for f in range(KI - 1):
                    drain_u(f)
                act.wait_ge(dt_ready, blk * KI + KI)
                column(0, 0)
                drain_u(KI - 1)
                decays(0, 0)
                column(0, 1)
                decays(0, 1)
                act.wait_ge(xs_zeroed, ZEROED)
                with act.Fori(0, NS - 1) as s:
                    for half in range(2):
                        column(s + 1, half)
                        decays(s + 1, half)
                        weigh_last(s, half)
                for half in range(2):
                    weigh_last(NS - 1, half)
                act.wait_ge(act_drained, job_a(b, f"late{m}", 2 * KI - EARLY) + RING)
                for f in range(KI):
                    act.activation(gate[:, f, :], gate[:, f, :], ACT.Silu).then_inc(gate_ready, 1)

            act.sem_inc(c_weighed, 1)
            with act.Fori(0, B) as b:
                for m in range(2):
                    mamba(b, m)
                turned(b, "oT", oT, shift=1)
                for j in range(TT // 2):
                    drain(job_a(b, "v", j), bank_a("v", j), v_sb[:, 2 * j:2 * j + 2, :].rearrange("p t d -> p (t d)"))
                turned(b, "rT", rT, halves_first=False)
                root_of(rt[:, :], aggr[:, :, 1], 1.0, (ln_stats, b * (4 * TT) + 2 * TT), 1)
                turned(b, "xaT", xaT)
                turned(b, "qT", qT, halves_first=False)

                def exps(t):
                    for n in range(2):
                        act.wait_ge(dve_drained, job_d(b, "score", score_job(t, n)) + 1 + RING)
                        act.activation(prob[:, t % 4, n, :], prob[:, t % 4, n, :], ACT.Exp).then_inc(expo, 1)

                exps(0)
                exps(1)
                for t in range(TT + 2):
                    if t < TT:
                        for n in range(2):
                            j = probs_job(t, n)
                            drain(job_a(b, "probs", j), bank_a("probs", j), probT[:, t % 4, n, :])
                    if t + 2 < TT:
                        exps(t + 2)
                    if t >= 2:
                        j = heads_job(t - 2)
                        act.wait_ge(act_full, job_a(b, "probs", j) + 1)
                        act.activation(attT[:, :, (t - 2) * P:(t - 1) * P], psA[:, bank_a("probs", j), 0:KD * P]
                                       .rearrange("p (k t) -> p k t", k=KD), ACT.Copy).then_inc(act_drained, 1)
                root_of(rt[:, :], aggr[:, :, 1], 1.0, (ln_stats, b * (4 * TT) + 4 * TT))

            for j, (k, c) in enumerate(turn_order):
                drain(END_A + j, j % RING, x2T[:, k, c * BANK:(c + 1) * BANK])
            act.wait_ge(route_step, GAP_STEP)
            act.activation(rest[:, 1, :], rest[:, 0, :], ACT.Exp).then_inc(gap_exp, 1)
            act.sem_inc(tileT_ready, 1)

            def tile_turned(i):
                act.wait_ge(tileT_full, i + 2)
                act.activation(tileT, psA[:, 0, 0:KD * P].rearrange("p (k t) -> p k t", k=KD), ACT.Copy)\
                   .then_inc(tileT_ready, 1)

            def gelu(i, d=0):
                for n in range(2):
                    act.wait_ge(turn_full, i * 2 + (2 * d + n + 1))
                    act.wait_ge(hid_ready, i * 2 + (2 * d + n + 3))
                    act.activation(act_hid[:, n * BANK:(n + 1) * BANK], hid[:, n * BANK:(n + 1) * BANK], ACT.Gelu)\
                       .then_inc(gelu_ready, 1)

            act.sem_inc(gelu_ready, 2)
            tile_turned(0)
            act.wait_ge(routed, 1)
            with act.Fori(0, E // 2) as pair:
                for r in range(2):
                    first, end = expert_tiles(act, pair * 2 + r)
                    gelu(first)
                    tile_turned(first + 1)
                    with act.Fori(first, end - 1) as i:
                        gelu(i, 1)
                        tile_turned(i + 2)
            for q in range(B):
                for r in range(2):
                    act.wait_ge(fin_step, FIN_PER * q + 2 * TT + r * (FIN_NORM + 3) + 2 * TT)
                    act.activation(frt[:, q % 2, r, :], faggr[:, q % 2, :, 1], ACT.Sqrt, bias=eps_sb[:, 0:1])\
                       .then_inc(fin_root, 1)

        @block.tensor
        def _(pe):
            def claim_a(job):
                pe.wait_ge(act_drained, job + 1)

            def claim_d(job):
                pe.wait_ge(dve_drained, job + 1)

            def turn(b, stage, src, ready=None, first=0):
                for j in range(2 * KD):
                    k, half = j % KD, j // KD
                    if ready is not None and k == 0:
                        pe.wait_ge(ready, first + (half + 1) * JT)
                    claim_a(job_a(b, stage, j))
                    for t in range(JT):
                        mm = pe.transpose(psA[:, bank_a(stage, j), t * P:(t + 1) * P],
                                          src[:, half * JT + t, k * P:(k + 1) * P], ident[:, :])
                    mm.then_inc(act_full, 1)

            def product(out_ap, pairs):
                for i, (lhs, rhs) in enumerate(pairs):
                    mm = pe.matmul(out_ap, lhs, rhs, start=i == 0, stop=i == len(pairs) - 1)
                return mm

            def token_rows(bank, ps, t0, lhs, rhs, tiles):
                for r in range(2):
                    mm = product(ps[:, bank, r * D:(r + 1) * D],
                                 [(lhs[:, k, (t0 + r) * P:(t0 + r + 1) * P], rhs[:, k, :]) for k in range(tiles)])
                return mm

            pe.wait_ge(w_loaded, LOADED)
            pe.wait_ge(consts_ready, CONSTS)
            for m in range(KD):
                claim_d(m)
                product(psD[:, m, 0:B * M].rearrange("p (b m) -> p b m", b=B),
                        [(wk_sb[:, c, m * P:(m + 1) * P], ctx_sb[:, c, :, 0:M]) for c in range(2)])\
                    .then_inc(dve_full, 1)
            for j in range(B // 2):
                claim_d(KD + j)
                for r in range(2):
                    mm = product(psD[:, KD + j, r * D:(r + 1) * D],
                                 [(ctx_sb[:, c, 2 * j + r, :], wv_sb[:, c, :]) for c in range(2)])
                mm.then_inc(dve_full, 1)

            def mamba(b, m):
                blk = b * 2 + m
                turn(b, f"xnT{m}", xn, normed, blk * TT)

                def project_in(stage, j, n):
                    f, half = n // 2, n % 2
                    if n < 2:
                        pe.wait_ge(act_drained, job_a(b, f"xnT{m}", (half + 1) * KD) + RING)
                    claim_a(job_a(b, stage, j))
                    product(psA[:, bank_a(stage, j), :],
                            [(in_w_sb[:, k, f * P:(f + 1) * P], xnT[:, k, half * HALF:(half + 1) * HALF])
                             for k in range(KD)]).then_inc(act_full, 1)

                for j in range(2 * KI + EARLY):
                    project_in(f"in{m}", j, j)
                for j in range(2):
                    claim_a(job_a(b, f"rank{m}", j))
                    for k in range(KI):
                        if j == 0:
                            pe.wait_ge(xm_ready, blk * KI + k + 1)
                        mm = pe.matmul(psA[0:R, bank_a(f"rank{m}", j), :], xp_w_sb[:, k, 0:R],
                                       xm[:, k, j * HALF:(j + 1) * HALF], start=k == 0, stop=k == KI - 1)
                    mm.then_inc(act_full, 1)
                for j in range(2 * KI):
                    f, half = j // 2, j % 2
                    pe.wait_ge(act_drained, job_a(b, f"rank{m}", half) + 1 + RING)
                    claim_d(job_d(b, f"z{m}", j))
                    pe.matmul(psD[:, bank_d(f"z{m}", j), :], dt_w_sb[:, f * P:(f + 1) * P],
                              rank_sb[:, half * HALF:(half + 1) * HALF], start=True, stop=True).then_inc(dve_full, 1)
                for j in range(2):
                    claim_a(job_a(b, f"bc{m}", j))
                    for t in range(JT):
                        mm = product(psA[:, bank_a(f"bc{m}", j), t * 2 * NS:(t + 1) * 2 * NS],
                                     [(xm[:, k, (j * JT + t) * P:(j * JT + t + 1) * P], xp_w_sb[:, k, R:R + 2 * NS])
                                      for k in range(KI)])
                    mm.then_inc(act_full, 1)
                for j in range(2 * KI - EARLY):
                    project_in(f"late{m}", j, 2 * KI + EARLY + j)
                for j in range(2 * KI):
                    f, half = j // 2, j % 2
                    pe.wait_ge(dtu_ready, blk * KI + f + 1)
                    claim_a(job_a(b, f"uT{m}", j))
                    for t in range(JT):
                        mm = pe.transpose(psA[:, bank_a(f"uT{m}", j), t * P:(t + 1) * P],
                                          dtu[:, f, (half * JT + t) * P:(half * JT + t + 1) * P], ident[:, :])
                    mm.then_inc(act_full, 1)
                pe.wait_ge(dve_drained, job_d(b, f"z{m}", 2 * KI) + RING)

                def inputs(s, half):
                    u = unit(b, m, s, half)
                    pe.wait_ge(g_ready, u * JT + (2 * JT + 1))
                    for f in range(KI):
                        pe.wait_ge(scanned, u * KI + (f + 2))
                        for j in range(JT):
                            mm = pe.transpose(psD[:, f, j * P:(j + 1) * P], g[:, half, j, f * P:(f + 1) * P], ident[:, :])
                        mm.then_inc(dbu_full, 1)

                def states(s, half):
                    u = unit(b, m, s, half)
                    pe.wait_ge(scanned, u * KI + (2 * KI + 1))
                    for j in range(JT):
                        if j < JS:
                            pe.wait_ge(summed, u * JS + (j + 2))
                        else:
                            pe.wait_ge(c_weighed, u + 1)
                        for f in range(KI):
                            mm = pe.transpose(psA[:, j, f * P:(f + 1) * P], h[:, half, f, j * P:(j + 1) * P], ident[:, :])
                        mm.then_inc(hT_full, 1)

                inputs(0, 0)
                pe.wait_ge(act_drained, job_a(b, f"uT{m}", 2 * KI) + RING)
                alone(pe)
                with pe.Fori(0, NS - 1) as s:
                    inputs(s, 1)
                    states(s, 0)
                    inputs(s + 1, 0)
                    states(s, 1)
                inputs(NS - 1, 1)
                states(NS - 1, 0)
                states(NS - 1, 1)

                pe.wait_ge(scanned, unit(b, m, NS - 1, 1) * KI + (2 * KI + 1))
                for half in range(2):
                    last = unit(b, m, NS - 1, half)
                    pe.wait_ge(summed, last * JS + (2 * JS + 1))
                    pe.wait_ge(c_added, last + 3)
                    for f in range(KI):
                        j = half * KI + f
                        claim_d(job_d(b, f"y{m}", j))
                        for t in range(JT):
                            mm = pe.transpose(psD[:, bank_d(f"y{m}", j), t * P:(t + 1) * P],
                                              yT[:, half * JT + t, f * P:(f + 1) * P], ident[:, :])
                        mm.then_inc(dve_full, 1)
                for j in range(TT // 2):
                    pe.wait_ge(gated, blk * (2 * KI) + (KI if j < TT // 4 else 2 * KI))
                    claim_d(job_d(b, f"mo{m}", j))
                    token_rows(bank_d(f"mo{m}", j), psD, 2 * j, y, out_w_sb, KI).then_inc(dve_full, 1)

            pe.sem_inc(hT_full, JT + 1)
            pe.sem_inc(dbu_full, KI + 1)
            with pe.Fori(0, B) as b:
                for m in range(2):
                    mamba(b, m)
                pe.wait_ge(dve_drained, job_d(b, "mo1", TT // 2) + RING)
                turn(b, "oT", o2)
                pe.wait_ge(act_drained, job_a(b, "oT", 2 * KD) + RING)
                pe.wait_ge(blocks_ready, b * 3 + 1)
                for j in range(TT // 2):
                    claim_a(job_a(b, "v", j))
                    token_rows(bank_a("v", j), psA, 2 * j, oT[:, :, 1:T + 1], write_w_sb, KD).then_inc(act_full, 1)
                for j, (i, half) in enumerate(MEM_S):
                    lo, hi = max(P * i, half * HALF), (half + 1) * HALF
                    claim_d(job_d(b, "mem", j))
                    product(psD[:, bank_d("mem", j), 0:hi - lo],
                            [(oT[:, k, P * i:P * i + P], oT[:, k, 1 + lo:1 + hi]) for k in range(KD)]).then_inc(dve_full, 1)
                pe.wait_ge(act_drained, job_a(b, "v", TT // 2) + RING)
                pe.wait_ge(dve_drained, job_d(b, "mem", len(MEM_S)) + RING)
                for j in range(2 * KD):
                    k, half = j // 2, j % 2
                    claim_a(job_a(b, "rT", j))
                    tiles = [i for i in range(TT) if (i, half) in MEM_S]
                    for i in tiles:
                        lo, hi = max(P * i, half * HALF), (half + 1) * HALF
                        at0 = sm_first[(i, half)]
                        mm = pe.matmul(psA[:, bank_a("rT", j), lo - half * HALF:HALF], v_sb[:, i, k * P:(k + 1) * P],
                                       sm_flat[:, at0:at0 + hi - lo], start=i == 0, stop=i == tiles[-1])
                    mm.then_inc(act_full, 1)
                pe.wait_ge(act_drained, job_a(b, "rT", 2 * KD) + RING)
                for j in range(TT // 2):
                    claim_d(job_d(b, "rp", j))
                    token_rows(bank_d("rp", j), psD, 2 * j, rT, read_w_sb, KD).then_inc(dve_full, 1)

                turn(b, "xaT", xa, ln_done, b * (2 * TT))
                for j in range(2 * KD):
                    f, half = j // 2, j % 2
                    if f == 0:
                        pe.wait_ge(act_drained, job_a(b, "xaT", (half + 1) * KD) + RING)
                    claim_a(job_a(b, "qT", j))
                    product(psA[:, bank_a("qT", j), :], [(wq_sb[:, k, f * P:(f + 1) * P],
                            xaT[:, k, half * HALF:(half + 1) * HALF]) for k in range(KD)]).then_inc(act_full, 1)
                pe.wait_ge(act_drained, job_a(b, "qT", 2 * KD) + RING)
                pe.wait_ge(blocks_ready, b * 3 + 3)

                def scores(t):
                    for n in range(2):
                        j = score_job(t, n)
                        claim_d(job_d(b, "score", j))
                        bank = psD[:, bank_d("score", j), :]
                        pe.matmul(bank, qT[:, n, t * P:(t + 1) * P], kblk[:, n, :, :].rearrange("p h m -> p (h m)"),
                                  start=True, stop=False)
                        pe.matmul(bank.rearrange("p (h m) -> p h m", h=8), mask_ones[:, :], mask_row[0:1, bass.ds(b, 1), :].broadcast_to([1, 8, M]),
                                  start=False, stop=True).then_inc(dve_full, 1)

                def turn_probs(t):
                    for n in range(2):
                        j = probs_job(t, n)
                        pe.wait_ge(expo, b * (2 * TT) + (2 * t + n + 1))
                        claim_a(job_a(b, "probs", j))
                        for q in range(4):
                            mm = pe.transpose(psA[:, bank_a("probs", j), q * P:(q + 1) * P],
                                              prob[:, t % 4, n, q * P:(q + 1) * P], ident[:, :])
                        mm.then_inc(act_full, 1)

                def weigh(t):
                    j = out_job(t)
                    claim_d(job_d(b, "score", j))
                    pe.wait_ge(act_drained, job_a(b, "probs", probs_job(t, 1)) + 1 + RING)
                    for q in range(HEADS // 2):
                        mm = pe.matmul(psD[:, bank_d("score", j), q * 2 * VW:(q + 1) * 2 * VW],
                                       probT[:, t % 4, q // 4, (q % 4) * P:(q % 4 + 1) * P],
                                       vblk[:, q, :, :].rearrange("p h d -> p (h d)"), start=True, stop=True)
                    mm.then_inc(dve_full, 1)

                def turn_heads(t):
                    j = heads_job(t)
                    pe.wait_ge(dve_drained, job_d(b, "score", out_job(t)) + 1 + RING)
                    claim_a(job_a(b, "probs", j))
                    for k in range(KD):
                        mm = pe.transpose(psA[:, bank_a("probs", j), k * P:(k + 1) * P],
                                          att[:, t % 2, k * P:(k + 1) * P], ident[:, :])
                    mm.then_inc(act_full, 1)

                scores(0)
                scores(1)
                for t in range(TT + 2):
                    if t + 2 < TT:
                        scores(t + 2)
                    if t < TT:
                        turn_probs(t)
                    if 1 <= t <= TT:
                        weigh(t - 1)
                    if t >= 2:
                        turn_heads(t - 2)
                pe.wait_ge(act_drained, job_a(b, "probs", 3 * TT) + RING)
                for j in range(TT // 2):
                    claim_d(job_d(b, "wo", j))
                    token_rows(bank_d("wo", j), psD, 2 * j, attT, wo_sb, KD).then_inc(dve_full, 1)

            def turn_x2(q):
                for j, (k, c) in enumerate(turn_order):
                    if c // 2 == q:
                        claim_a(END_A + j)
                        for t in range(4):
                            mm = pe.transpose(psA[:, j % RING, t * P:(t + 1) * P],
                                              x2[:, 4 * c + t, k * P:(k + 1) * P], ident[:, :])
                        mm.then_inc(act_full, 1)

            def logits(q):
                j = batch_order.index(q)
                claim_d(END_D + j)
                pe.wait_ge(act_drained, END_A + 2 * KD * (j + 1) + RING)
                for t in range(TT):
                    mm = product(psD[:, (END_D + j) % RING, t * E:(t + 1) * E],
                                 [(x2T[:, k, (TT * q + t) * P:(TT * q + t + 1) * P], wg_sb[:, k, :])
                                  for k in range(KD)])
                mm.then_inc(dve_full, 1)

            pe.wait_ge(ln_done, B * 2 * TT)
            pe.wait_ge(x2_first, 16)
            turn_x2(0)
            turn_x2(B - 1)
            logits(0)
            logits(B - 1)
            pe.wait_ge(x2_middle, 16)
            for q in range(1, B - 1):
                turn_x2(q)
            for q in range(1, B - 1):
                logits(q)
            pe.wait_ge(route_step, SEL_STEP)
            for j, lhs in enumerate((below, ones)):
                claim_d(END_D + 4 + j)
                pe.matmul(psD[:, (END_D + 4 + j) % RING, 0:NT * E], lhs[:, :], sel.rearrange("p t e -> p (t e)"),
                          start=True, stop=True).then_inc(dve_full, 1)

            def turn_tile(i):
                pe.wait_ge(xs_loaded, i * 16 + 16)
                pe.wait_ge(tileT_ready, i + 1)
                for k in range(KD):
                    mm = pe.transpose(psA[:, 0, k * P:(k + 1) * P],
                                      tile_in[:, k * P:(k + 1) * P], ident[:, :])
                mm.then_inc(tileT_full, 1)

            def first_product(i, r, n, d=0):
                if n == 0:
                    pe.wait_ge(tileT_ready, i + (d + 2))
                pe.wait_ge(hid_ready, i * 2 + (2 * d + n + 1))
                product(psD[:, n, :], [(tileT[:, k, :], w1_sb[:, r, k, n * BANK:(n + 1) * BANK])
                                       for k in range(KD)]).then_inc(hid_full, 1)

            def turn_hidden(i, d=0):
                for n in range(2):
                    pe.wait_ge(gelu_ready, i * 2 + (2 * d + n + 3))
                    pe.wait_ge(hidT_ready, i * 2 + (2 * d + n + 3))
                    for k in range(4):
                        mm = pe.transpose(psA[:, 1 + n, k * P:(k + 1) * P],
                                          act_hid[:, (4 * n + k) * P:(4 * n + k + 1) * P], ident[:, :])
                    mm.then_inc(turn_full, 1)

            def second_product(i, r, d=0):
                pe.wait_ge(y_ready, i + (d + 1))
                for n in range(2):
                    pe.wait_ge(hidT_ready, i * 2 + (2 * d + n + 5))
                    for k in range(4 * n, 4 * n + 4):
                        mm = pe.matmul(psD[:, 2, 0:D], hidT[:, k, :], w2_sb[:, r, k, :],
                                       start=k == 0, stop=k == KH - 1)
                mm.then_inc(y_full, 1)

            pe.sem_inc(tileT_full, 1)
            pe.sem_inc(turn_full, 2)
            pe.wait_ge(dve_drained, END_D + 6 + RING)
            pe.wait_ge(act_drained, END_A + KD * CH + RING)
            turn_tile(0)
            with pe.Fori(0, E // 2) as pair:
                for r in range(2):
                    first, end = expert_tiles(pe, pair * 2 + r)
                    pe.wait_ge(w_ready[r], pair * 64 + 64)
                    alone(pe)
                    for n in range(2):
                        first_product(first, r, n)
                    turn_tile(first + 1)
                    with pe.Fori(first, end - 1) as i:
                        first_product(i, r, 0, 1)
                        turn_hidden(i)
                        first_product(i, r, 1, 1)
                        turn_tile(i + 2)
                        second_product(i, r)
                    turn_hidden(end, -1)
                    second_product(end, r, -1)

        @block.vector
        def _(dve):
            dve.sem_inc(dve_drained, RING)
            dve.sem_inc(scanned, KI + 1)
            dve.sem_inc(inverse, 1)
            dve.sem_inc(summed, JS + 1)
            dve.memset(eps_sb[:, 0:1], EPS).then_inc(eps_ready, 1)
            dve.memset(eps_sb[:, 1:2], EPS * SHRINK ** 2).then_inc(eps_ready, 1)
            dve.wait_ge(consts_ready, 4)
            dve.tensor_scalar(strip[:, :], iota_i, 0.0, None, ALU.max).then_inc(dve_setup, 1)
            dve.tensor_copy(expert_id[:, :], expert_i[:, :]).then_inc(expert_ready, 1)
            dve.wait_ge(w_loaded, LOADED)
            dve.tensor_scalar(lng[:, 4:5], lng[:, 0:1], -1.0, 0.0, ALU.mult, ALU.max).then_inc(dve_setup, 1)
            dve.wait_ge(act_setup, 4)
            dve.tensor_scalar(negA[:, :, :], alog_sb[:, :, :], -1.0, None, ALU.mult).then_inc(dve_setup, 1)
            dve.wait_ge(dve_setup, 3)
            dve.tensor_scalar(lng[:, 5:6], lng[:, 4:5], lng[:, 3:4], -1.0, ALU.add, ALU.mult).then_inc(dve_setup, 1)
            dve.tensor_scalar(mask_row[:, :, :], mask_u8[:, :, :], -1.0, -MASKED, ALU.add, ALU.mult).then_inc(dve_setup, 1)
            dve.memset(mask_ones[:, :], 1.0).then_inc(dve_setup, 1)
            dve.wait_ge(expert_ready, 1)
            dve.wait_ge(consts_ready, CONSTS)
            for m in range(KD):
                dve.wait_ge(dve_full, m + 1)
                dve.tensor_copy(kT[:, m, :, :].rearrange("p b m -> p (b m)"), psD[:, m, 0:B * M]).then_inc(dve_drained, 1)
            for j in range(B // 2):
                dve.wait_ge(dve_full, KD + j + 1)
                dve.tensor_copy(vdup[:, 2 * j:2 * j + 2, :].rearrange("p b d -> p (b d)"), psD[:, KD + j, :])\
                   .then_inc(dve_drained, 1)

            def mamba(b, m):
                blk = b * 2 + m
                src = xin if m == 0 else x1
                rb = b * 4 + m
                if m == 0:
                    dve.wait_ge(x2_stored, b * 16 + 16)
                dve.wait_ge(root, rb + 1)
                dve.reciprocal(rs[:, :], rt[:, :]).then_inc(inverse, 1)
                dve.wait_ge(inverse, b * 5 + (m + 2))
                for t in range(TT):
                    dve.tensor_scalar(xn[:, t, :], src[:, t, :], rs[:, t:t + 1], None, ALU.mult).then_inc(normed, 1)
                dve.memset(pre[:, :, 0:TAPS - 1], 0.0).then_inc(pads_zero, 1)
                for f in range(KI):
                    dve.wait_ge(tap0_ready, blk * KI + f + 1)
                    for tap in range(1, TAPS):
                        if tap > 1:
                            dve.wait_ge(conv_step, blk * ((TAPS - 1) * KI) + ((TAPS - 1) * f + tap - 1))
                        dve.scalar_tensor_tensor(xm[:, f, :], pre[:, f, tap:tap + T], conv_w_sb[:, f, tap:tap + 1],
                                                 xm[:, f, :], op0=ALU.mult, op1=ALU.add).then_inc(conv_step, 1)
                for j in range(2 * KI):
                    f, half = j // 2, j % 2
                    dve.wait_ge(dve_full, job_d(b, f"z{m}", j) + 1)
                    dve.tensor_scalar(dt[:, f, half * HALF:(half + 1) * HALF], psD[:, bank_d(f"z{m}", j), :],
                                      dt_b_sb[:, f:f + 1], None, ALU.add).then_inc(dve_drained, 1)

                def times_u(f):
                    dve.wait_ge(dt_ready, blk * KI + f + 1)
                    dve.tensor_tensor(dtu[:, f, :], dt[:, f, :], xm[:, f, :], ALU.mult).then_inc(dtu_ready, 1)

                for f in range(2):
                    dve.wait_ge(soft_exp, blk * KI + f + 1)
                    alone(dve)
                    dve.tensor_scalar(is_small[:, f, :], soft_e[:, f, :], SMALL_E, None, ALU.is_lt)\
                       .then_inc(small_first, 1)
                for f in range(KI):
                    done = blk * (2 * KI) + 2 * f
                    dve.wait_ge(cubic_step, blk * KI + f + 1)
                    dve.scalar_tensor_tensor(series[:, f, :], series[:, f, :], 1.0, soft_e[:, f, :],
                                             op0=ALU.add, op1=ALU.mult).then_inc(series_step, 1)
                    if f >= 1:
                        times_u(f - 1)
                    if f < 2:
                        dve.wait_ge(small_first, blk * 2 + f + 1)
                    else:
                        dve.wait_ge(small_found, blk * (KI - 2) + (f - 1))
                    dve.wait_ge(soft_log, blk * KI + f + 1)
                    dve.wait_ge(series_step, done + 1)
                    alone(dve)
                    dve.copy_predicated(soft_ln[:, f, :], is_small[:, f, :], series[:, f, :]).then_inc(series_step, 1)
                    dve.wait_ge(series_step, done + 2)
                    dve.scalar_tensor_tensor(dt[:, f, :], dt[:, f, :], 0.0, soft_ln[:, f, :],
                                             op0=ALU.max, op1=ALU.add).then_inc(dt_ready, 1)
                times_u(KI - 1)

                def scans(s, half):
                    u = unit(b, m, s, half)
                    dve.wait_ge(hT_full, u * JT + 1)
                    if half == 1:
                        dve.wait_ge(scanned, u * KI + (KI + 1))
                    for f in range(KI):
                        dve.wait_ge(da_ready, u * KI + (f + 1))
                        dve.wait_ge(dbu_full, u * KI + (KI + f + 2))
                        start = 0.0 if half == 0 else h[:, 0, f, HALF - 1:HALF]
                        dve.tensor_tensor_scan(h[:, half, f, :], da[:, half, f, :], psD[:, f, :], start,
                                               ALU.mult, ALU.add).then_inc(scanned, 1)

                def sums(s, half):
                    u = unit(b, m, s, half)
                    dve.wait_ge(summed, u * JS + 1)
                    for j in range(JS):
                        t = half * JT + j
                        dve.wait_ge(hT_full, u * JT + (JT + j + 2))
                        dve.scalar_tensor_tensor(yT[:, t, :], psA[:, j, :],
                                                 bc[:, t, bass.ds(s + NS, 1)], yT[:, t, :],
                                                 op0=ALU.mult, op1=ALU.add).then_inc(summed, 1)

                dve.memset(yT_flat, 0.0).then_inc(y_zero, 1)
                dve.wait_ge(y_zero, blk + 1)
                scans(0, 0)
                with dve.Fori(0, NS - 1) as s:
                    scans(s, 1)
                    sums(s, 0)
                    scans(s + 1, 0)
                    sums(s, 1)
                scans(NS - 1, 1)
                sums(NS - 1, 0)
                sums(NS - 1, 1)

                for half in range(2):
                    cols = slice(half * HALF, (half + 1) * HALF)
                    for f in range(KI):
                        j = half * KI + f
                        dve.wait_ge(dve_full, job_d(b, f"y{m}", j) + 1)
                        dve.scalar_tensor_tensor(y[:, f, cols], xm[:, f, cols], d_sb[:, f:f + 1],
                                                 psD[:, bank_d(f"y{m}", j), :], op0=ALU.mult, op1=ALU.add)\
                           .then_inc(dve_drained, 1)
                    for f in range(KI):
                        dve.wait_ge(dve_drained, job_d(b, f"y{m}", half * KI + f) + 1 + RING)
                        dve.wait_ge(gate_ready, blk * KI + f + 1)
                        dve.tensor_tensor(y[:, f, cols], y[:, f, cols], gate[:, f, cols], ALU.mult).then_inc(gated, 1)
                if m == 0:
                    dve.wait_ge(xb_ready, b + 1)
                for j in range(TT // 2):
                    dve.wait_ge(dve_full, job_d(b, f"mo{m}", j) + 1)
                    ps = psD[:, bank_d(f"mo{m}", j), :].rearrange("p (t d) -> p t d", t=2)
                    if m == 0:
                        dve.tensor_tensor(x1[:, 2 * j:2 * j + 2, :], ps, base[:, 2 * j:2 * j + 2, :], ALU.add)\
                           .then_inc(dve_drained, 1)
                    else:
                        dve.tensor_tensor(o2[:, 2 * j:2 * j + 2, :], ps,
                                          out_b_sb[:, :].unsqueeze(1).broadcast_to([P, 2, D]), ALU.add)\
                           .then_inc(dve_drained, 1)

            def tile_stats(b, stage, j, z):
                dve.wait_ge(dve_drained, job_d(b, stage, j) + 1 + RING)
                for t in (2 * j, 2 * j + 1):
                    dve.bn_stats(stats[:, t, :], z[:, t, :]).then_inc(ln_stats, 1)

            def layer_norm(b, n, z, dst):
                dve.wait_ge(ln_stats, b * (4 * TT) + (2 * TT * n + TT))
                alone(dve)
                for t in range(TT):
                    dve.bn_aggr(aggr[:, t, :], stats[:, t, :]).then_inc(ln_stats, 1)
                dve.wait_ge(root, b * 4 + (3 + n))
                dve.reciprocal(rs[:, :], rt[:, :]).then_inc(inverse, 1)
                dve.wait_ge(inverse, b * 5 + (4 + 2 * n))
                if n == 0:
                    dve.scalar_tensor_tensor(rs[:, :], aggr[:, :, 1], VAR_LIMIT / D, rs[:, :],
                                             op0=ALU.is_le, op1=ALU.mult).then_inc(inverse, 1)
                    dve.wait_ge(inverse, b * 5 + 5)
                for t in range(TT):
                    dve.tensor_scalar(dst[:, t, :], z[:, t, :], aggr[:, t, 0:1], rs[:, t:t + 1],
                                      ALU.subtract, ALU.mult).then_inc(ln_done, 1)

            with dve.Fori(0, B) as b:
                for m in range(2):
                    mamba(b, m)
                dve.memset(oT[:, :, 0:1], 0.0).then_inc(blocks_ready, 1)
                for j, (i, half) in enumerate(MEM_S):
                    lo, hi = max(P * i, half * HALF), (half + 1) * HALF
                    at0 = sm_first[(i, half)]
                    dve.wait_ge(dve_full, job_d(b, "mem", j) + 1)
                    dve.tensor_tensor(sm_flat[:, at0:at0 + hi - lo], psD[:, bank_d("mem", j), 0:hi - lo],
                                      strip[:, lo - P * i:hi - P * i], ALU.mult).then_inc(dve_drained, 1)
                for k in range(KD):
                    last = dve.tensor_tensor(kblk[:, k, :, :], kT[:, k, bass.ds(b, 1), :].broadcast_to([P, 8, M]),
                                             headmask[:, :].unsqueeze(2).broadcast_to([P, 8, M]), ALU.mult)
                last.then_inc(blocks_ready, 1)
                for r in range(2):
                    dve.tensor_scalar(vblk[:, :, r, 0:HD], vdup[:, bass.ds(b, 1), :].rearrange(
                        "p o (q r d) -> p (o q) r d", r=2, d=HD)[:, :, r, :], pairmask[:, r:r + 1], None, ALU.mult)
                    last = dve.tensor_copy(vblk[:, :, r, HD:VW], pairmask[:, r:r + 1].unsqueeze(1)
                                           .broadcast_to([P, HEADS // 2, 1]))
                last.then_inc(blocks_ready, 1)
                dve.wait_ge(base_ready, b * 2 + 2)
                for j in range(TT // 2):
                    dve.wait_ge(dve_full, job_d(b, "rp", j) + 1)
                    dve.scalar_tensor_tensor(base[:, 2 * j:2 * j + 2, :].rearrange("p t d -> p (t d)"),
                                             psD[:, bank_d("rp", j), :], ALPHA * SHRINK,
                                             base[:, 2 * j:2 * j + 2, :].rearrange("p t d -> p (t d)"),
                                             op0=ALU.mult, op1=ALU.add).then_inc(dve_drained, 1)
                    if j >= 1:
                        tile_stats(b, "rp", j - 1, base)
                tile_stats(b, "rp", TT // 2 - 1, base)
                layer_norm(b, 0, base, xa)

                def less_max(t):
                    for n in range(2):
                        j = score_job(t, n)
                        bank = psD[:, bank_d("score", j), :].rearrange("p (h m) -> p h m", h=8)
                        dve.wait_ge(dve_full, job_d(b, "score", j) + 1)
                        dve.tensor_reduce(mx[:, n, :], bank, AX.X, ALU.max).then_inc(score_max, 1)
                        dve.wait_ge(score_max, b * (2 * TT) + (2 * t + n + 1))
                        if t >= 4:
                            dve.wait_ge(act_full, job_a(b, "probs", probs_job(t - 4, n)) + 1)
                        dve.tensor_tensor(prob[:, t % 4, n, :].rearrange("p (h m) -> p h m", h=8), bank,
                                          mx[:, n, :].unsqueeze(2).broadcast_to([P, 8, M]), ALU.subtract)\
                           .then_inc(dve_drained, 1)

                def normalise(t):
                    bank = psD[:, bank_d("score", out_job(t)), 0:HEADS * VW].rearrange("p (h d) -> p h d", h=HEADS)
                    dve.wait_ge(dve_full, job_d(b, "score", out_job(t)) + 1)
                    dve.reciprocal(rsum[:, t % 2, :], bank[:, :, HD]).then_inc(sum_inv, 1)
                    dve.wait_ge(sum_inv, b * TT + (t + 1))
                    if t >= 2:
                        dve.wait_ge(act_full, job_a(b, "probs", heads_job(t - 2)) + 1)
                    dve.tensor_tensor(att[:, t % 2, :].rearrange("p (h d) -> p h d", h=HEADS), bank[:, :, 0:HD],
                                      rsum[:, t % 2, :].unsqueeze(2).broadcast_to([P, HEADS, HD]), ALU.mult)\
                       .then_inc(dve_drained, 1)

                less_max(0)
                less_max(1)
                for t in range(TT + 1):
                    if t + 2 < TT:
                        less_max(t + 2)
                    if t >= 1:
                        normalise(t - 1)
                for j in range(TT // 2):
                    dve.wait_ge(dve_full, job_d(b, "wo", j) + 1)
                    dve.tensor_tensor(base[:, 2 * j:2 * j + 2, :].rearrange("p t d -> p (t d)"),
                                      psD[:, bank_d("wo", j), :],
                                      xa[:, 2 * j:2 * j + 2, :].rearrange("p t d -> p (t d)"), ALU.add)\
                       .then_inc(dve_drained, 1)
                    if j >= 1:
                        tile_stats(b, "wo", j - 1, base)
                tile_stats(b, "wo", TT // 2 - 1, base)
                layer_norm(b, 1, base, x2_out)

            for j, q in enumerate(batch_order):
                dve.wait_ge(dve_full, END_D + j + 1)
                dve.tensor_tensor(logit[:, TT * q:TT * (q + 1), :], psD[:, (END_D + j) % RING, 0:8 * E]
                                  .rearrange("p (t e) -> p t e", e=E),
                                  bg_sb[:, :].unsqueeze(1).broadcast_to([P, 8, E]), ALU.add).then_inc(dve_drained, 1)
            dve.wait_ge(dve_drained, END_D + 4 + RING)
            route = 0

            def link(ins, wait=True):
                nonlocal route
                route += 1
                ins.then_inc(route_step, 1)
                if wait:
                    dve.wait_ge(route_step, route)

            for t in range(NT):
                link(dve.max(top[:, t, :], logit[:, t, :]), wait=t == NT - 1)
            link(dve.tensor_tensor(rest[:, 0, :], top[:, :, 1], top[:, :, 0], ALU.subtract), wait=False)
            assert route == GAP_STEP
            for t in range(NT):
                link(dve.max_index(topi[:, t, :], top[:, t, :], logit[:, t, :]), wait=t == NT - 1)
            link(dve.tensor_copy(topf[:, :, 0:2], topi[:, :, 0:2]))
            for r, dst in enumerate((sel1, sel2)):
                link(dve.tensor_tensor(dst, topf[:, :, r:r + 1].broadcast_to([P, NT, E]),
                                       expert_id[:, :].unsqueeze(1).broadcast_to([P, NT, E]), ALU.is_equal))
            link(dve.tensor_tensor(sel, sel1, sel2, ALU.add))
            assert route == SEL_STEP
            dve.wait_ge(gap_exp, 1)
            link(dve.tensor_scalar(rest[:, 2, :], rest[:, 1, :], 1.0, None, ALU.add))
            link(dve.reciprocal(rest[:, 3, :], rest[:, 2, :]))
            link(dve.tensor_tensor(rest[:, 4, :], rest[:, 1, :], rest[:, 3, :], ALU.mult))
            dve.wait_ge(steps_ready, 1)
            link(dve.tensor_copy(steps, steps_i))
            for j, dst in enumerate((place, total)):
                dve.wait_ge(dve_full, END_D + 5 + j)
                dve.tensor_copy(dst.rearrange("p t e -> p (t e)"), psD[:, (END_D + 4 + j) % RING, 0:NT * E])\
                   .then_inc(dve_drained, 1)
            dve.wait_ge(dve_drained, END_D + 6 + RING)
            for e in range(E):
                link(dve.tensor_tensor_scan(cum[:, :, e], ones[:, 0:NT], total[:, :, e], 0.0, ALU.mult, ALU.add),
                     wait=e == E - 1)
            link(dve.tensor_tensor(place, place, cum, ALU.add))
            link(dve.tensor_tensor(place, place, total, ALU.subtract))
            link(dve.tensor_tensor(over, cum[:, NT - 1, :].unsqueeze(2).broadcast_to([P, E, STEPS]), steps, ALU.is_gt))
            link(dve.tensor_reduce(count, over, AX.X, ALU.add))
            link(dve.tensor_scalar(count, count, 2.0, None, ALU.max))
            link(dve.tensor_tensor_scan(ends, ones[:, 0:E], count, 0.0, ALU.mult, ALU.add))
            link(dve.tensor_tensor(firsts, ends, count, ALU.subtract))
            link(dve.tensor_copy(bound[:, 0:E], firsts), wait=False)
            link(dve.tensor_copy(bound[:, E:E + 1], ends[:, E - 1:E]), wait=False)
            link(dve.tensor_scalar(firsts, firsts, float(P), None, ALU.mult))
            link(dve.tensor_tensor(place, place, firsts.unsqueeze(1).broadcast_to([P, NT, E]), ALU.add))
            for r, which in enumerate((sel1, sel2)):
                link(dve.tensor_tensor(weighed, which, place, ALU.mult))
                link(dve.tensor_reduce(rest[:, 5 + r, :], weighed, AX.X, ALU.add))
            dve.tensor_copy(slot[:, :, :], rest[:, 5:7, :]).then_inc(routed, 1)

            def add_b1(i, r, n, d=0):
                dve.wait_ge(gelu_ready, i * 2 + (2 * d + n + 1))
                dve.wait_ge(hid_full, i * 2 + (2 * d + n + 1))
                dve.tensor_tensor(hid[:, n * BANK:(n + 1) * BANK], psD[:, n, :],
                                  b1_sb[:, r, n * BANK:(n + 1) * BANK], ALU.add).then_inc(hid_ready, 1)

            def copy_turned(i, d=0):
                for n in range(2):
                    dve.wait_ge(turn_full, i * 2 + (2 * d + n + 3))
                    dve.tensor_copy(hidT[:, 4 * n:4 * n + 4, :].rearrange("p k t -> p (k t)"), psA[:, 1 + n, :])\
                       .then_inc(hidT_ready, 1)

            def add_b2(i, r, d=0):
                dve.wait_ge(y_full, i + (d + 1))
                dve.tensor_tensor(ys[:, bass.ds(i + d, 1), :].rearrange("p o d -> p (o d)"), psD[:, 2, 0:D],
                                  b2_sb[:, r, :], ALU.add).then_inc(y_ready, 1)

            dve.sem_inc(hid_ready, 2)
            dve.sem_inc(hidT_ready, 4)
            dve.sem_inc(y_ready, 1)
            dve.wait_ge(routed, 1)
            with dve.Fori(0, E // 2) as pair:
                for r in range(2):
                    first, end = expert_tiles(dve, pair * 2 + r)
                    dve.wait_ge(w_ready[r], pair * 64 + 64)
                    alone(dve)
                    for n in range(2):
                        add_b1(first, r, n)
                    with dve.Fori(first, end - 1) as i:
                        add_b1(i, r, 0, 1)
                        copy_turned(i)
                        add_b1(i, r, 1, 1)
                        add_b2(i, r)
                    copy_turned(end, -1)
                    add_b2(end, r, -1)

            n = 0

            def fin(ins):
                nonlocal n
                n += 1
                ins.then_inc(fin_step, 1)

            def norm(q, r):
                for t in range(TT):
                    fin(dve.bn_stats(fstats[:, q % 2, t, :], acc[:, q * TT + t, :]))
                dve.wait_ge(fin_step, n)
                for t in range(TT):
                    fin(dve.bn_aggr(faggr[:, q % 2, t, :], fstats[:, q % 2, t, :]))
                dve.wait_ge(fin_root, 2 * q + r + 1)
                fin(dve.reciprocal(frt[:, q % 2, r, :], frt[:, q % 2, r, :]))
                dve.wait_ge(fin_step, n)
                for t in range(TT):
                    fin(dve.tensor_scalar(acc[:, q * TT + t, :], acc[:, q * TT + t, :], faggr[:, q % 2, t, 0:1],
                                          frt[:, q % 2, r, t:t + 1], ALU.subtract, ALU.mult))
                dve.wait_ge(fin_step, n)

            for q in range(B):
                rows = acc[:, q * TT:(q + 1) * TT, :]
                dve.wait_ge(picked_in[q], 2 * TT * 16)
                for r in range(2):
                    for t in range(q * TT, (q + 1) * TT):
                        fin(dve.scalar_tensor_tensor(acc[:, t, :], picked[:, r, t, :], rest[:, 3 + r, t:t + 1],
                                                     (x2 if r == 0 else acc)[:, t, :], op0=ALU.mult, op1=ALU.add))
                    dve.wait_ge(fin_step, n)
                norm(q, 0)
                fin(dve.tensor_tensor(rows, rows, gamma_sb[:, :].unsqueeze(1).broadcast_to([P, TT, D]), ALU.mult))
                dve.wait_ge(fin_step, n)
                fin(dve.tensor_tensor(rows, rows, beta_sb[:, :].unsqueeze(1).broadcast_to([P, TT, D]), ALU.add))
                dve.wait_ge(fin_step, n)
                fin(dve.tensor_tensor(rows, rows, x2[:, q * TT:(q + 1) * TT, :], ALU.add))
                dve.wait_ge(fin_step, n)
                norm(q, 1)
                assert n == FIN_PER * (q + 1)


def _layouts(np, a):
    def vec(v):
        return v.reshape(-1, 128).T

    def rows(v):
        return v.reshape(v.shape[0] // 128, 128, -1).transpose(1, 0, 2)

    return {
        "x": a["x"], "ctxT": a["ctx_768"].transpose(0, 2, 1), "ctx_mask": a["mask_BxS2_bf1"].view(np.uint8),
        "norm1_w": vec(a["L0_attn_norm1_w"]), "norm2_w": vec(a["L0_attn_norm2_w"]),
        "in_wT": a["L0_attn_in_proj_w"].T, "in_b": vec(a["L0_attn_in_proj_b"]),
        "conv_w": rows(a["L0_attn_conv_w"][:, 0, :]), "conv_b": vec(a["L0_attn_conv_b"]),
        "xp_wT": a["L0_attn_x_proj_w"].T, "dt_wT": a["L0_attn_dt_proj_w"].T, "dt_b": vec(a["L0_attn_dt_proj_b"]),
        "A_log": rows(a["L0_attn_A_log"]), "D_ssm": vec(a["L0_attn_D_ssm"]),
        "out_wT": a["L0_attn_out_proj_w"].T, "out_b": a["L0_attn_out_proj_b"],
        "write_wT": a["L0_attn_proj_write_w"].T, "read_wT": a["L0_attn_proj_read_w"].T,
        "decay": a["L0_attn_decay"].reshape(1),
        "Wq": a["L0_xattn_Wq"], "Wk": a["L0_xattn_Wk"], "Wv": a["L0_xattn_Wv"], "Wo": a["L0_xattn_Wo"],
        "Wg": a["L0_ffn_Wg"], "bg": a["L0_ffn_bg"], "W1": a["L0_ffn_W1"],
        "b1": a["L0_ffn_b1"],
        "W2": a["L0_ffn_W2"], "b2": a["L0_ffn_b2"], "gamma": a["L0_ffn_gamma"], "beta": a["L0_ffn_beta"],
    }


def kernel(**inputs):
    import numpy as _np
    import concourse.bacc as _bacc
    from concourse import mybir as _mybir
    from concourse.bass_utils import run_bass_kernel_spmd as _run

    nc = _bacc.Bacc("TRN2", target_bir_lowering=False, num_devices=1)
    arrays, args = {}, []
    for name, a in _layouts(_np, {k: _np.asarray(v) for k, v in inputs.items()}).items():
        a = _np.ascontiguousarray(a)
        arrays[f"in_{name}"] = a
        args.append(nc.dram_tensor(f"in_{name}", a.shape, _mybir.dt.from_np(a.dtype), kind="ExternalInput").ap())
    shape = tuple(inputs["x"].shape)
    args.append(nc.dram_tensor("out_0", shape, _mybir.dt.float32, kind="ExternalOutput").ap())
    decoder_layer(nc, *args)
    r = _run(nc, [arrays], core_ids=[0])
    return r.results[0]["out_0"]
```
